# Optimizing a Trainium2 kernel written in Bass

```python
import numpy as np
import jax
import jax.numpy as jnp

def _softmax(x, axis=-1):
    return jax.nn.softmax(x, axis=axis)

def _gelu(x):
    return jax.nn.gelu(x, approximate=True)

def _silu(x):
    return jax.nn.silu(x)

def _sigmoid(x):
    return jax.nn.sigmoid(x)

def _layernorm(x, axis=-1, eps=1e-05):
    m = jnp.mean(x, axis=axis, keepdims=True)
    v = jnp.var(x, axis=axis, keepdims=True)
    return (x - m) / jnp.sqrt(v + eps)

def _scatter_add(tgt, idx, src, axis=0):
    return tgt.at[idx].add(src)

def _segment_sum(src, seg, n):
    return jax.ops.segment_sum(src, seg, n)
kernel_name = 'mk_seq_postln_d2_jaxref_r8_99f123'

def setup_inputs(seed: int=0):
    np.random.seed(seed)
    _w = jnp.asarray

    def _L0_attn_setup():
        import jax, jax.numpy as jnp
        import numpy as np
        B, L = (2, 128)
        D_MODEL, D_CKV, D_CQ = (128, 32, 64)
        N_HEAD, D_HEAD, D_ROPE = (8, 64, 32)
        N_IDX_HEAD = 4
        K_TS, LW = (96, 64)
        ROPE_BASE = 10000.0

        def _pope(x, angles):
            cos, sin = (jnp.cos(angles), jnp.sin(angles))
            mu1, mu2 = jnp.split(jax.nn.softplus(x), 2, axis=-1)
            return jnp.concatenate([mu1 * cos - mu2 * sin, mu1 * sin + mu2 * cos], axis=-1)

        def _forward(x, W_dkv, W_uk, W_uv, W_dq, W_uq, W_qr, W_kr, W_out, idx_wq, idx_wk, idx_w, raw_delta):
            B_, L_, _ = x.shape
            c_kv = x @ W_dkv
            q_i = (x @ idx_wq).reshape(B_, L_, N_IDX_HEAD, D_HEAD)
            k_i = x @ idx_wk
            s_i = jax.nn.relu(jnp.einsum('bthd,bsd->bths', q_i, k_i))
            I = jnp.einsum('bths,h->bts', s_i, idx_w)
            qpos = jnp.arange(L_)[:, None]
            kpos = jnp.arange(L_)[None, :]
            local = (kpos >= qpos - LW + 1) & (kpos <= qpos)
            causal = kpos > qpos
            I = jnp.where(local[None], jnp.inf, I)
            I = jnp.where(causal[None], -jnp.inf, I)
            kk = min(K_TS, L_)
            _, idx = jax.lax.top_k(I, kk)
            bi = jnp.arange(B_)[:, None, None]
            key_c = (c_kv @ W_uk)[bi, idx].reshape(B_, L_, kk, N_HEAD, D_HEAD)
            value = (c_kv @ W_uv)[bi, idx].reshape(B_, L_, kk, N_HEAD, D_HEAD)
            c_q = x @ W_dq
            query_c = (c_q @ W_uq).reshape(B_, L_, N_HEAD, D_HEAD)
            half = D_ROPE // 2
            theta = 1.0 / ROPE_BASE ** (2.0 * jnp.arange(half, dtype=jnp.float32) / D_ROPE)
            delta = -2.0 * jnp.pi * jax.nn.sigmoid(raw_delta)
            angles_q = jnp.arange(L_, dtype=jnp.float32)[:, None] * theta[None, :] + delta
            query_r = _pope((c_q @ W_qr).reshape(B_, L_, N_HEAD, D_ROPE), angles_q[None, :, None, :])
            kr_sel = (x @ W_kr)[bi, idx]
            angles_k = jnp.arange(kk, dtype=jnp.float32)[:, None] * theta[None, :] + delta
            key_r = _pope(kr_sel, angles_k[None, None, :, :])
            scale = (D_HEAD + D_ROPE) ** (-0.5)
            q_c = query_c.transpose(0, 2, 1, 3)
            q_r = query_r.transpose(0, 2, 1, 3)
            k_c = key_c.transpose(0, 3, 1, 2, 4)
            v = value.transpose(0, 3, 1, 2, 4)
            scores = (jnp.einsum('bhld,bhlkd->bhlk', q_c, k_c) + jnp.einsum('bhld,blkd->bhlk', q_r, key_r)) * scale
            attn = jax.nn.softmax(scores.astype(jnp.float32), axis=-1).astype(v.dtype)
            out = jnp.einsum('bhlk,bhlkd->bhld', attn, v)
            out = out.transpose(0, 2, 1, 3).reshape(B_, L_, N_HEAD * D_HEAD)
            return out @ W_out
        key = jax.random.key(seed)
        ks = jax.random.split(key, 14)

        def w(k, shape, fan_in):
            return jax.random.normal(k, shape, dtype=jnp.float32) * fan_in ** (-0.5)
        return {'x': jax.random.normal(ks[0], (B, L, D_MODEL), dtype=jnp.float32), 'W_dkv': w(ks[1], (D_MODEL, D_CKV), D_MODEL), 'W_uk': w(ks[2], (D_CKV, N_HEAD * D_HEAD), D_CKV), 'W_uv': w(ks[3], (D_CKV, N_HEAD * D_HEAD), D_CKV), 'W_dq': w(ks[4], (D_MODEL, D_CQ), D_MODEL), 'W_uq': w(ks[5], (D_CQ, N_HEAD * D_HEAD), D_CQ), 'W_qr': w(ks[6], (D_CQ, N_HEAD * D_ROPE), D_CQ), 'W_kr': w(ks[7], (D_MODEL, D_ROPE), D_MODEL), 'W_out': w(ks[8], (N_HEAD * D_HEAD, D_MODEL), N_HEAD * D_HEAD), 'idx_wq': w(ks[9], (D_MODEL, N_IDX_HEAD * D_HEAD), D_MODEL), 'idx_wk': w(ks[10], (D_MODEL, D_HEAD), D_MODEL), 'idx_w': jnp.ones((N_IDX_HEAD,), dtype=jnp.float32), 'raw_delta': jax.random.normal(ks[11], (D_ROPE // 2,), dtype=jnp.float32) * 0.1}
    _L0_attn_in = _L0_attn_setup()

    def _L0_ffn_setup():
        import jax, jax.numpy as jnp
        import numpy as np
        B, S, H, FFN, E = (2, 256, 128, 512, 8)
        key = jax.random.key(seed)
        k0, k1, k2, k3 = jax.random.split(key, 4)
        return {'hidden_states': jax.random.normal(k0, (B, S, H), dtype=jnp.float32), 'Wr': jax.random.normal(k1, (H, E), dtype=jnp.float32) * 0.02, 'br': jnp.zeros((E,), dtype=jnp.float32), 'W1': jax.random.normal(k2, (E, H, FFN), dtype=jnp.float32) * 0.02, 'W2': jax.random.normal(k3, (E, FFN, H), dtype=jnp.float32) * 0.02}
    _L0_ffn_in = _L0_ffn_setup()

    def _L1_attn_setup():
        import jax, jax.numpy as jnp
        import numpy as np
        LN_EPS = 1e-05
        key = jax.random.key(seed)
        ks = jax.random.split(key, 7)
        B, L, D, N = (8, 256, 128, 16)
        x = jax.random.normal(ks[0], (B, L, D), jnp.float32)
        A = jax.random.normal(ks[1], (D, N, N), jnp.float32) * (0.2 / np.sqrt(N))
        Bp = jax.random.normal(ks[2], (D, N), jnp.float32)
        Cp = jax.random.normal(ks[3], (D, N), jnp.float32)
        Dp = jax.random.normal(ks[4], (D,), jnp.float32)
        Wg = jax.random.normal(ks[5], (D, D), jnp.float32) / np.sqrt(D)
        bg = jnp.zeros((D,), jnp.float32)
        gamma = jnp.ones((D,), jnp.float32)
        beta = jnp.zeros((D,), jnp.float32)
        return dict(x=x, A=A, Bp=Bp, Cp=Cp, Dp=Dp, Wg=Wg, bg=bg, gamma=gamma, beta=beta)
    _L1_attn_in = _L1_attn_setup()

    def _L1_ffn_setup():
        import jax, jax.numpy as jnp
        import numpy as np
        B, S, D, H, M, E, K = (4, 256, 128, 256, 64, 8, 2)

        def _layernorm(x, g, b, eps=1e-05):
            mu = x.mean(-1, keepdims=True)
            var = ((x - mu) ** 2).mean(-1, keepdims=True)
            return (x - mu) * jax.lax.rsqrt(var + eps) * g + b

        def _forward(inputs_embeds, enc_W, enc_b, s2c_W, s2c_b, rW1, rb1, rW2, rb2, We1, be1, We2, be2, c2s_W, c2s_b, dec_W, dec_b, ln_g, ln_b):
            b, s, _ = inputs_embeds.shape
            spikes_enc = jax.nn.sigmoid(inputs_embeds @ enc_W + enc_b)
            flat = spikes_enc.reshape(b * s, H)
            cont = flat @ s2c_W + s2c_b
            logits = jnp.tanh(cont @ rW1 + rb1) @ rW2 + rb2
            probs = jax.nn.softmax(logits, axis=-1)
            topw, topi = jax.lax.top_k(probs, K)
            w = topw / topw.sum(-1, keepdims=True)
            gates = (jax.nn.one_hot(topi, E, dtype=cont.dtype) * w[..., None]).sum(1)
            h = jax.nn.relu(jnp.einsum('nm,emh->enh', cont, We1) + be1[:, None, :])
            expert_out = jnp.einsum('enh,ehm->enm', h, We2) + be2[:, None, :]
            output_flat = jnp.einsum('enm,ne->nm', expert_out, gates)
            spikes_moe = jax.nn.sigmoid(output_flat @ c2s_W + c2s_b).reshape(b, s, H)
            decoded = jax.nn.sigmoid(spikes_moe @ dec_W + dec_b)
            return _layernorm(decoded, ln_g, ln_b)
        key = jax.random.key(seed)
        ks = jax.random.split(key, 10)
        r = lambda k, shape: jax.random.normal(k, shape, dtype=jnp.float32) * 0.02
        return {'inputs_embeds': jax.random.normal(ks[0], (B, S, D), dtype=jnp.float32), 'enc_W': r(ks[1], (D, H)), 'enc_b': jnp.zeros((H,), jnp.float32), 's2c_W': r(ks[2], (H, M)), 's2c_b': jnp.zeros((M,), jnp.float32), 'rW1': r(ks[3], (M, 64)), 'rb1': jnp.zeros((64,), jnp.float32), 'rW2': r(ks[4], (64, E)), 'rb2': jnp.zeros((E,), jnp.float32), 'We1': r(ks[5], (E, M, H // 2)), 'be1': jnp.zeros((E, H // 2), jnp.float32), 'We2': r(ks[6], (E, H // 2, M)), 'be2': jnp.zeros((E, M), jnp.float32), 'c2s_W': r(ks[7], (M, H)), 'c2s_b': jnp.zeros((H,), jnp.float32), 'dec_W': r(ks[8], (H, D)), 'dec_b': jnp.zeros((D,), jnp.float32), 'ln_g': jnp.ones((D,), jnp.float32), 'ln_b': jnp.zeros((D,), jnp.float32)}
    _L1_ffn_in = _L1_ffn_setup()
    _d = {'L0_attn_x': _L0_attn_in['x'], 'L0_attn_W_dkv': _L0_attn_in['W_dkv'], 'L0_attn_W_uk': _L0_attn_in['W_uk'], 'L0_attn_W_uv': _L0_attn_in['W_uv'], 'L0_attn_W_dq': _L0_attn_in['W_dq'], 'L0_attn_W_uq': _L0_attn_in['W_uq'], 'L0_attn_W_qr': _L0_attn_in['W_qr'], 'L0_attn_W_kr': _L0_attn_in['W_kr'], 'L0_attn_W_out': _L0_attn_in['W_out'], 'L0_attn_idx_wq': _L0_attn_in['idx_wq'], 'L0_attn_idx_wk': _L0_attn_in['idx_wk'], 'L0_attn_idx_w': _L0_attn_in['idx_w'], 'L0_attn_raw_delta': _L0_attn_in['raw_delta'], 'L0_ffn_Wr': _L0_ffn_in['Wr'], 'L0_ffn_br': _L0_ffn_in['br'], 'L0_ffn_W1': _L0_ffn_in['W1'], 'L0_ffn_W2': _L0_ffn_in['W2'], 'L1_attn_A': _L1_attn_in['A'], 'L1_attn_Bp': _L1_attn_in['Bp'], 'L1_attn_Cp': _L1_attn_in['Cp'], 'L1_attn_Dp': _L1_attn_in['Dp'], 'L1_attn_Wg': _L1_attn_in['Wg'], 'L1_attn_bg': _L1_attn_in['bg'], 'L1_attn_gamma': _L1_attn_in['gamma'], 'L1_attn_beta': _L1_attn_in['beta'], 'L1_ffn_enc_W': _L1_ffn_in['enc_W'], 'L1_ffn_enc_b': _L1_ffn_in['enc_b'], 'L1_ffn_s2c_W': _L1_ffn_in['s2c_W'], 'L1_ffn_s2c_b': _L1_ffn_in['s2c_b'], 'L1_ffn_rW1': _L1_ffn_in['rW1'], 'L1_ffn_rb1': _L1_ffn_in['rb1'], 'L1_ffn_rW2': _L1_ffn_in['rW2'], 'L1_ffn_rb2': _L1_ffn_in['rb2'], 'L1_ffn_We1': _L1_ffn_in['We1'], 'L1_ffn_be1': _L1_ffn_in['be1'], 'L1_ffn_We2': _L1_ffn_in['We2'], 'L1_ffn_be2': _L1_ffn_in['be2'], 'L1_ffn_c2s_W': _L1_ffn_in['c2s_W'], 'L1_ffn_c2s_b': _L1_ffn_in['c2s_b'], 'L1_ffn_dec_W': _L1_ffn_in['dec_W'], 'L1_ffn_dec_b': _L1_ffn_in['dec_b'], 'L1_ffn_ln_g': _L1_ffn_in['ln_g'], 'L1_ffn_ln_b': _L1_ffn_in['ln_b']}
    _x0 = _d['L0_attn_x']
    _d['L0_attn_x'] = jax.random.normal(jax.random.fold_in(jax.random.key(seed), 1), (8, 256, 128), dtype=_x0.dtype)
    del _x0
    return _d

def reference(L0_attn_x, L0_attn_W_dkv, L0_attn_W_uk, L0_attn_W_uv, L0_attn_W_dq, L0_attn_W_uq, L0_attn_W_qr, L0_attn_W_kr, L0_attn_W_out, L0_attn_idx_wq, L0_attn_idx_wk, L0_attn_idx_w, L0_attn_raw_delta, L0_ffn_Wr, L0_ffn_br, L0_ffn_W1, L0_ffn_W2, L1_attn_A, L1_attn_Bp, L1_attn_Cp, L1_attn_Dp, L1_attn_Wg, L1_attn_bg, L1_attn_gamma, L1_attn_beta, L1_ffn_enc_W, L1_ffn_enc_b, L1_ffn_s2c_W, L1_ffn_s2c_b, L1_ffn_rW1, L1_ffn_rb1, L1_ffn_rW2, L1_ffn_rb2, L1_ffn_We1, L1_ffn_be1, L1_ffn_We2, L1_ffn_be2, L1_ffn_c2s_W, L1_ffn_c2s_b, L1_ffn_dec_W, L1_ffn_dec_b, L1_ffn_ln_g, L1_ffn_ln_b):

    def _L0_attn_ref(x, W_dkv, W_uk, W_uv, W_dq, W_uq, W_qr, W_kr, W_out, idx_wq, idx_wk, idx_w, raw_delta):
        import jax, jax.numpy as jnp
        import numpy as np
        B, L = (2, 128)
        D_MODEL, D_CKV, D_CQ = (128, 32, 64)
        N_HEAD, D_HEAD, D_ROPE = (8, 64, 32)
        N_IDX_HEAD = 4
        K_TS, LW = (96, 64)
        ROPE_BASE = 10000.0

        def _pope(x, angles):
            cos, sin = (jnp.cos(angles), jnp.sin(angles))
            mu1, mu2 = jnp.split(jax.nn.softplus(x), 2, axis=-1)
            return jnp.concatenate([mu1 * cos - mu2 * sin, mu1 * sin + mu2 * cos], axis=-1)

        def _forward(x, W_dkv, W_uk, W_uv, W_dq, W_uq, W_qr, W_kr, W_out, idx_wq, idx_wk, idx_w, raw_delta):
            B_, L_, _ = x.shape
            c_kv = x @ W_dkv
            q_i = (x @ idx_wq).reshape(B_, L_, N_IDX_HEAD, D_HEAD)
            k_i = x @ idx_wk
            s_i = jax.nn.relu(jnp.einsum('bthd,bsd->bths', q_i, k_i))
            I = jnp.einsum('bths,h->bts', s_i, idx_w)
            qpos = jnp.arange(L_)[:, None]
            kpos = jnp.arange(L_)[None, :]
            local = (kpos >= qpos - LW + 1) & (kpos <= qpos)
            causal = kpos > qpos
            I = jnp.where(local[None], jnp.inf, I)
            I = jnp.where(causal[None], -jnp.inf, I)
            kk = min(K_TS, L_)
            _, idx = jax.lax.top_k(I, kk)
            bi = jnp.arange(B_)[:, None, None]
            key_c = (c_kv @ W_uk)[bi, idx].reshape(B_, L_, kk, N_HEAD, D_HEAD)
            value = (c_kv @ W_uv)[bi, idx].reshape(B_, L_, kk, N_HEAD, D_HEAD)
            c_q = x @ W_dq
            query_c = (c_q @ W_uq).reshape(B_, L_, N_HEAD, D_HEAD)
            half = D_ROPE // 2
            theta = 1.0 / ROPE_BASE ** (2.0 * jnp.arange(half, dtype=jnp.float32) / D_ROPE)
            delta = -2.0 * jnp.pi * jax.nn.sigmoid(raw_delta)
            angles_q = jnp.arange(L_, dtype=jnp.float32)[:, None] * theta[None, :] + delta
            query_r = _pope((c_q @ W_qr).reshape(B_, L_, N_HEAD, D_ROPE), angles_q[None, :, None, :])
            kr_sel = (x @ W_kr)[bi, idx]
            angles_k = jnp.arange(kk, dtype=jnp.float32)[:, None] * theta[None, :] + delta
            key_r = _pope(kr_sel, angles_k[None, None, :, :])
            scale = (D_HEAD + D_ROPE) ** (-0.5)
            q_c = query_c.transpose(0, 2, 1, 3)
            q_r = query_r.transpose(0, 2, 1, 3)
            k_c = key_c.transpose(0, 3, 1, 2, 4)
            v = value.transpose(0, 3, 1, 2, 4)
            scores = (jnp.einsum('bhld,bhlkd->bhlk', q_c, k_c) + jnp.einsum('bhld,blkd->bhlk', q_r, key_r)) * scale
            attn = jax.nn.softmax(scores.astype(jnp.float32), axis=-1).astype(v.dtype)
            out = jnp.einsum('bhlk,bhlkd->bhld', attn, v)
            out = out.transpose(0, 2, 1, 3).reshape(B_, L_, N_HEAD * D_HEAD)
            return out @ W_out
        return _forward(x, W_dkv, W_uk, W_uv, W_dq, W_uq, W_qr, W_kr, W_out, idx_wq, idx_wk, idx_w, raw_delta)

    def _L0_ffn_ref(hidden_states, Wr, br, W1, W2):
        import jax, jax.numpy as jnp
        import numpy as np
        B, S, H, FFN, E = (2, 256, 128, 512, 8)
        b, s, h = hidden_states.shape
        x = hidden_states.reshape(-1, h)
        route = jax.nn.sigmoid(x @ Wr + br)
        max_prob = jnp.max(route, axis=1, keepdims=True)
        max_ind = jnp.argmax(route, axis=1)
        out = jnp.zeros_like(x)
        n_experts = Wr.shape[1]
        for e in range(n_experts):
            mask = (max_ind == e)[:, None].astype(x.dtype)
            y = jax.nn.gelu(x @ W1[e], approximate=False) @ W2[e]
            out = out + mask * y
        out = out * max_prob
        return out.reshape(b, s, h)

    def _L1_attn_ref(x, A, Bp, Cp, Dp, Wg, bg, gamma, beta):
        import jax, jax.numpy as jnp
        import numpy as np
        LN_EPS = 1e-05
        gate = jax.nn.sigmoid(jnp.einsum('bld,ed->ble', x, Wg) + bg)
        xg = x * gate
        Bsz, L, D = xg.shape
        N = A.shape[-1]

        def step(s, xt):
            s = jnp.einsum('bdn,dnm->bdm', s, A) + xt[..., None] * Bp
            y = jnp.einsum('bdn,dn->bd', s, Cp) + Dp * xt
            return (s, y)
        s0 = jnp.zeros((Bsz, D, N), xg.dtype)
        _, ys = jax.lax.scan(step, s0, jnp.moveaxis(xg, 1, 0))
        y = jnp.moveaxis(ys, 0, 1) + xg
        mu = jnp.mean(y, axis=-1, keepdims=True)
        var = jnp.var(y, axis=-1, keepdims=True)
        return (y - mu) * jax.lax.rsqrt(var + LN_EPS) * gamma + beta

    def _L1_ffn_ref(inputs_embeds, enc_W, enc_b, s2c_W, s2c_b, rW1, rb1, rW2, rb2, We1, be1, We2, be2, c2s_W, c2s_b, dec_W, dec_b, ln_g, ln_b):
        import jax, jax.numpy as jnp
        import numpy as np
        B, S, D, H, M, E, K = (4, 256, 128, 256, 64, 8, 2)

        def _layernorm(x, g, b, eps=1e-05):
            mu = x.mean(-1, keepdims=True)
            var = ((x - mu) ** 2).mean(-1, keepdims=True)
            return (x - mu) * jax.lax.rsqrt(var + eps) * g + b

        def _forward(inputs_embeds, enc_W, enc_b, s2c_W, s2c_b, rW1, rb1, rW2, rb2, We1, be1, We2, be2, c2s_W, c2s_b, dec_W, dec_b, ln_g, ln_b):
            b, s, _ = inputs_embeds.shape
            spikes_enc = jax.nn.sigmoid(inputs_embeds @ enc_W + enc_b)
            flat = spikes_enc.reshape(b * s, H)
            cont = flat @ s2c_W + s2c_b
            logits = jnp.tanh(cont @ rW1 + rb1) @ rW2 + rb2
            probs = jax.nn.softmax(logits, axis=-1)
            topw, topi = jax.lax.top_k(probs, K)
            w = topw / topw.sum(-1, keepdims=True)
            gates = (jax.nn.one_hot(topi, E, dtype=cont.dtype) * w[..., None]).sum(1)
            h = jax.nn.relu(jnp.einsum('nm,emh->enh', cont, We1) + be1[:, None, :])
            expert_out = jnp.einsum('enh,ehm->enm', h, We2) + be2[:, None, :]
            output_flat = jnp.einsum('enm,ne->nm', expert_out, gates)
            spikes_moe = jax.nn.sigmoid(output_flat @ c2s_W + c2s_b).reshape(b, s, H)
            decoded = jax.nn.sigmoid(spikes_moe @ dec_W + dec_b)
            return _layernorm(decoded, ln_g, ln_b)
        return _forward(inputs_embeds, enc_W, enc_b, s2c_W, s2c_b, rW1, rb1, rW2, rb2, We1, be1, We2, be2, c2s_W, c2s_b, dec_W, dec_b, ln_g, ln_b)
    x = L0_attn_x
    x = _layernorm(x + _L0_attn_ref(x, L0_attn_W_dkv, L0_attn_W_uk, L0_attn_W_uv, L0_attn_W_dq, L0_attn_W_uq, L0_attn_W_qr, L0_attn_W_kr, L0_attn_W_out, L0_attn_idx_wq, L0_attn_idx_wk, L0_attn_idx_w, L0_attn_raw_delta), axis=-1)
    x = _layernorm(x + _L0_ffn_ref(x, L0_ffn_Wr, L0_ffn_br, L0_ffn_W1, L0_ffn_W2), axis=-1)
    x = _layernorm(x + _L1_attn_ref(x, L1_attn_A, L1_attn_Bp, L1_attn_Cp, L1_attn_Dp, L1_attn_Wg, L1_attn_bg, L1_attn_gamma, L1_attn_beta), axis=-1)
    x = _layernorm(x + _L1_ffn_ref(x, L1_ffn_enc_W, L1_ffn_enc_b, L1_ffn_s2c_W, L1_ffn_s2c_b, L1_ffn_rW1, L1_ffn_rb1, L1_ffn_rW2, L1_ffn_rb2, L1_ffn_We1, L1_ffn_be1, L1_ffn_We2, L1_ffn_be2, L1_ffn_c2s_W, L1_ffn_c2s_b, L1_ffn_dec_W, L1_ffn_dec_b, L1_ffn_ln_g, L1_ffn_ln_b), axis=-1)
    return x

_drawn_inputs = setup_inputs


def setup_inputs(seed=0):
    import zlib

    import numpy as np

    out = dict(_drawn_inputs(seed))
    spreads = {'L0_attn_idx_w': (1.0, 0.6),
     'L0_ffn_br': (0.0, 0.386),
     'L1_attn_bg': (0.0, 0.486),
     'L1_attn_gamma': (1.0, 0.2),
     'L1_attn_beta': (0.0, 0.1),
     'L1_ffn_enc_b': (0.0, 0.8),
     'L1_ffn_s2c_b': (0.0, 0.8),
     'L1_ffn_rb1': (0.0, 0.8),
     'L1_ffn_rb2': (0.0, 0.8),
     'L1_ffn_be1': (0.0, 0.8),
     'L1_ffn_be2': (0.0, 0.8),
     'L1_ffn_c2s_b': (0.0, 0.454),
     'L1_ffn_dec_b': (0.0, 0.1),
     'L1_ffn_ln_g': (1.0, 0.2),
     'L1_ffn_ln_b': (0.0, 0.1)}
    factors = {'L0_attn_raw_delta': 64.0,
     'L0_ffn_Wr': 2.931,
     'L1_ffn_enc_W': 8.0,
     'L1_ffn_s2c_W': 8.0,
     'L1_ffn_rW1': 8.0,
     'L1_ffn_rW2': 8.0,
     'L1_ffn_We1': 8.0,
     'L1_ffn_We2': 8.0,
     'L1_ffn_c2s_W': 8.0}
    for name, (base, spread) in spreads.items():
        noise = np.random.default_rng([zlib.crc32(name.encode()), seed]).standard_normal(out[name].shape)
        drawn = base * np.exp(spread * noise) if base else spread * noise
        out[name] = jnp.asarray(drawn.astype(out[name].dtype))
    for name, factor in factors.items():
        out[name] = (out[name] * factor).astype(out[name].dtype)
    return out
```

```python
from contextlib import ExitStack

import numpy as np
import concourse.bass as bass
from concourse import mybir

F32 = mybir.dt.float32
BF16 = mybir.dt.bfloat16
U32 = mybir.dt.uint32
I32 = mybir.dt.int32
ALU = mybir.AluOpType
ACT = mybir.ActivationFunctionType
AX = mybir.AxisListType.X

B, L, D = 8, 256, 128
NT = B * L // 128
NH = 8
SCALE = 96.0 ** -0.5
BIG = 1.0e30
LOW = -3.0e38


class Tok:

    def __init__(self, queue):
        self.queue, self.used, self.value = queue, False, 0

    def target(self):
        return self.queue.sem, self.value


class Group:

    def __init__(self, sem):
        self.sem, self.count, self.used = sem, 0, False

    def target(self):
        return self.sem, 16 * self.count


class Queue:

    def __init__(self, sem, chained):
        self.sem, self.items, self.chained, self.last = sem, [], chained, None

    def __call__(self, fn, *waits):
        tok = Tok(self)
        if self.chained:
            waits += (self.last,) if self.last else ()
            self.last = tok
        for w in waits:
            w.used = True
        self.items.append((waits, fn, tok))
        return tok

    def dma(self, group, fn, *waits):
        for w in waits:
            w.used = True
        group.count += 1
        self.items.append((waits, fn, group))
        return group

    def hold(self, *waits):
        for w in waits:
            w.used = True
        self.items.append((waits, None, None))

    def count(self):
        n = 0
        for _, _, tok in self.items:
            if isinstance(tok, Tok) and tok.used:
                n += 1
                tok.value = n

    def write(self, eng):
        reached = {}
        for waits, fn, tok in self.items:
            for w in waits:
                sem, value = w.target()
                if reached.get(id(sem), 0) < value:
                    eng.wait_ge(sem, value)
                    reached[id(sem)] = value
            if fn is None:
                continue
            ins = fn(eng)
            if isinstance(tok, Group):
                ins.then_inc(tok.sem, 16)
            elif tok.used:
                ins.then_inc(self.sem, 1)


class Banks:

    def __init__(self, banks):
        self.banks, self.free, self.at = banks, [() for _ in banks], 0

    def take(self):
        n = self.at % len(self.banks)
        self.at += 1
        free = self.free[n]
        assert free is not None
        self.free[n] = None
        return n, self.banks[n], free

    def give(self, n, *toks):
        self.free[n] = toks


def constants():
    cols, at = [], {}

    def put(name, a):
        a = np.asarray(a, np.float32).reshape(128, -1)
        start = sum(c.shape[1] for c in cols)
        cols.append(a)
        at[name] = (start, start + a.shape[1])

    p = np.arange(128)
    put("ident", np.eye(128))
    put("d8", p[:, None] % 8 == np.arange(8)[None])
    put("rep", p[:, None] % 8 == p[None] % 8)
    put("iotap", np.stack([p, p + 128], 1))
    put("iota8", np.broadcast_to(np.arange(8), (128, 8)))
    half = 16
    theta = (1.0 / np.float32(10000.0) ** (np.float32(2.0) * np.arange(half, dtype=np.float32) / np.float32(32))).astype(np.float32)
    t = np.arange(L)
    ang = [(t.astype(np.float32)[:, None] * theta[None]).astype(np.float32),
           ((t + np.maximum(t - 63, 0)).astype(np.float32)[:, None] * theta[None]).astype(np.float32)]
    tab = np.stack([np.stack([np.cos(a.astype(np.float64)), np.sin(a.astype(np.float64))], 1) for a in ang], 1)
    put("rope", tab.reshape(2, 128, 4, 16).transpose(1, 0, 2, 3))
    ak = ((64 + np.arange(32)).astype(np.float32)[None] * theta[:, None]).astype(np.float32).astype(np.float64)
    c, s = np.cos(ak), np.sin(ak)
    z = np.zeros((32, 32))
    put("h1", np.concatenate([c, c, z, s, s, z]))
    put("h2", np.concatenate([-s, -s, z, c, c, z]))
    put("h3", np.concatenate([z, z + 1, z, z]))
    s192 = np.arange(192)
    put("im1", np.where(s192[None] <= p[:, None] + 64, 0.0, -BIG))
    put("im0", np.where(np.arange(64)[None] <= p[:, None] % 64, 0.0, -BIG))
    j, h, tt = p // 32, (p // 4) % 8, p % 4
    for r in range(4):
        for t0 in ([192 + 16 * r] + ([64 + 16 * r] if r < 2 else [])):
            tok = t0 + 4 * j + tt
            s0 = (t0 // 64 - 1) * 64
            sl = s0 + np.arange(128)
            ok = (sl[None] >= tok[:, None] - 63) & (sl[None] <= tok[:, None])
            col = np.arange(128)
            near = (col[None] // 32 == tt[:, None]) & (col[None] % 32 < tok[:, None] - 63)
            m = np.concatenate([ok, near], 1)
            if t0 < 96:
                sf = 64 + np.arange(32)
                m = np.concatenate([m, sf[None] > tok[:, None]], 1)
            put(f"mask{t0 if t0 < 96 else r}", np.where(m, 0.0, -BIG))
    put("t128", np.broadcast_to(128 * np.arange(16), (128, 16)))
    put("iotat", np.broadcast_to(np.arange(NT + 7), (128, NT + 7)))
    put("eps", np.full((128, 1), 1e-5))
    put("mpi", np.full((128, 1), -np.pi))
    return np.ascontiguousarray(np.concatenate(cols, 1)), at


CONST, CAT = constants()


def attention(nc, ctx, sem, group, queues, bank, a, c, ident, X0, XT, Y, g_c, g_x, transposed, stats):
    PE, S, V, G, SP = queues

    def sb(name, shape, dt=F32):
        return ctx.enter_context(nc.sbuf_tensor(name, shape, dt))

    ring = Banks(bank[0:6])
    pcring = Banks(bank[6:8])

    Wp = sb("Wp", [128, 128])
    Wi = sb("Wi", [128, 384])
    Wq2 = sb("Wq2", [64, 512])
    QT = sb("QT", [128, 2, NH * 512])
    Wuq, Wuk, Wuv = QT[0:64, 1, 0:512], QT[0:32, 1, 512:1024], QT[0:32, 1, 1024:1536]
    Wout = sb("Wout", [128, 4, 128])
    WuqT = sb("WuqT", [128, 4, 64])
    WukT = sb("WukT", [128, 4, 32])
    WuvT = sb("WuvT", [128, 4, 32])
    Wvo = sb("Wvo", [32, NH, 128])
    wix = sb("wix", [128, 4])
    RD = sb("RD", [128, 17])
    g_w1, g_w2, g_w3, g_rd = [group(n) for n in ("g_w1", "g_w2", "g_w3", "g_rd")]

    def load(g, dst, src):
        SP.dma(g, lambda e: e.dma_start(dst, src))

    load(g_w1, Wp[:, 0:64], a["W_dq"])
    load(g_w1, Wp[:, 64:96], a["W_dkv"])
    load(g_w1, Wp[:, 96:128], a["W_kr"])
    load(g_w1, Wi[:, 0:64], a["idx_wk"])
    load(g_w1, Wi[:, 64:128], a["idx_wk"])
    load(g_w1, Wi[:, 128:384], a["idx_wq"])
    load(g_w1, wix[:, :], a["idx_w"].partition_broadcast(128))
    load(g_rd, RD[:, 0:16], a["raw_delta"].partition_broadcast(128))
    for k in range(8):
        load(g_rd, RD[16 * k:16 * k + 16, 16:17], a["raw_delta"].rearrange("(i o) -> i o", o=1))
    load(g_w2, Wuq, a["W_uq"])
    load(g_w2, Wuk, a["W_uk"])
    load(g_w2, Wq2[:, 256:512], a["W_qr"])
    load(g_w3, Wuv, a["W_uv"])
    load(g_w3, Wout[:, :, :], a["W_out"].rearrange("(c p) d -> p c d", p=128))

    sd = sb("sd", [128, 17])
    cd = sb("cd", [128, 17])
    ra = sb("ra", [128, 8, 16])
    rb = sb("rb", [128, 8, 16])
    RT = sb("RT", [128, 2, 2, 2, 16])
    GT = sb("GT", [128, 32])
    t = S(lambda e: e.activation(RD[:, :], RD[:, :], ACT.Exp, scale=-1.0), g_rd)
    t = V(lambda e: e.tensor_scalar(RD[:, :], RD[:, :], 1.0, None, ALU.add), t)
    t = V(lambda e: e.reciprocal(RD[:, :], RD[:, :]), t)
    t1 = S(lambda e: e.activation(sd[:, :], RD[:, :], ACT.Sin, scale=float(np.float32(2 * np.pi)), bias=c("mpi")), t, g_c)
    t2 = S(lambda e: e.activation(cd[:, :], RD[:, :], ACT.Sin, scale=float(np.float32(np.pi))), t)
    t = V(lambda e: e.tensor_tensor(cd[:, :], cd[:, :], cd[:, :], ALU.mult), t2)
    t = V(lambda e: e.tensor_scalar(cd[:, :], cd[:, :], -2.0, 1.0, ALU.mult, ALU.add), t)
    rope = c("rope").rearrange("p (k i) -> p k i", i=16)
    t3 = V(lambda e: e.tensor_tensor(ra[:, :, :], rope, cd[:, 0:16].unsqueeze(1).to_broadcast([128, 8, 16]), ALU.mult), t, g_c)
    t4 = V(lambda e: e.tensor_tensor(rb[:, :, :], rope, sd[:, 0:16].unsqueeze(1).to_broadcast([128, 8, 16]), ALU.mult), t1)
    rav = ra[:, :, :].rearrange("p (k f) i -> p k f i", f=2)
    rbv = rb[:, :, :].rearrange("p (k f) i -> p k f i", f=2)
    RTv = RT[:, :, :, :, :].rearrange("p a k f i -> p (a k) f i")
    t5 = V(lambda e: e.tensor_tensor(RTv[:, :, 0, :], rav[:, :, 0, :], rbv[:, :, 1, :], ALU.subtract), t3, t4)
    t_rt = V(lambda e: e.tensor_tensor(RTv[:, :, 1, :], rbv[:, :, 0, :], rav[:, :, 1, :], ALU.add), t3, t4)
    t = V(lambda e: e.tensor_scalar(GT[:, :], c("h1"), cd[:, 16:17], None, ALU.mult), t)
    t = V(lambda e: e.tensor_tensor(GT[:, :], GT[:, :], c("h3"), ALU.add), t)
    t_gt = V(lambda e: e.scalar_tensor_tensor(out=GT[:, :], in0=c("h2"), scalar=sd[:, 16:17], in1=GT[:, :],
                                              op0=ALU.mult, op1=ALU.add), t)

    def turned(src, dst, rows, g):
        n, bk, free = ring.take()
        for k in range(4):
            t = PE(lambda e, k=k: e.transpose(bk[:, k * rows:k * rows + rows], src[:, k * 128:k * 128 + 128],
                                              ident[0:rows, 0:rows]), *((g, g_c) + free if k == 0 else ()))
        t = V(lambda e: e.tensor_copy(dst[:, :, :], bk[:, 0:4 * rows].rearrange("p (k r) -> p k r", k=4)), t)
        ring.give(n, t)
        return t

    t1 = turned(Wuq, WuqT, 64, g_w2)
    t2 = turned(Wuk, WukT, 32, g_w2)
    t3 = turned(Wuv, WuvT, 32, g_w3)
    for f in range(2):
        r = slice(64 * f, 64 * f + 64)
        n, bk, free = ring.take()
        for k in range(4):
            t = PE(lambda e, k=k, r=r, bk=bk: e.matmul(bk[0:64, 32 * k:32 * k + 32], WuqT[r, k, :], WukT[r, k, :],
                                                       start=True, stop=True), *((t1, t2) + free if k == 0 else ()))
        t_wabs = V(lambda e, f=f, bk=bk: e.tensor_copy(
            Wq2[:, 0:256].rearrange("p (k f c) -> p f k c", f=2, c=32)[:, f, :, :],
            bk[0:64, 0:128].rearrange("p (k c) -> p k c", c=32)), t)
        ring.give(n, t_wabs)
    for f in range(2):
        r = slice(64 * f, 64 * f + 64)
        n, bk, free = ring.take()
        for k in range(4):
            t = PE(lambda e, r=r, k=k, bk=bk: e.matmul(bk[0:32, 128 * k:128 * k + 128], WuvT[r, k, :], Wout[r, k, :],
                                                       start=True, stop=True), *((t3, g_w3) + free if k == 0 else ()))
        t_wvo = V(lambda e, f=f, bk=bk: e.tensor_copy(Wvo[:, f:NH:2, :],
                                                      bk[0:32, :].rearrange("p (h d) -> p h d", h=4)), t)
        ring.give(n, t_wvo)

    cqT = sb("cqT", [64, 512])
    kiT = sb("kiT", [128, 512])
    qiT = sb("qiT", [128, 2, 512])
    AB = sb("AB", [128, 4, 288])
    M = sb("M", [128, 4, 288])
    SRC = sb("SRC", [128, 4, 64])
    RS = sb("RS", [128, 4, 64])
    R2 = sb("R2", [128, 4, 64])
    Qtok = sb("Qtok", [128, 4, NH, 128])
    pa = sb("pa", [128, NH, 2, 16])
    pb = sb("pb", [128, NH, 2, 16])
    ka = sb("ka", [128, 2, 2, 16])
    kb = sb("kb", [128, 2, 2, 16])
    Kt = sb("Kt", [128, 4, 128])
    Kf = sb("Kf", [128, 2, 128])
    RL = sb("RL", [128, 4, 192])
    I1 = sb("I1", [128, 3, 192])
    V8 = sb("V8", [128, 3, 32])
    IX = sb("IX", [128, 3, 32], U32)
    IXb = sb("IXb", [128, 3, 32], BF16)
    KL = sb("KL", [128, 2, 512])
    KF = sb("KF", [128, 2, 2, 32])
    KG = sb("KG", [128, 2, 4, 3, 128], BF16)
    CK = sb("CK", [128, 2, 4, 32])
    CM = sb("CM", [128, 2, 2, 32])
    BC = sb("BC", [128, 2, 6144], BF16)
    OH = sb("OH", [128, 6144], BF16)
    OH2 = sb("OH2", [64, 2048], BF16)
    NB = 3
    Gs = sb("Gs", [128, NB, 512])
    Vg = sb("Vg", [128, NB, 4, 32])
    P = sb("P", [128, NB, 288])
    mx = sb("mx", [128, NB, 4])
    PT = sb("PT", [128, NB, 384])
    pcT = sb("pcT", [32, 2, NH, 128])
    idxd = nc.dram_tensor("idxd", [B, 192 * 32], BF16, kind="Internal").ap()

    G(lambda e: e.memset(Kt[:, :, :], 0.0))
    t_zero = G(lambda e: e.memset(Kf[:, :, :], 0.0))

    fences = {}

    def prepare(p):
        q = p % 2
        before = fences.get(("prepare", p - 1), ()) + fences.get(("attend", 2 * p - 3), ())
        for queue in (PE, S, V, G, SP):
            queue.hold(*before)
        t_x = transposed(ring, X0, p, g_x[p], g_c)
        xs = slice(512 * p, 512 * p + 512)

        def project(w, rows, dst, eng):
            n, bk, free = ring.take()
            t = PE(lambda e: e.matmul(bk[0:rows, :], w, XT[:, xs], start=True, stop=True), t_x, g_w1, *free)
            if eng is S:
                t = S(lambda e: e.activation(dst, bk[0:rows, :], ACT.Copy), t)
            else:
                t = V(lambda e: e.tensor_copy(dst, bk[0:rows, :]), t)
            ring.give(n, t)
            return t

        t_cq = project(Wp[:, 0:64], 64, cqT[:, :], V)
        t_ki = project(Wi[:, 0:128], 128, kiT[:, :], S)
        t_q0 = project(Wi[:, 128:256], 128, qiT[:, 0, :], V)
        t_q1 = project(Wi[:, 256:384], 128, qiT[:, 1, :], S)

        def best(k, rows_of, width, mask):
            banks = []
            m = 128 if width == 192 else 64
            for f in range(2):
                n, bk, free = ring.take()
                r = slice(64 * f, 64 * f + 64)
                first = (t_ki, t_q0, t_q1) + free
                for g in range(2):
                    for o, b in rows_of:
                        tq = 256 * b + m
                        t = PE(lambda e, r=r, g=g, o=o, b=b, tq=tq, bk=bk: e.matmul(
                            bk[o:o + m, g * width:g * width + width], qiT[r, g, tq:tq + m],
                            kiT[r, 256 * b:256 * b + width], start=True, stop=True), *first)
                        first = ()
                t = S(lambda e, f=f, bk=bk: e.activation(
                    RL[:, f:4:2, 0:width], bk[:, 0:2 * width].rearrange("p (h s) -> p h s", h=2), ACT.Relu), t, *used_rl)
                ring.give(n, t)
                banks.append(t)
            I = I1[:, k, 0:width]
            t = V(lambda e: e.scalar_tensor_tensor(out=I, in0=RL[:, 0, 0:width], scalar=wix[:, 0:1], in1=mask,
                                                   op0=ALU.mult, op1=ALU.add), *banks)
            for h in range(1, 4):
                t = V(lambda e, h=h: e.scalar_tensor_tensor(out=I, in0=RL[:, h, 0:width], scalar=wix[:, h:h + 1], in1=I,
                                                            op0=ALU.mult, op1=ALU.add), t)
            used_rl[:] = [t]
            for r in range(4):
                v8 = V8[:, k, 8 * r:8 * r + 8]
                t = V(lambda e, v8=v8: e.max(v8, I), t)
                t = V(lambda e, v8=v8, r=r: e.max_index(IX[:, k, 8 * r:8 * r + 8], v8, I), t)
                if r < 3:
                    t = V(lambda e, v8=v8: e.match_replace(I, v8, I, LOW), t)
            return V(lambda e: e.tensor_copy(IXb[:, k, :], IX[:, k, :]), t)

        used_rl = []
        t_i = [best(0, [(0, 0)], 192, c("im1")), best(1, [(0, 1)], 192, c("im1")),
               best(2, [(0, 0), (64, 1)], 64, c("im0"))]
        g_i = group(f"g_i{p}")
        for o in range(2):
            b = 2 * p + o
            SP.dma(g_i, lambda e, b=b, o=o: e.dma_start(idxd[b, 2048:6144].rearrange("(t k) -> t k", k=32), IXb[:, o, :]), t_i[o])
            SP.dma(g_i, lambda e, b=b, o=o: e.dma_start(idxd[b, 0:2048].rearrange("(t k) -> t k", k=32),
                                                        IXb[64 * o:64 * o + 64, 2, :]), t_i[2])
        nk, bkv, free = ring.take()
        for i in range(4):
            t = PE(lambda e, i=i: e.matmul(bkv[:, 64 * i:64 * i + 64], XT[:, 512 * p + 128 * i:512 * p + 128 * i + 128],
                                           Wp[:, 64:128], start=True, stop=True), *free)
        for o in range(2):
            t = PE(lambda e, o=o: e.matmul(bkv[:, 256 + 32 * o:288 + 32 * o],
                                           XT[:, 512 * p + 256 * o + 64:512 * p + 256 * o + 192], Wp[:, 64:96],
                                           start=True, stop=True))
        kv = bkv[:, 0:256].rearrange("p (i f) -> p i f", i=4)
        S(lambda e: e.activation(CM[:, q, :, :], bkv[:, 256:320].rearrange("p (o f) -> p o f", o=2), ACT.Copy), t)
        S(lambda e: e.activation(CK[:, q, :, :], kv[:, :, 0:32], ACT.Copy))
        S(lambda e: e.activation(SRC[:, :, 32:64], kv[:, :, 0:32], ACT.Copy))
        S(lambda e: e.activation(Kt[:, :, 32:64], kv[:, :, 0:32], ACT.Copy), t_zero)
        t_ck = S(lambda e: e.activation(Kf[:, :, 32:64], kv[:, 0:4:2, 0:32], ACT.Copy))
        t = S(lambda e: e.activation(AB[:, :, 0:32], kv[:, :, 32:64], ACT.Abs))
        qb = []
        for i in range(4):
            nq, bq, fq = ring.take()
            t = PE(lambda e, i=i, bq=bq: e.matmul(bq[:, :], cqT[:, 128 * i:128 * i + 128], Wq2[:, :], start=True, stop=True),
                   t_cq, t_wabs, *fq)
            t = S(lambda e, i=i, bq=bq: e.activation(AB[:, i, 32:288], bq[:, 256:512], ACT.Abs), t)
            t2 = S(lambda e, i=i, bq=bq: e.activation(Qtok[:, i, :, 32:64],
                                                      bq[:, 0:256].rearrange("p (h f) -> p h f", h=NH), ACT.Copy))
            qb.append((nq, bq, t2))
        t = S(lambda e: e.activation(AB[:, :, :], AB[:, :, :], ACT.Exp, scale=-1.0), t)
        t = S(lambda e: e.activation(AB[:, :, :], AB[:, :, :], ACT.Ln, bias=1.0), t)
        t_k = V(lambda e: e.scalar_tensor_tensor(out=M[:, :, 0:32], in0=kv[:, :, 32:64], scalar=0.0, in1=AB[:, :, 0:32],
                                                 op0=ALU.max, op1=ALU.add), t)
        ring.give(nk, t_k, t_ck)
        t_m = []
        for i, (nq, bq, t2) in enumerate(qb):
            t_m.append(V(lambda e, i=i, bq=bq: e.scalar_tensor_tensor(out=M[:, i, 32:288], in0=bq[:, 256:512], scalar=0.0,
                                                                      in1=AB[:, i, 32:288], op0=ALU.max, op1=ALU.add)))
            ring.give(nq, t_m[-1], t2)

        def part3(k):
            return KG[:, q, :, k, 0:64]

        def both(k):
            return KG[:, q, :, k, :].rearrange("p i (r f) -> p i r f", r=2)

        def twice(s):
            return s.unsqueeze(2).to_broadcast([128, 4, 2, 64])

        t = V(lambda e: e.tensor_copy(SRC[:, :, 0:32], M[:, :, 0:32]), t_k)
        t = V(lambda e: e.tensor_copy(both(0), twice(SRC[:, :, :])), t, t_ck)
        t = V(lambda e: e.tensor_tensor(RS[:, :, :], SRC[:, :, :], part3(0), ALU.subtract), t)
        t = V(lambda e: e.tensor_copy(both(1), twice(RS[:, :, :])), t)
        t = V(lambda e: e.tensor_tensor(R2[:, :, :], RS[:, :, :], part3(1), ALU.subtract), t)
        t_kg = V(lambda e: e.tensor_copy(both(2), twice(R2[:, :, :])), t)

        t = t_k
        for o in range(2):
            mk = M[:, 2 * o:2 * o + 2, 0:32].rearrange("p i (f j) -> p i f j", f=2)
            cs, sn = [RT[:, :, 0, f, :].unsqueeze(2).to_broadcast([128, 2, 2, 16]) for f in range(2)]
            t = G(lambda e, mk=mk, cs=cs: e.tensor_tensor(ka[:, :, :, :], mk, cs, ALU.mult), t, t_rt)
            t = G(lambda e, mk=mk, sn=sn: e.tensor_tensor(kb[:, :, :, :], mk, sn, ALU.mult), t)
            t = G(lambda e, o=o: e.tensor_tensor(Kt[:, 2 * o:2 * o + 2, 96:112], ka[:, :, 0, :], kb[:, :, 1, :], ALU.subtract), t)
            t = G(lambda e, o=o: e.tensor_tensor(Kt[:, 2 * o:2 * o + 2, 112:128], kb[:, :, 0, :], ka[:, :, 1, :], ALU.add), t)
        t_kt = G(lambda e: e.tensor_copy(Kf[:, :, 0:32], Kt[:, 0:4:2, 96:128]), t)
        t_q = []
        for i in range(4):
            mq = M[:, i, 32:288].rearrange("p (h f j) -> p h f j", h=NH, f=2)

            def tab(k, f, i=i):
                return RT[:, i % 2, k, f, :].unsqueeze(1).unsqueeze(1).to_broadcast([128, NH, 2, 16])

            for k in range(2):
                E = V if (k == 0 and i % 2) else G
                x_a, x_b = (pa, pb) if E is G else (qa, qbuf)
                t = E(lambda e, mq=mq, k=k, tab=tab, x_a=x_a: e.tensor_tensor(x_a[:, :, :, :], mq, tab(k, 0), ALU.mult), t_m[i], t_rt)
                t = E(lambda e, mq=mq, k=k, tab=tab, x_b=x_b: e.tensor_tensor(x_b[:, :, :, :], mq, tab(k, 1), ALU.mult), t)
                at = 96 if k else 0
                t = E(lambda e, i=i, at=at, x_a=x_a, x_b=x_b: e.tensor_tensor(Qtok[:, i, :, at:at + 16], x_a[:, :, 0, :], x_b[:, :, 1, :], ALU.subtract), t)
                t = E(lambda e, i=i, at=at, x_a=x_a, x_b=x_b: e.tensor_tensor(Qtok[:, i, :, at + 16:at + 32], x_b[:, :, 0, :], x_a[:, :, 1, :], ALU.add), t)
                if k == 0:
                    t = E(lambda e, i=i, x_a=x_a, x_b=x_b: e.tensor_tensor(Qtok[:, i, :, 64:80], x_b[:, :, 0, :], x_a[:, :, 1, :], ALU.add), t)
                    t = E(lambda e, i=i, x_a=x_a, x_b=x_b: e.tensor_tensor(Qtok[:, i, :, 80:96], x_b[:, :, 1, :], x_a[:, :, 0, :], ALU.subtract), t)
                t_q.append(t)
        n, bk, free = ring.take()
        for i in range(4):
            t = PE(lambda e, i=i, bk=bk: e.transpose(bk[:, 128 * i:128 * i + 128], Kt[:, i, :], ident), t_kt, t_ck, *free)
        t_kl = S(lambda e, bk=bk: e.activation(KL[:, q, :], bk[:, :], ACT.Copy), t)
        ring.give(n, t_kl)
        n, bk, free = ring.take()
        for o in range(2):
            t = PE(lambda e, o=o, bk=bk: e.transpose(bk[:, 128 * o:128 * o + 128], Kf[:, o, :], ident), *free)
        t_kf = S(lambda e, bk=bk: e.activation(KF[:, q, :, :], bk[:, 0:256].rearrange("p (o s) -> p o s", o=2)[:, :, 64:96], ACT.Copy), t)
        ring.give(n, t_kf)
        for i in range(4):
            for f in range(2):
                n, bk, free = ring.take()
                for h in range(4):
                    t = PE(lambda e, i=i, f=f, h=h, bk=bk: e.transpose(bk[:, 128 * h:128 * h + 128], Qtok[:, i, 4 * f + h, :], ident),
                           *(free + tuple(t_q) + (qb[i][2],) if h == 0 else ()))
                dst = QT[:, q, :].rearrange("p (g h t) -> p h g t", h=NH, t=4)[:, 4 * f:4 * f + 4, 32 * i:32 * i + 32, :]
                src = bk[:, :].rearrange("p (h g t) -> p h g t", h=4, t=4)
                if f:
                    t_qt = S(lambda e, dst=dst, src=src: e.activation(dst, src, ACT.Copy), t)
                else:
                    t_qv = t_qt = V(lambda e, dst=dst, src=src: e.tensor_copy(dst, src), t)
                ring.give(n, t_qt)
        fences["prepare", p] = (t, t_qt, t_qv, t_q[-1], t_kt, g_i)
        fences["ready", p] = (t_qt, t_qv, t_kl, t_kf, t_kg, t_ck)
        fences["far", p] = g_i

    qa = sb("qa", [128, NH, 2, 16])
    qbuf = sb("qbuf", [128, NH, 2, 16])
    slot = {}
    last_out = []
    g_b = [group(f"g_b{b}") for b in range(B)]

    def spread(b):
        SP.dma(g_b[b], lambda e: e.dma_start(BC[:, b % 2, :], idxd[b, :].partition_broadcast(128)), fences["far", b // 2],
               *fences.get(("onehot", b - 2), ()))

    def attend(b):
        p, o, q = b // 2, b % 2, (b // 2) % 2
        ready = fences["ready", p]
        if b == 0:
            spread(0)
        if b < B - 1:
            spread(b + 1)
        t1 = V(lambda e: e.tensor_scalar(OH[:, :], BC[:, o, :], c("iotap")[:, 0:1], None, ALU.is_equal), g_b[b],
               *fences.get(("gathered", b - 1), ()))
        t_oh = V(lambda e: e.tensor_scalar(OH2[:, :], BC[0:64, o, 4096:6144], c("iotap", slice(0, 64))[:, 1:2], None,
                                           ALU.is_equal))
        fences["onehot", b] = (t_oh,)
        state = {}

        def old(name, r, *keys):
            return tuple(slot.get((name, r % NB, k)) for k in keys if slot.get((name, r % NB, k)))

        def gather(r):
            t0 = 16 * r
            if t0 < 64:
                return
            cols = slice((t0 - 64) * 32, (t0 - 64) * 32 + 512)
            n, bk, free = ring.take()
            two = t0 >= 192
            for k in range(3):
                t = PE(lambda e, k=k: e.matmul(bk[:, :], KG[:, q, 2 * o, k, :], OH[:, cols], start=(k == 0),
                                               stop=(k == 2 and not two)), *((t1,) + ready + free if k == 0 else ()))
            if two:
                c2 = slice((t0 - 192) * 32, (t0 - 192) * 32 + 512)
                for k in range(3):
                    t = PE(lambda e, k=k: e.matmul(bk[:, :], KG[0:64, q, 2 * o + 1, k, :], OH2[:, c2], start=False,
                                                   stop=(k == 2)), t_oh)
            state["pe", r] = t
            t = V(lambda e: e.tensor_tensor(Gs[:, r % NB, :].rearrange("p (t k) -> p t k", k=32),
                                            bk[:, :].rearrange("p (t k) -> p t k", k=32),
                                            GT[:, :].unsqueeze(1).to_broadcast([128, 16, 32]), ALU.mult), t, t_gt,
                  *old("Gs", r, "s", "v"))
            ring.give(n, t)
            state["Gs", r] = t

        def score(r):
            t0 = 16 * r
            tq = 256 * o + t0
            far = t0 >= 64
            future = far and t0 < 96
            s0 = 256 * o + (max(t0 // 64 - 1, 0)) * 64
            near = 128 if far else 96
            width = near + (128 if far else 0) + (32 if future else 0)
            n, bk, free = ring.take()
            rows = QT[:, q, 8 * tq:8 * tq + 128]
            t = PE(lambda e: e.matmul(bk[:, 0:near], rows, KL[:, q, s0:s0 + near], start=True, stop=True), *(ready + free))
            if far:
                nv, bv, fv = ring.take()
                for j in range(4):
                    PE(lambda e, j=j: e.matmul(bk[32 * j:32 * j + 32, 128:256], QT[:, q, 8 * tq + 32 * j:8 * tq + 32 * j + 32],
                                               Gs[:, r % NB, 128 * j:128 * j + 128], start=True, stop=True),
                       *((state["Gs", r],) if j == 0 else ()))
                if future:
                    PE(lambda e: e.matmul(bk[:, 256:288], rows, KF[:, q, o, :], start=True, stop=True))
                t = PE(lambda e: e.transpose(bv[:, 0:32], Gs[32:64, r % NB, 0:128], ident[32:64, 32:64]), *fv)
                for j in range(1, 4):
                    t = PE(lambda e, j=j: e.transpose(bv[:, 32 * j:32 * j + 32], Gs[32:64, r % NB, 128 * j:128 * j + 128],
                                                      ident[32:64, 32:64]))
                slot["Gs", r % NB, "s"] = t
                tv = S(lambda e: e.activation(Vg[:, r % NB, :, :], bv[:, 0:128].rearrange("p (j f) -> p j f", j=4), ACT.Copy), t,
                       *old("Vg", r, "pe"))
                ring.give(nv, tv)
                state["Vg", r] = tv
            waits = (t,) + old("P", r, "pe")
            Pr, m = P[:, r % NB, 0:width], mx[:, r % NB, :]
            if far:
                mask = c(f"mask{t0 if future else r % 4}")
                t = V(lambda e: e.tensor_tensor_reduce(out=Pr, in0=bk[:, 0:width], in1=mask, scale=1.0, scalar=LOW, op0=ALU.add,
                                                       op1=ALU.max, accum_out=m[:, 0:1]), *waits)
                src = Pr
            else:
                t = V(lambda e: e.tensor_reduce(m[:, 0:1], bk[:, 0:width], AX, ALU.max), *waits)
                src = bk[:, 0:width]
            t2 = V(lambda e: e.tensor_scalar(m[:, 1:2], m[:, 0:1], -SCALE, None, ALU.mult), t)
            t3 = S(lambda e: e.activation(Pr, src, ACT.Exp, scale=SCALE, bias=m[:, 1:2], accum_out=m[:, 2:3]), t2)
            ring.give(n, t if far else t3)
            t4 = V(lambda e: e.reciprocal(m[:, 3:4], m[:, 2:3]), t3)
            state["P", r] = V(lambda e: e.tensor_scalar(Pr, Pr, m[:, 3:4], None, ALU.mult), t4)
            state["w", r] = (near, far, future)

        def turn(r):
            near, far, future = state["w", r]
            n, bk, free = ring.take()
            t = PE(lambda e: e.transpose(bk[0:near, 0:128], P[:, r % NB, 0:near], ident), state["P", r], *free)
            if far:
                t = PE(lambda e: e.transpose(bk[:, 128:256], P[:, r % NB, 128:256], ident))
            if future:
                t = PE(lambda e: e.transpose(bk[0:32, 256:384], P[:, r % NB, 256:288], ident))
            slot["P", r % NB, "pe"] = t
            waits = (t,) + old("PT", r, "pe")
            if far:
                t = S(lambda e: e.activation(PT[:, r % NB, 0:256], bk[:, 0:256], ACT.Copy), *waits)
                if future:
                    t = S(lambda e: e.activation(PT[0:32, r % NB, 256:384], bk[0:32, 256:384], ACT.Copy))
            else:
                t = S(lambda e: e.activation(PT[0:near, r % NB, 0:128], bk[0:near, 0:128], ACT.Copy), *waits)
            ring.give(n, t)
            state["PT", r] = t

        def value(r):
            near, far, future = state["w", r]
            t0 = 16 * r
            if r % 4 == 0:
                state["pc"] = pcring.take()
            n, bk, free = state["pc"]
            i = t0 // 64
            v = CK[0:near, q, 2 * o, :] if i < 2 else CM[:, q, o, :] if i == 2 else CK[:, q, 2 * o + 1, :]
            if i == 3:
                v = CK[:, q, 2 * o + 1, :]
            col = 128 * (r % 4)
            t = PE(lambda e: e.matmul(bk[0:32, col:col + 128], v, PT[0:near, r % NB, 0:128], start=True, stop=not far),
                   state["PT", r], *(free if r % 4 == 0 else ()))
            if far:
                for j in range(4):
                    t = PE(lambda e, j=j: e.matmul(bk[0:32, col + 32 * j:col + 32 * j + 32], Vg[:, r % NB, j, :],
                                                   PT[:, r % NB, 128 + 32 * j:160 + 32 * j], start=False,
                                                   stop=(j == 3 and not future)),
                           *((state["Vg", r],) if j == 0 else ()))
            if future:
                t = PE(lambda e: e.matmul(bk[0:32, col:col + 128], CM[0:32, q, o, :], PT[0:32, r % NB, 256:384], start=False,
                                          stop=True))
            slot["PT", r % NB, "pe"] = slot["Vg", r % NB, "pe"] = t
            if r % 4 == 3:
                k = (r // 4) % 2
                t = V(lambda e: e.tensor_copy(pcT[:, r // 8, :, 64 * k:64 * k + 64].rearrange("p h (g t) -> p h g t", t=4),
                                        bk[0:32, :].rearrange("p (g h t) -> p h g t", h=NH, t=4)), t,
                      *([last_out[-1]] if last_out else []))
                pcring.give(n, t)
                if k == 1:
                    project_out(r // 8, t)

        def project_out(f, t):
            i = 2 * b + f
            n, bk, free = ring.take()
            for h in range(NH):
                t = PE(lambda e, h=h: e.matmul(bk[:, 0:128], pcT[:, f, h, :], Wvo[:, h, :], start=(h == 0),
                                               stop=(h == NH - 1)), *((t, t_wvo) + free if h == 0 else ()))
            last_out.append(t)
            t = V(lambda e: e.tensor_tensor(Y[:, i, :], bk[:, 0:128], X0[:, i, :], ALU.add), t, g_x[i // 4])
            ring.give(n, t)
            state["y"] = stats(i, t)

        for k in range(16 + 3):
            if k < 16:
                gather(k)
            if 1 <= k < 17:
                score(k - 1)
            if 2 <= k < 18:
                turn(k - 2)
            if 3 <= k:
                value(k - 3)
        fences["gathered", b] = (state["pe", 15],)
        fences["attend", b] = (last_out[-1], state["y"], state["PT", 15])
        return state["y"]

    prepare(0)
    for p in range(4):
        if p < 3:
            prepare(p + 1)
        attend(2 * p)
        t = attend(2 * p + 1)
    return t


def experts(nc, ctx, sem, group, queues, bank, a, c, ident, X0, XT, Y, transposed, stats):
    PE, S, V, G, SP = queues
    E, NF = 8, 512
    TS = NT + E - 1

    def sb(name, shape, dt=F32):
        return ctx.enter_context(nc.sbuf_tensor(name, shape, dt))

    ring = Banks(bank[0:8])
    W1 = sb("W1", [128, E * NF])
    W2 = sb("W2", [128, E * 4 * 128])
    Wr = sb("Wr", [128, E])
    br = sb("br", [1, E])
    one = sb("one", [128, 128])
    oneb = sb("oneb", [128, 128], BF16)
    before = sb("before", [128, 128], BF16)
    zero = sb("zero", [128, 512])
    route = sb("route", [128, NT, E])
    top = sb("top", [128, NT, 8])
    topi = sb("topi", [128, NT, 8], U32)
    pick = sb("pick", [128, NT])
    hot = sb("hot", [128, NT, E])
    hotb = sb("hotb", [128, NT, E], BF16)
    rank = sb("rank", [128, NT, E])
    cnt = sb("cnt", [128, E])
    cmp16 = sb("cmp16", [128, E, 16])
    tiles = sb("tiles", [128, E])
    ends = sb("ends", [128, E])
    starts = sb("starts", [128, E])
    pos = sb("pos", [128, NT])
    posu = sb("posu", [128, NT], U32)
    cmpt = sb("cmpt", [128, TS, E])
    tef = sb("tef", [128, TS])
    tei = sb("tei", [128, TS], I32)
    NB = 3
    Xs = sb("Xs", [128, NB, 128])
    XsT = sb("XsT", [128, NB, 128])
    H = sb("H", [128, NB, NF])
    HT = sb("HT", [128, NB, 4, 128])
    Ys = sb("Ys", [128, NB, 128])
    Yg = sb("Yg", [128, NT, 128])
    xs_d = nc.dram_tensor("xs_d", [TS * 128, 128], F32, kind="Internal").ap()
    ys_d = nc.dram_tensor("ys_d", [TS * 128, 128], F32, kind="Internal").ap()

    g_r, g_1, g_2, g_z, g_s, g_l, g_y, g_g = [group(f"g_f{k}") for k in ("r", "1", "2", "z", "s", "l", "y", "g")]
    SP.dma(g_r, lambda e: e.dma_start(Wr[:, :], a["Wr"]))
    SP.dma(g_r, lambda e: e.dma_start(br[:, :], a["br"].rearrange("(o n) -> o n", o=1)))
    t_z = G(lambda e: e.memset(zero[:, :], 0.0))
    zv = xs_d.rearrange("(p r) d -> p (r d)", p=128)
    for k in range(0, TS * 128, 512):
        w = min(512, TS * 128 - k)
        SP.dma(g_z, lambda e, k=k, w=w: e.dma_start(zv[:, k:k + w], zero[:, 0:w]), t_z)
    for e0 in range(0, E, 4):
        SP.dma(g_1, lambda e, e0=e0: e.dma_start(W1[:, e0 * NF:(e0 + 4) * NF].rearrange("p (e f) -> p e f", e=4),
                                                 a["W1"][e0:e0 + 4].rearrange("e p f -> p e f")))
    for e0 in range(0, E, 4):
        SP.dma(g_2, lambda e, e0=e0: e.dma_start(
            W2[:, e0 * 512:(e0 + 4) * 512].rearrange("p (e c d) -> p (e c) d", e=4, c=4),
            a["W2"][e0:e0 + 4].rearrange("e (c p) d -> p (e c) d", p=128)))
    G(lambda e: e.memset(one[:, :], 1.0))
    G(lambda e: e.memset(oneb[:, :], 1.0))
    t_one = G(lambda e: e.affine_select(out=before[:, :], in_=oneb[:, :], compare_op=ALU.is_gt, fill=0.0, base=0,
                                        pattern=[[1, 128]], channel_multiplier=-1))

    for p in range(4):
        t_xt = transposed(ring, X0, p)
    n, bk, free = ring.take()
    for i in range(NT):
        PE(lambda e, i=i, bk=bk: e.matmul(bk[:, E * i:E * i + E], one[0:1, :], br[:, :], start=True, stop=False),
           *((t_xt, g_r, t_one) + free if i == 0 else ()))
        t = PE(lambda e, i=i, bk=bk: e.matmul(bk[:, E * i:E * i + E], XT[:, 128 * i:128 * i + 128], Wr[:, :], start=False, stop=True))
    t = S(lambda e, bk=bk: e.activation(route[:, :, :], bk[:, 0:128].rearrange("p (i e) -> p i e", e=E), ACT.Sigmoid), t)
    ring.give(n, t)
    for i in range(NT):
        V(lambda e, i=i: e.max(top[:, i, :], route[:, i, :]), t)
        V(lambda e, i=i: e.max_index(topi[:, i, :], top[:, i, :], route[:, i, :]))
    V(lambda e: e.tensor_copy(pick[:, :], topi[:, :, 0]))
    V(lambda e: e.tensor_tensor(hot[:, :, :], c("iota8").unsqueeze(1).to_broadcast([128, NT, E]),
                                pick[:, :].unsqueeze(2).to_broadcast([128, NT, E]), ALU.is_equal))
    t_hot = V(lambda e: e.tensor_copy(hotb[:, :, :], hot[:, :, :]))

    n, bk, free = ring.take()
    hots = hotb[:, :, :].rearrange("p i e -> p (i e)")
    PE(lambda e, bk=bk: e.matmul(bk[:, 0:128], before[:, :], hots, start=True, stop=False), t_hot, t_one, *free)
    for k in range(1, NT):
        t = PE(lambda e, k=k, bk=bk: e.matmul(bk[:, E * k:128], oneb[:, :], hots[:, 0:128 - E * k], start=False, stop=(k == NT - 1)))
    t = V(lambda e, bk=bk: e.tensor_copy(rank[:, :, :].rearrange("p i e -> p (i e)"), bk[:, 0:128]), t)
    ring.give(n, t)
    n, bk, free = ring.take()
    for k in range(NT):
        t = PE(lambda e, k=k, bk=bk: e.matmul(bk[:, 0:E], oneb[:, :], hots[:, E * k:E * k + E], start=(k == 0), stop=(k == NT - 1)), *free)
    t = V(lambda e, bk=bk: e.tensor_copy(cnt[:, :], bk[:, 0:E]), t)
    ring.give(n, t)
    V(lambda e: e.tensor_tensor(cmp16[:, :, :], cnt[:, :].unsqueeze(2).to_broadcast([128, E, 16]),
                                c("t128").unsqueeze(1).to_broadcast([128, E, 16]), ALU.is_gt))
    V(lambda e: e.tensor_reduce(tiles[:, :], cmp16[:, :, :], AX, ALU.add))
    V(lambda e: e.tensor_tensor_scan(ends[:, :], one[:, 0:E], tiles[:, :], 0.0, ALU.mult, ALU.add), t_one)
    V(lambda e: e.tensor_tensor(starts[:, :], ends[:, :], tiles[:, :], ALU.subtract))
    V(lambda e: e.tensor_scalar(starts[:, :], starts[:, :], 128.0, None, ALU.mult))
    V(lambda e: e.tensor_tensor(rank[:, :, :], rank[:, :, :], starts[:, :].unsqueeze(1).to_broadcast([128, NT, E]), ALU.add))
    V(lambda e: e.tensor_tensor(rank[:, :, :], rank[:, :, :], hot[:, :, :], ALU.mult))
    V(lambda e: e.tensor_reduce(pos[:, :], rank[:, :, :], AX, ALU.add))
    t_pos = V(lambda e: e.tensor_copy(posu[:, :], pos[:, :]))
    for i in range(NT):
        G.dma(g_s, lambda e, i=i: e.indirect_dma_start(xs_d, bass.IndirectOffsetOnAxis(posu[:, i:i + 1], 0), X0[:, i, :], None),
              t_pos, g_z)
    V(lambda e: e.tensor_tensor(cmpt[:, :, :], ends[:, :].unsqueeze(1).to_broadcast([128, TS, E]),
                                c("iotat").unsqueeze(2).to_broadcast([128, TS, E]), ALU.is_le))
    V(lambda e: e.tensor_reduce(tef[:, :], cmpt[:, :, :], AX, ALU.add))
    V(lambda e: e.tensor_scalar(tef[:, :], tef[:, :], float(E - 1), float(NF), ALU.min, ALU.mult))
    t_te = V(lambda e: e.tensor_copy(tei[:, :], tef[:, :]))

    at = {}
    g_ld = [group(f"g_ld{k}") for k in range(TS)]
    g_st = [group(f"g_st{k}") for k in range(TS)]
    st = {}

    def load(k):
        SP.dma(g_ld[k], lambda e: e.dma_start(Xs[:, k % NB, :], xs_d[128 * k:128 * k + 128, :]), g_s,
               *([st["x", k - NB]] if k >= NB else []))

    def first(k):
        n, bk, free = ring.take()
        t = PE(lambda e: e.transpose(bk[:, 0:128], Xs[:, k % NB, :], ident), g_ld[k], *free)
        st["x", k] = t
        t = V(lambda e: e.tensor_copy(XsT[:, k % NB, :], bk[:, 0:128]), t, *([st["h", k - NB]] if k >= NB else []))
        ring.give(n, t)
        n, bk2, free = ring.take()

        def mm(e):
            at[k] = e.value_load(tei[0:1, k:k + 1], min_val=0, max_val=(E - 1) * NF)
            return e.matmul(bk2[:, :], XsT[:, k % NB, :], W1[:, bass.ds(at[k], NF)], start=True, stop=True)

        t = st["h", k] = PE(mm, t, t_te, g_1, *free)
        t = S(lambda e: e.activation(H[:, k % NB, :], bk2[:, :], ACT.Gelu), t, *([st["ht", k - NB]] if k >= NB else []))
        ring.give(n, t)
        st["g", k] = t

    def second(k):
        n, bk, free = ring.take()
        for f in range(4):
            t = PE(lambda e, f=f: e.transpose(bk[:, 128 * f:128 * f + 128], H[:, k % NB, 128 * f:128 * f + 128], ident),
                   *((st["g", k],) + free if f == 0 else ()))
        st["ht", k] = t
        t = V(lambda e: e.tensor_copy(HT[:, k % NB, :, :], bk[:, :].rearrange("p (f t) -> p f t", f=4)), t,
              *([st["y", k - NB]] if k >= NB else []))
        ring.give(n, t)
        st["hts", k] = t

    def third(k):
        n, bk, free = ring.take()
        for f in range(4):
            t = PE(lambda e, f=f: e.matmul(bk[:, 0:128], HT[:, k % NB, f, :], W2[:, bass.ds(at[k] + 128 * f, 128)],
                                           start=(f == 0), stop=(f == 3)), *((st["hts", k], g_2) + free if f == 0 else ()))
        st["y", k] = t
        t = S(lambda e: e.activation(Ys[:, k % NB, :], bk[:, 0:128], ACT.Copy), t, *([g_st[k - NB]] if k >= NB else []))
        ring.give(n, t)
        SP.dma(g_st[k], lambda e: e.dma_start(ys_d[128 * k:128 * k + 128, :], Ys[:, k % NB, :]), t)

    for k in range(TS + 2):
        if k < TS:
            load(k)
            first(k)
        if 1 <= k <= TS:
            second(k - 1)
        if k >= 2:
            third(k - 2)
    for i in range(NT):
        G.dma(g_g, lambda e, i=i: e.indirect_dma_start(Yg[:, i, :], None, ys_d, bass.IndirectOffsetOnAxis(posu[:, i:i + 1], 0)),
              *g_st)
    for i in range(NT):
        t = V(lambda e, i=i: e.scalar_tensor_tensor(out=Y[:, i, :], in0=Yg[:, i, :], scalar=top[:, i, 0:1], in1=X0[:, i, :],
                                                    op0=ALU.mult, op1=ALU.add), g_g)
        t = stats(i, t)
    return t


def scan(nc, ctx, sem, group, queues, bank, a, c, ident, X0, XT, Y, transposed, stats, normalise, mv):
    PE, S, V, G, SP = queues
    ring = Banks(bank[0:8])

    def sb(name, shape, dt=F32):
        return ctx.enter_context(nc.sbuf_tensor(name, shape, dt))

    Wg = sb("Wg", [128, 128])
    WgT = sb("WgT", [128, 128])
    bg = sb("bg", [128, 1])
    gam = sb("gam", [128, 128])
    bet = sb("bet", [128, 128])
    SC = sb("SC", [128, 304])
    Af = SC[:, 0:256].rearrange("p (g m) -> p g m", g=16)
    Bc, Cc, Dr = SC[:, 256:272], SC[:, 272:288], SC[:, 288:304]
    PA = [sb(f"PA{k}", [128, 16, 128]) for k in range(4)]
    PB = [sb(f"PB{k}", [128, 16, 128]) for k in range(2)]
    Uc = sb("Uc", [128, 16, 16])
    Vc = sb("Vc", [128, 16, 16])
    Vr = sb("Vr", [128, 16, 16])
    Hk = sb("Hk", [128, 31, 16])
    Tc = sb("Tc", [128, 16, 16])
    BX = sb("BX", [128, 16, 128])
    Win = sb("Win", [128, 16, 128])
    Wou = sb("Wou", [128, 16, 128])
    Wto = sb("Wto", [128, 16, 128])
    GA = sb("GA", [128, 2048])
    U = sb("U", [128, 16, 128])
    XP = sb("XP", [128, NT, 128])
    xg_d = nc.dram_tensor("xg_d", [128, 16, 128], F32, kind="Internal").ap()
    y_d = nc.dram_tensor("y_d", [128, 16, 128], F32, kind="Internal").ap()

    g_w, g_a, g_xg, g_u, g_t, g_yd, g_y = [group(f"g_n{k}") for k in ("w", "a", "xg", "u", "t", "yd", "y")]
    SP.dma(g_w, lambda e: e.dma_start(Wg[:, :], a["Wg"]))
    SP.dma(g_w, lambda e: e.dma_start(bg[:, :], a["bg"].rearrange("(p o) -> p o", o=1)))
    SP.dma(g_w, lambda e: e.dma_start(gam[:, :], a["gamma"].partition_broadcast(128)))
    SP.dma(g_w, lambda e: e.dma_start(bet[:, :], a["beta"].partition_broadcast(128)))
    SP.dma(g_a, lambda e: e.dma_start(SC[:, :], a["packed"]))

    for p in range(4):
        t_xt = transposed(ring, X0, p)
    n, bk, free = ring.take()
    t = PE(lambda e, bk=bk: e.transpose(bk[:, 0:128], Wg[:, :], ident), g_w, *free)
    t_wg = V(lambda e, bk=bk: e.tensor_copy(WgT[:, :], bk[:, 0:128]), t)
    ring.give(n, t_wg)
    XG = GA
    for p in range(4):
        n, bk, free = ring.take()
        xs = slice(512 * p, 512 * p + 512)
        t = PE(lambda e, bk=bk, xs=xs: e.matmul(bk[:, :], WgT[:, :], XT[:, xs], start=True, stop=True), t_xt, t_wg, *free)
        t = S(lambda e, bk=bk, xs=xs: e.activation(Y[:, 4 * (xs.start // 512):4 * (xs.start // 512) + 4, :].rearrange("p i d -> p (i d)"),
                                                   bk[:, :], ACT.Sigmoid, bias=bg[:, :]), t)
        ring.give(n, t)
    gate = Y[:, :, :].rearrange("p i d -> p (i d)")
    t = V(lambda e: e.tensor_tensor(XG[:, :].rearrange("p (j q) -> p q j", j=16), XT[:, :].rearrange("p (q j) -> p q j", j=16),
                                    gate.rearrange("p (q j) -> p q j", j=16), ALU.mult), t)
    t_xg = t
    SP.dma(g_xg, lambda e: e.dma_start(xg_d, XG[:, :].rearrange("p (j q) -> p j q", j=16)), t)
    xv = xg_d.rearrange("(g d) j q -> j d g q", d=8)
    for j in range(16):
        SP.dma(g_u, lambda e, j=j: e.dma_start(U[8 * j:8 * j + 8, :, :], xv[j]), g_xg)

    for p in range(4):
        n, bk, free = ring.take()
        for i in range(4 * p, 4 * p + 4):
            t = PE(lambda e, i=i, p=p, bk=bk: e.transpose(bk[:, 128 * (i - 4 * p):128 * (i - 4 * p) + 128], XT[:, i:2048:16], ident),
                   *((t_xt,) + free))
        t_xp = S(lambda e, p=p, bk=bk: e.activation(XP[:, 4 * p:4 * p + 4, :], bk[:, :].rearrange("p (i d) -> p i d", i=4), ACT.Copy), t)
        ring.give(n, t_xp)
    t_xp = G(lambda e: e.tensor_tensor(XP[:, :, :], XP[:, :, :], bet[:, :].unsqueeze(1).to_broadcast([128, NT, 128]), ALU.add), t_xp, g_w)

    def spread(eng, dst, src, *waits):
        return eng(lambda e: e.tensor_tensor(dst[:, :, :].rearrange("p g (i d) -> p g i d", d=8),
                                             src[:, :, :].unsqueeze(3).to_broadcast([128, 16, 16, 8]),
                                             c("d8").unsqueeze(1).unsqueeze(1).to_broadcast([128, 16, 16, 8]), ALU.mult), *waits)

    def turn_all(dst, src, *waits):
        for k in range(4):
            n, bk, free = ring.take()
            for g in range(4 * k, 4 * k + 4):
                t = PE(lambda e, g=g, k=k, bk=bk: e.transpose(bk[:, 128 * (g - 4 * k):128 * (g - 4 * k) + 128], src[:, g, :], ident),
                       *(waits + free))
            E = S if k % 2 else V
            out, got = dst[:, 4 * k:4 * k + 4, :], bk[:, :].rearrange("p (g m) -> p g m", g=4)
            if E is S:
                ts = t = S(lambda e, out=out, got=got: e.activation(out, got, ACT.Copy), t)
            else:
                tv = t = V(lambda e, out=out, got=got: e.tensor_copy(out, got), t)
            ring.give(n, t)
        return ts, tv

    def product(dst, lhs, rhs, *waits):
        for k in range(4):
            n, bk, free = ring.take()
            for g in range(4 * k, 4 * k + 4):
                t = PE(lambda e, g=g, k=k, bk=bk: e.matmul(bk[:, 128 * (g - 4 * k):128 * (g - 4 * k) + 128], lhs[:, g, :], rhs[:, g, :],
                                                           start=True, stop=True), *(waits + free))
            out, got = dst[:, 4 * k:4 * k + 4, :], bk[:, :].rearrange("p (g m) -> p g m", g=4)
            if k % 2:
                ts = t = S(lambda e, out=out, got=got: e.activation(out, got, ACT.Copy), t)
            else:
                tv = t = V(lambda e, out=out, got=got: e.tensor_copy(out, got), t)
            ring.give(n, t)
        return ts, tv

    def columns(dst, lhs, src, k, m, *waits):
        n, bk, free = ring.take()
        for g in range(16):
            t = PE(lambda e, g=g: e.matmul(bk[:, m * g:m * g + m], lhs[:, g, :], src(g, m), start=True, stop=True), *(waits + free))
        t = V(lambda e: e.tensor_copy(dst[:, :, k:k + m], bk[:, 0:16 * m].rearrange("p (g m) -> p g m", g=16)), t)
        ring.give(n, t)
        return t

    t = spread(V, PA[0], Af, g_a)
    pw = turn_all(PB[0], PA[0], t)
    pw = pw + (t,)
    t_u = columns(Uc, PB[0], lambda g, m: Cc[:, g:g + 1], 0, 1, *pw)
    t_v = G(lambda e: e.tensor_copy(Vc[:, :, 0:1].rearrange("p g o -> p (g o)"), Bc), g_a)
    cur_a, cur_b = PA[0], PB[0]
    nexta, nextb = [PA[1], PA[0], PA[1], PA[0]], [PB[1], PB[0], PB[1], PB[0]]
    for p in range(4):
        m = 2 ** p
        t_u = columns(Uc, cur_b, lambda g, m: Uc[:, g, 0:m], m, m, t_u, *pw)
        t_v = columns(Vc, cur_a, lambda g, m: Vc[:, g, 0:m], m, m, t_v, *pw)
        pa = product(nexta[p], cur_b, cur_a, *pw)
        pw = pa + product(nextb[p], cur_a, cur_b, *pw)
        cur_a, cur_b = nexta[p], nextb[p]
    power = [cur_a]
    for p in range(3):
        dst = [PA[1], PA[2], PA[3]][p]
        pa = product(dst, cur_b, cur_a, *pw)
        if p < 2:
            pw = pw + pa + product(PB[1] if cur_b is PB[0] else PB[0], cur_a, cur_b, *pw)
            cur_b = PB[1] if cur_b is PB[0] else PB[0]
        else:
            pw = pw + pa
        cur_a = dst
        power.append(dst)

    for k in range(16):
        t = G(lambda e, k=k: e.tensor_copy(Vr[:, :, 15 - k:16 - k], Vc[:, :, k:k + 1]), t_v)
    t = spread(G, BX, Vr, t)
    t_win = turn_all(Win, BX, t)
    t_wou = spread(G, Wou, Uc, t_u)
    t = V(lambda e: e.tensor_tensor(Vr[:, :, :], Vc[:, :, :], Cc.unsqueeze(2).to_broadcast([128, 16, 16]), ALU.mult), t)
    n, bk, free = ring.take()
    t = PE(lambda e, bk=bk: e.matmul(bk[:, 0:256], c("rep"), Vr[:, :, :].rearrange("p g k -> p (g k)"), start=True, stop=True), t, *free)
    t = V(lambda e, bk=bk: e.tensor_copy(Hk[:, 15:31, :], bk[:, 0:256].rearrange("p (g k) -> p k g", g=16)), t)
    ring.give(n, t)
    V(lambda e: e.tensor_scalar(Dr, Dr, 1.0, None, ALU.add), g_a)
    t = V(lambda e: e.tensor_tensor(Hk[:, 15, :], Hk[:, 15, :], Dr, ALU.add))
    t2 = G(lambda e: e.memset(Hk[:, 0:15, :], 0.0))
    for j in range(16):
        r = slice(8 * j, 8 * j + 8)
        SP.dma(g_t, lambda e, j=j, r=r: e.dma_start(Tc[r, :, :], Hk[r, 15 - j:31 - j, :]), t, t2)
    t_wto = spread(G, Wto, Tc[:, :, :].rearrange("p i g -> p g i"), g_t)

    ES = BX
    got = {}
    taken = []
    for k in range(4):
        n, bk, free = ring.take()
        taken.append((n, bk))
        for g in range(4 * k, 4 * k + 4):
            t = PE(lambda e, g=g, k=k, bk=bk: e.matmul(bk[:, 128 * (g - 4 * k):128 * (g - 4 * k) + 128], Win[:, g, :], U[:, g, :],
                                                       start=(g == 4 * k), stop=False, skip_group_check=True),
                   *(t_win + (g_u,) + free))
        got[k] = t

    def state_out(k):
        n, bk = taken[k]
        dst, src = ES[:, 4 * k:4 * k + 4, :], bk[:, :].rearrange("p (g q) -> p g q", g=4)
        if k % 2:
            return S(lambda e: e.activation(dst, src, ACT.Copy), got[k], *t_win)
        return V(lambda e: e.tensor_copy(dst, src), got[k], *t_win)

    for p in range(4):
        s = 2 ** p
        outs = [state_out(k) for k in range(4)]
        for k in range(4):
            n, bk = taken[k]
            for g in range(4 * k, 4 * k + 4):
                w = slice(128 * (g - 4 * k), 128 * (g - 4 * k) + 128)
                t = PE(lambda e, g=g, w=w, p=p, s=s, bk=bk: e.matmul(
                    bk[:, w].rearrange("p (b q) -> p b q", b=8)[:, :, s:16], power[p][:, g, :],
                    ES[:, g, :].rearrange("p (b q) -> p b q", b=8)[:, :, 0:16 - s], start=False, stop=(p == 3),
                    skip_group_check=True), outs[k], *pw)
            got[k] = t
    outs = [state_out(k) for k in range(4)]
    for k in range(4):
        ring.give(taken[k][0], outs[k])
    YC = PB[0]
    for k in range(4):
        n, bk, free = ring.take()
        for g in range(4 * k, 4 * k + 4):
            w = slice(128 * (g - 4 * k), 128 * (g - 4 * k) + 128)
            PE(lambda e, g=g, w=w, bk=bk: e.matmul(bk[:, w], Wto[:, g, :], U[:, g, :], start=True, stop=False), t_wto, g_u, *free)
            t = PE(lambda e, g=g, w=w, bk=bk: e.matmul(
                bk[:, w].rearrange("p (b q) -> p b q", b=8)[:, :, 1:16], Wou[:, g, :],
                ES[:, g, :].rearrange("p (b q) -> p b q", b=8)[:, :, 0:15], start=False, stop=True), t_wou, outs[k])
        dst, src = YC[:, 4 * k:4 * k + 4, :], bk[:, :].rearrange("p (g q) -> p g q", g=4)
        if k % 2:
            t_s = t = S(lambda e, dst=dst, src=src: e.activation(dst, src, ACT.Copy), t)
        else:
            t_v = t = V(lambda e, dst=dst, src=src: e.tensor_copy(dst, src), t)
        ring.give(n, t)
    yv = y_d.rearrange("(g d) i q -> i d g q", d=8)
    for i in range(16):
        SP.dma(g_yd, lambda e, i=i: e.dma_start(yv[i], YC[8 * i:8 * i + 8, :, :]), t_s, t_v)
    YT = GA
    SP.dma(g_y, lambda e: e.dma_start(YT[:, :].rearrange("p (i q) -> p i q", i=16), y_d), g_yd)
    for p in range(4):
        n, bk, free = ring.take()
        for i in range(4 * p, 4 * p + 4):
            t = PE(lambda e, i=i, p=p, bk=bk: e.transpose(bk[:, 128 * (i - 4 * p):128 * (i - 4 * p) + 128], YT[:, 128 * i:128 * i + 128], ident),
                   g_y, *free)
        t = S(lambda e, p=p, bk=bk: e.activation(Y[:, 4 * p:4 * p + 4, :], bk[:, :].rearrange("p (i d) -> p i d", i=4), ACT.Copy), t)
        ring.give(n, t)
        for i in range(4 * p, 4 * p + 4):
            ts = stats(i, t)
    return scaled(V, G, X0, Y, XP, gam, normalise, stats, ts, t_xp)


def scaled(V, G, X0, Y, XP, gam, normalise, stats, ts, t_xp):
    normalise(Y, 0, NT, ts)
    for p in range(4):
        V(lambda e, p=p: e.tensor_tensor(Y[:, 4 * p:4 * p + 4, :], Y[:, 4 * p:4 * p + 4, :],
                                         gam[:, :].unsqueeze(1).to_broadcast([128, 4, 128]), ALU.mult))
        t = V(lambda e, p=p: e.tensor_tensor(Y[:, 4 * p:4 * p + 4, :], Y[:, 4 * p:4 * p + 4, :], XP[:, 4 * p:4 * p + 4, :], ALU.add), t_xp)
        for i in range(4 * p, 4 * p + 4):
            t = stats(i, t)
    return t


def mixture(nc, ctx, sem, group, queues, bank, a, c, ident, X0, XT, Y, transposed, stats, normalise):
    PE, S, V, G, SP = queues
    E = 8

    def sb(name, shape, dt=F32):
        return ctx.enter_context(nc.sbuf_tensor(name, shape, dt))

    ring = Banks(bank[0:7])
    logits = bank[7]
    Wen = sb("Wen", [128, 256])
    ben = sb("ben", [128, 2])
    Wsc = sb("Wsc", [128, 2, 64])
    bsc = sb("bsc", [64, 1])
    Wr1 = sb("Wr1", [64, 64])
    br1 = sb("br1", [64, 1])
    Wr2 = sb("Wr2", [64, E])
    br2 = sb("br2", [1, E])
    We1 = sb("We1", [64, E, 128])
    be1 = sb("be1", [128, E])
    We2 = sb("We2", [128, E, 64])
    be2 = sb("be2", [1, 512])
    Wcs = sb("Wcs", [64, 256])
    bcs = sb("bcs", [128, 2])
    Wde = sb("Wde", [128, 2, 128])
    bde = sb("bde", [1, 128])
    gam = sb("lng", [128, 128])
    bet = sb("lnb", [128, 128])
    ones = sb("ones1", [1, 128])
    EN = sb("EN", [128, 2, 512])
    CT = sb("CT", [64, 2048])
    T1 = sb("T1", [64, 2048])
    LG = sb("LG", [128, NT, E])
    lm = sb("lm", [128, NT])
    ls = sb("ls", [128, NT])
    top = sb("top2", [128, NT, 8])
    topi = sb("topi2", [128, NT, 8], U32)
    tf = sb("tf2", [128, NT, 2])
    w2 = sb("w2", [128, NT, 2])
    gt = sb("gt", [128, NT, E])
    gu = sb("gu", [128, NT, E])
    HE = sb("HE", [128, E, 512])
    PR = sb("PR", [128, 2, 512])
    OF = sb("OF", [128, NT, 64])
    OT = sb("OT", [64, 2, 512])
    SM = sb("SM", [128, 2, 2, 512])
    XB = sb("XB", [128, NT, 128])
    g_w = [group(f"g_m{k}") for k in range(3)]

    def load(k, dst, src):
        SP.dma(g_w[k], lambda e: e.dma_start(dst, src))

    def col(s):
        return s.rearrange("(p o) -> p o", o=1)

    def row(s):
        return s.rearrange("(o n) -> o n", o=1)

    load(0, Wen[:, :], a["enc_W"])
    load(0, ben[:, :], a["enc_b"])
    load(0, Wsc[:, :, :], a["s2c_W"].rearrange("(k p) m -> p k m", p=128))
    load(0, bsc[:, :], col(a["s2c_b"]))
    load(0, Wr1[:, :], a["rW1"])
    load(0, br1[:, :], col(a["rb1"]))
    load(0, Wr2[:, :], a["rW2"])
    load(0, br2[:, :], row(a["rb2"]))
    load(1, We1[:, :, :], a["We1"].rearrange("e m h -> m e h"))
    load(1, be1[:, :], a["be1"])
    load(1, We2[:, :, :], a["We2"].rearrange("e h m -> h e m"))
    load(1, be2[:, :], row(a["be2"].rearrange("e m -> (e m)")))
    load(2, Wcs[:, :], a["c2s_W"])
    load(2, bcs[:, :], a["c2s_b"])
    load(2, Wde[:, :, :], a["dec_W"].rearrange("(k p) d -> p k d", p=128))
    load(2, bde[:, :], row(a["dec_b"]))
    load(2, gam[:, :], a["ln_g"].partition_broadcast(128))
    load(2, bet[:, :], a["ln_b"].partition_broadcast(128))
    t_one = G(lambda e: e.memset(ones[:, :], 1.0))
    t_xb = G(lambda e: e.tensor_tensor(XB[:, :, :], X0[:, :, :], bet[:, :].unsqueeze(1).to_broadcast([128, NT, 128]), ALU.add), g_w[2])

    for p in range(4):
        t_x = transposed(ring, X0, p)
        xs = slice(512 * p, 512 * p + 512)
        for k in range(2):
            n, bk, free = ring.take()
            t = PE(lambda e, k=k, xs=xs, bk=bk: e.matmul(bk[:, :], Wen[:, 128 * k:128 * k + 128], XT[:, xs], start=True, stop=True),
                   t_x, g_w[0], *free)
            t = S(lambda e, k=k, bk=bk: e.activation(EN[:, k, :], bk[:, :], ACT.Sigmoid, bias=ben[:, k:k + 1]), t)
            ring.give(n, t)
        n, bk, free = ring.take()
        for k in range(2):
            t = PE(lambda e, k=k, bk=bk, t=t: e.matmul(bk[0:64, :], Wsc[:, k, :], EN[:, k, :], start=(k == 0), stop=(k == 1)), t, *free)
        t_ct = V(lambda e, xs=xs, bk=bk: e.tensor_scalar(CT[:, xs], bk[0:64, :], bsc[:, :], None, ALU.add), t)
        ring.give(n, t_ct)
        n, bk, free = ring.take()
        t = PE(lambda e, xs=xs, bk=bk: e.matmul(bk[0:64, :], Wr1[:, :], CT[:, xs], start=True, stop=True), t_ct, *free)
        t = S(lambda e, xs=xs, bk=bk: e.activation(T1[:, xs], bk[0:64, :], ACT.Tanh, bias=br1[:, :]), t)
        ring.give(n, t)
        for i in range(4 * p, 4 * p + 4):
            PE(lambda e, i=i: e.matmul(logits[:, E * i:E * i + E], ones[:, :], br2[:, :], start=True, stop=False), t_one, t)
            t_lg = PE(lambda e, i=i: e.matmul(logits[:, E * i:E * i + E], T1[:, 128 * i:128 * i + 128], Wr2[:, :], start=False, stop=True))

    lv = logits[:, 0:128].rearrange("p (i e) -> p i e", e=E)

    def wide(s, k=E):
        return s.unsqueeze(2).to_broadcast([128, NT, k])

    V(lambda e: e.tensor_reduce(lm[:, :], lv, AX, ALU.max), t_lg)
    t = V(lambda e: e.tensor_tensor(LG[:, :, :], lv, wide(lm[:, :]), ALU.subtract))
    t = S(lambda e: e.activation(LG[:, :, :], LG[:, :, :], ACT.Exp), t)
    V(lambda e: e.tensor_reduce(ls[:, :], LG[:, :, :], AX, ALU.add), t)
    V(lambda e: e.reciprocal(ls[:, :], ls[:, :]))
    V(lambda e: e.tensor_tensor(LG[:, :, :], LG[:, :, :], wide(ls[:, :]), ALU.mult))
    for i in range(NT):
        V(lambda e, i=i: e.max(top[:, i, :], LG[:, i, :]))
        V(lambda e, i=i: e.max_index(topi[:, i, :], top[:, i, :], LG[:, i, :]))
    V(lambda e: e.tensor_copy(tf[:, :, :], topi[:, :, 0:2]))
    V(lambda e: e.tensor_reduce(ls[:, :], top[:, :, 0:2], AX, ALU.add))
    V(lambda e: e.reciprocal(ls[:, :], ls[:, :]))
    V(lambda e: e.tensor_tensor(w2[:, :, :], top[:, :, 0:2], wide(ls[:, :], 2), ALU.mult))
    iota = c("iota8").unsqueeze(1).to_broadcast([128, NT, E])
    for k in range(2):
        dst = gu if k else gt
        V(lambda e, k=k, dst=dst: e.tensor_tensor(dst[:, :, :], iota, wide(tf[:, :, k]), ALU.is_equal))
        V(lambda e, k=k, dst=dst: e.tensor_tensor(dst[:, :, :], dst[:, :, :], wide(w2[:, :, k]), ALU.mult))
    t_gt = V(lambda e: e.tensor_tensor(gt[:, :, :], gt[:, :, :], gu[:, :, :], ALU.add))

    t_he2 = ()
    for p in range(4):
        xs = slice(512 * p, 512 * p + 512)
        hs = []
        for x in range(E):
            n, bk, free = ring.take()
            t = PE(lambda e, x=x, xs=xs, bk=bk: e.matmul(bk[:, :], We1[:, x, :], CT[:, xs], start=True, stop=True), t_ct, g_w[1], *free)
            if x % 2:
                t = S(lambda e, x=x, bk=bk: e.activation(HE[:, x, :], bk[:, :], ACT.Relu, bias=be1[:, x:x + 1]), t, *t_he2)
            else:
                t = V(lambda e, x=x, bk=bk: e.tensor_scalar(HE[:, x, :], bk[:, :], be1[:, x:x + 1], 0.0, ALU.add, ALU.max), t, *t_he2)
            ring.give(n, t)
            hs.append(t)
        for i in range(4 * p, 4 * p + 4):
            n, bk, free = ring.take()
            PE(lambda e, bk=bk: e.matmul(bk[:, :], ones[:, :], be2[:, :], start=True, stop=False), t_one, g_w[1], *free)
            for x in range(E):
                o = 128 * (i - 4 * p)
                t = PE(lambda e, x=x, o=o, bk=bk: e.matmul(bk[:, 64 * x:64 * x + 64], HE[:, x, o:o + 128], We2[:, x, :], start=False,
                                                           stop=(x == E - 1)), hs[x])
            t_he2 = (t,)
            t = V(lambda e, i=i, bk=bk: e.tensor_tensor(PR[:, i % 2, :].rearrange("p (e m) -> p e m", e=E),
                                                        bk[:, :].rearrange("p (e m) -> p e m", e=E),
                                                        gt[:, i, :].unsqueeze(2).to_broadcast([128, E, 64]), ALU.mult), t, t_gt)
            ring.give(n, t)
            t_of = V(lambda e, i=i: e.tensor_reduce(OF[:, i, :], PR[:, i % 2, :].rearrange("p (e m) -> p m e", e=E), AX, ALU.add))
        n, bk, free = ring.take()
        for i in range(4):
            t = PE(lambda e, i=i, p=p, bk=bk: e.transpose(bk[0:64, 128 * i:128 * i + 128], OF[:, 4 * p + i, :], ident), t_of, *free)
        t = S(lambda e, p=p, bk=bk: e.activation(OT[:, p % 2, :], bk[0:64, :], ACT.Copy), t)
        ring.give(n, t)
        t_ot = t
        for k in range(2):
            n, bk, free = ring.take()
            t = PE(lambda e, k=k, p=p, bk=bk: e.matmul(bk[:, :], Wcs[:, 128 * k:128 * k + 128], OT[:, p % 2, :], start=True, stop=True),
                   t_ot, g_w[2], *free)
            t = S(lambda e, k=k, p=p, bk=bk: e.activation(SM[:, p % 2, k, :], bk[:, :], ACT.Sigmoid, bias=bcs[:, k:k + 1]), t)
            ring.give(n, t)
        n, bk, free = ring.take()
        for i in range(4):
            o = slice(128 * i, 128 * i + 128)
            PE(lambda e, o=o, bk=bk: e.matmul(bk[:, o], ones[:, :], bde[:, :], start=True, stop=False), t, *free)
            for k in range(2):
                t2 = PE(lambda e, k=k, o=o, p=p, bk=bk: e.matmul(bk[:, o], SM[:, p % 2, k, o], Wde[:, k, :], start=False, stop=(k == 1)))
        t = S(lambda e, p=p, bk=bk: e.activation(Y[:, 4 * p:4 * p + 4, :], bk[:, :].rearrange("p (i d) -> p i d", i=4), ACT.Sigmoid), t2)
        ring.give(n, t)
        for i in range(4 * p, 4 * p + 4):
            ts = stats(i, t)
    return scaled(V, G, X0, Y, XB, gam, normalise, stats, ts, t_xb)


def program(nc, x, a, f0, a1, f1, const, out):
    with ExitStack() as ctx:
        def sb(name, shape, dt=F32):
            return ctx.enter_context(nc.sbuf_tensor(name, shape, dt))

        def sem(name):
            return ctx.enter_context(nc.semaphore(name))

        def group(name):
            return Group(sem(name))

        PE, S, V, G, SP = [Queue(sem(n), n in ("s_act", "s_dve", "s_pool"))
                           for n in ("s_pe", "s_act", "s_dve", "s_pool", "s_sp")]
        bank = [ctx.enter_context(nc.psum_tensor(f"bank{i}", [128, 512], F32)) for i in range(8)]

        C = sb("C", [128, CONST.shape[1]])

        def c(name, rows=slice(0, 128)):
            return C[rows, CAT[name][0]:CAT[name][1]]

        ident = c("ident")
        X0 = sb("X0", [128, NT, D])
        Y = sb("Y", [128, NT, D])
        XT = sb("XT", [128, NT * 128])
        st6 = sb("st6", [128, NT, 6])
        mv = sb("mv", [128, NT, 2])
        rstd = sb("rstd", [128, NT])

        g_c = group("g_c")
        g_x = [group(f"g_x{i}") for i in range(4)]
        SP.dma(g_c, lambda e: e.dma_start(C[:, :], const))
        xv = x.rearrange("b (h p) d -> p (b h) d", p=128)
        for p in range(4):
            SP.dma(g_x[p], lambda e, p=p: e.dma_start(X0[:, 4 * p:4 * p + 4, :], xv[:, 4 * p:4 * p + 4, :]))

        def transposed(ring, src, p, *waits):
            n, bk, free = ring.take()
            for i in range(4):
                t = PE(lambda e, i=i: e.transpose(bk[:, i * 128:i * 128 + 128], src[:, 4 * p + i, :], ident),
                       *((free + waits) if i == 0 else ()))
            t = S(lambda e: e.activation(XT[:, p * 512:p * 512 + 512], bk[:, :], ACT.Copy), t)
            ring.give(n, t)
            return t

        def stats(i, *waits):
            t = V(lambda e: e.bn_stats(st6[:, i, :], Y[:, i, :]), *waits)
            return V(lambda e: e.bn_aggr(mv[:, i, :], st6[:, i, :]), t)

        def normalise(dst, lo, hi, *waits):
            t = S(lambda e: e.activation(rstd[:, lo:hi], mv[:, lo:hi, 1], ACT.Sqrt, bias=c("eps")), *waits)
            t = r = V(lambda e: e.reciprocal(rstd[:, lo:hi], rstd[:, lo:hi]), t)
            for i in range(lo, hi):
                t = V(lambda e, i=i: e.tensor_scalar(dst[:, i, :], Y[:, i, :], mv[:, i, 0:1], rstd[:, i:i + 1],
                                                     ALU.subtract, ALU.mult), r)
            return t

        def fence():
            ends = [q.items[-1][2] for q in (PE, S, V, G)]
            for q in (PE, S, V, G, SP):
                q.hold(*ends)

        with ExitStack() as part:
            x1 = attention(nc, part, sem, group, (PE, S, V, G, SP), bank, a, c, ident, X0, XT, Y, g_c, g_x,
                           transposed, stats)
        x1 = normalise(X0, 0, NT, x1)
        fence()
        with ExitStack() as part:
            x2 = experts(nc, part, sem, group, (PE, S, V, G, SP), bank, f0, c, ident, X0, XT, Y, transposed, stats)
        x2 = normalise(X0, 0, NT, x2)
        fence()
        with ExitStack() as part:
            x3 = scan(nc, part, sem, group, (PE, S, V, G, SP), bank, a1, c, ident, X0, XT, Y, transposed, stats, normalise, mv)
        x3 = normalise(X0, 0, NT, x3)
        fence()
        with ExitStack() as part:
            x4 = mixture(nc, part, sem, group, (PE, S, V, G, SP), bank, f1, c, ident, X0, XT, Y, transposed, stats, normalise)
        x4 = normalise(X0, 0, NT, x4)

        g_out = group("g_out")
        ov = out.rearrange("b (q i) d -> (b q) i d", i=16)
        SP.dma(g_out, lambda e: e.dma_start(ov, X0[:, :, :]), x4)
        SP.hold(g_out)

        queues = (PE, S, V, G, SP)
        for q in queues:
            q.count()
        block = ctx.enter_context(nc.Block())

        @block.tensor
        def _(eng):
            PE.write(eng)

        @block.scalar
        def _(eng):
            S.write(eng)

        @block.vector
        def _(eng):
            V.write(eng)

        @block.gpsimd
        def _(eng):
            G.write(eng)

        @block.sync
        def _(eng):
            SP.write(eng)


NAMES = ['L0_attn_x', 'L0_attn_W_dkv', 'L0_attn_W_uk', 'L0_attn_W_uv', 'L0_attn_W_dq', 'L0_attn_W_uq', 'L0_attn_W_qr', 'L0_attn_W_kr', 'L0_attn_W_out', 'L0_attn_idx_wq', 'L0_attn_idx_wk', 'L0_attn_idx_w', 'L0_attn_raw_delta', 'L0_ffn_Wr', 'L0_ffn_br', 'L0_ffn_W1', 'L0_ffn_W2', 'L1_attn_A', 'L1_attn_Bp', 'L1_attn_Cp', 'L1_attn_Dp', 'L1_attn_Wg', 'L1_attn_bg', 'L1_attn_gamma', 'L1_attn_beta', 'L1_ffn_enc_W', 'L1_ffn_enc_b', 'L1_ffn_s2c_W', 'L1_ffn_s2c_b', 'L1_ffn_rW1', 'L1_ffn_rb1', 'L1_ffn_rW2', 'L1_ffn_rb2', 'L1_ffn_We1', 'L1_ffn_be1', 'L1_ffn_We2', 'L1_ffn_be2', 'L1_ffn_c2s_W', 'L1_ffn_c2s_b', 'L1_ffn_dec_W', 'L1_ffn_dec_b', 'L1_ffn_ln_g', 'L1_ffn_ln_b']


def kernel(**inputs):
    import concourse.bacc as bacc
    from concourse.bass_utils import run_bass_kernel_spmd

    nc = bacc.Bacc("TRN2", target_bir_lowering=False, num_devices=1)
    arrays, aps = {}, {}
    for name in NAMES:
        v = np.ascontiguousarray(inputs[name])
        arrays[name] = v
        aps[name] = nc.dram_tensor(name, v.shape, mybir.dt.from_np(v.dtype), kind="ExternalInput").ap()
    arrays["shape_constants"] = CONST
    const = nc.dram_tensor("shape_constants", CONST.shape, F32, kind="ExternalInput").ap()
    out = nc.dram_tensor("result", (B, L, D), F32, kind="ExternalOutput").ap()

    def part(prefix):
        return {n[len(prefix):]: aps[n] for n in NAMES if n.startswith(prefix)}

    def lay(name, v):
        arrays[name] = v = np.ascontiguousarray(v)
        return nc.dram_tensor(name, v.shape, F32, kind="ExternalInput").ap()

    def by_state(v):
        v = v.reshape((16, 8) + v.shape[1:])
        return v.transpose((2, 1, 0) + tuple(range(3, v.ndim))).reshape(128, -1)

    a1, f1 = part("L1_attn_"), part("L1_ffn_")
    skip = np.broadcast_to(np.asarray(inputs["L1_attn_Dp"])[:, None], (128, 16))
    a1["packed"] = lay("scan_packed", np.concatenate(
        [by_state(np.asarray(inputs[f"L1_attn_{k}"])) for k in ("A", "Bp", "Cp")] + [by_state(skip)], 1))
    for k in ("enc_b", "c2s_b"):
        f1[k] = lay(f"{k}_columns", np.asarray(inputs[f"L1_ffn_{k}"]).reshape(2, 128).T)
    f1["be1"] = lay("be1_columns", np.asarray(inputs["L1_ffn_be1"]).T)
    program(nc, aps["L0_attn_x"], part("L0_attn_"), part("L0_ffn_"), a1, f1, const, out)
    r = run_bass_kernel_spmd(nc, [arrays], core_ids=[0])
    return r.results[0]["result"]
```

```python
from contextlib import ExitStack

import numpy as np
import concourse.bass as bass
from concourse import mybir

F32 = mybir.dt.float32
BF16 = mybir.dt.bfloat16
U32 = mybir.dt.uint32
I32 = mybir.dt.int32
ALU = mybir.AluOpType
ACT = mybir.ActivationFunctionType
AX = mybir.AxisListType.X

B, L, D = 8, 256, 128
NT = B * L // 128
NH = 8
TILES = NT + 7
SCALE = 96.0 ** -0.5
BIG = 1.0e30
LOW = -3.0e38


class Tok:

    def __init__(self, queue):
        self.queue, self.used, self.value = queue, False, 0

    def target(self):
        return self.queue.sem, self.value


class Group:

    def __init__(self, sem):
        self.sem, self.count, self.used = sem, 0, False

    def target(self):
        return self.sem, 16 * self.count


class Queue:

    def __init__(self, sem, chained):
        self.sem, self.items, self.chained, self.last = sem, [], chained, None

    def __call__(self, fn, *waits):
        tok = Tok(self)
        if self.chained:
            waits += (self.last,) if self.last else ()
            self.last = tok
        for w in waits:
            w.used = True
        self.items.append((waits, fn, tok))
        return tok

    def free(self, fn, *waits):
        tok = Tok(self)
        if self.chained:
            self.last = tok
        for w in waits:
            w.used = True
        self.items.append((waits, fn, tok))
        return tok

    def dma(self, group, fn, *waits):
        for w in waits:
            w.used = True
        group.count += 1
        self.items.append((waits, fn, group))
        return group

    def hold(self, *waits):
        for w in waits:
            w.used = True
        self.items.append((waits, None, None))

    def count(self):
        n = 0
        for _, _, tok in self.items:
            if isinstance(tok, Tok) and tok.used:
                n += 1
                tok.value = n

    def write(self, eng):
        reached = {}
        for waits, fn, tok in self.items:
            for w in waits:
                sem, value = w.target()
                if reached.get(id(sem), 0) < value:
                    eng.wait_ge(sem, value)
                    reached[id(sem)] = value
            if fn is None:
                continue
            ins = fn(eng)
            if isinstance(tok, Group):
                ins.then_inc(tok.sem, 16)
            elif tok.used:
                ins.then_inc(self.sem, 1)


class Banks:

    def __init__(self, banks):
        self.banks, self.free, self.at = banks, [() for _ in banks], 0

    def take(self):
        n = self.at % len(self.banks)
        self.at += 1
        free = self.free[n]
        assert free is not None
        self.free[n] = None
        return n, self.banks[n], free

    def give(self, n, *toks):
        self.free[n] = toks


    def join(self, other):
        both = Banks(self.banks + other.banks)
        both.free = self.free + other.free
        return both


def constants():
    cols, at = [], {}

    def put(name, a):
        a = np.asarray(a, np.float32).reshape(128, -1)
        start = sum(c.shape[1] for c in cols)
        cols.append(a)
        at[name] = (start, start + a.shape[1])

    p = np.arange(128)
    put("ident", np.eye(128))
    put("d8", p[:, None] % 8 == np.arange(8)[None])
    put("rep", p[:, None] % 8 == p[None] % 8)
    put("d16", p[:, None] // 8 == np.arange(16)[None])
    put("iotap", np.stack([p, p + 128], 1))
    put("iota8", np.broadcast_to(np.arange(8), (128, 8)))
    half = 16
    theta = (1.0 / np.float32(10000.0) ** (np.float32(2.0) * np.arange(half, dtype=np.float32) / np.float32(32))).astype(np.float32)
    t = np.arange(L)
    ang = [(t.astype(np.float32)[:, None] * theta[None]).astype(np.float32),
           ((t + np.maximum(t - 63, 0)).astype(np.float32)[:, None] * theta[None]).astype(np.float32)]
    tab = np.stack([np.stack([np.cos(a.astype(np.float64)), np.sin(a.astype(np.float64))], 1) for a in ang], 1)
    put("rope", tab.reshape(2, 128, 4, 16).transpose(1, 0, 2, 3))
    ak = ((64 + np.arange(32)).astype(np.float32)[None] * theta[:, None]).astype(np.float32).astype(np.float64)
    c, s = np.cos(ak), np.sin(ak)
    z = np.zeros((32, 32))
    put("h1", np.concatenate([c, c, z, s, s, z]))
    put("h2", np.concatenate([-s, -s, z, c, c, z]))
    put("h3", np.concatenate([z, z + 1, z, z]))
    s192 = np.arange(192)
    put("im1", np.where(s192[None] <= p[:, None] + 64, 0.0, -BIG))
    put("im0", np.where(np.arange(64)[None] <= p[:, None] % 64, 0.0, -BIG))
    put("t128", np.broadcast_to(128 * np.arange(16), (128, 16)))
    put("iotat", np.broadcast_to(np.arange(NT + 7), (128, NT + 7)))
    put("eps", np.full((128, 1), 1e-5))
    put("mpi", np.full((128, 1), -np.pi))
    j, h, tt = p // 32, (p // 4) % 8, p % 4
    for r in range(4):
        for t0 in ([192 + 16 * r] + ([64 + 16 * r] if r < 2 else [])):
            tok = t0 + 4 * j + tt
            s0 = (t0 // 64 - 1) * 64
            sl = s0 + np.arange(128)
            ok = (sl[None] >= tok[:, None] - 63) & (sl[None] <= tok[:, None])
            col = np.arange(128)
            near = (col[None] // 32 == tt[:, None]) & (col[None] % 32 < tok[:, None] - 63)
            m = np.concatenate([ok, near], 1)
            if t0 < 96:
                sf = 64 + np.arange(32)
                m = np.concatenate([m, sf[None] > tok[:, None]], 1)
            put(f"mask{t0 if t0 < 96 else r}", np.where(m, 0.0, -BIG))
    return np.ascontiguousarray(np.concatenate(cols, 1)), at


CONST, CAT = constants()


PACK = (("Wi", 384), ("wix", 4), ("Wp", 128), ("rd", 17), ("WuqT", 256), ("WukT", 128), ("Wq2", 512), ("WuvT", 128), ("Wout", 512))
PACK_AT, PACK_COLS = {}, 0
for _name, _width in PACK:
    PACK_AT[_name] = (PACK_COLS, PACK_COLS + _width)
    PACK_COLS += _width


def attention(nc, ctx, sem, group, queues, bank, a, c, ident, X0, XT, Y, g_c, g_x0, g_x, stats, load_x, after_pair):
    PE, S, V, G, SP = queues

    def sb(name, shape, dt=F32):
        return ctx.enter_context(nc.sbuf_tensor(name, shape, dt))

    ring = Banks(bank[0:4])
    pring = Banks(bank[4:6])
    pcring = Banks(bank[6:8])

    WP = sb("WP", [128, PACK_COLS])

    def w(name, rows=slice(0, 128)):
        return WP[rows, PACK_AT[name][0]:PACK_AT[name][1]]

    Wp, Wi, Wq2 = w("Wp"), w("Wi"), w("Wq2", slice(0, 64))
    WuqT, WukT, WuvT, Wout = [w(n).rearrange("p (k r) -> p k r", k=4) for n in ("WuqT", "WukT", "WuvT", "Wout")]
    wix, RD = w("wix"), w("rd")
    Wvo = sb("Wvo", [128, 2, 128])
    g_w = group("g_w")
    g_w1 = group("g_w1")
    SP.dma(g_w1, lambda e: e.dma_start(WP[:, 0:388], a["packed"][:, 0:388]))
    load_x(0)
    SP.dma(g_w, lambda e: e.dma_start(WP[:, 388:], a["packed"][:, 388:]))
    load_x(1)

    sd = sb("sd", [128, 17])
    cd = sb("cd", [128, 17])
    ra = sb("ra", [128, 8, 16])
    rb = sb("rb", [128, 8, 16])
    RT = sb("RT", [128, 2, 2, 2, 16])
    GT = sb("GT", [128, 32])
    t = S(lambda e: e.activation(RD, RD, ACT.Exp, scale=-1.0), g_w)
    t = V(lambda e: e.tensor_scalar(RD, RD, 1.0, None, ALU.add), t)
    t = V(lambda e: e.reciprocal(RD, RD), t)
    t1 = S(lambda e: e.activation(sd[:, :], RD, ACT.Sin, scale=float(np.float32(2 * np.pi)), bias=c("mpi")), t, g_c[0])
    t2 = S(lambda e: e.activation(cd[:, :], RD, ACT.Sin, scale=float(np.float32(np.pi))), t)
    t = V(lambda e: e.tensor_tensor(cd[:, :], cd[:, :], cd[:, :], ALU.mult), t2)
    t = V(lambda e: e.tensor_scalar(cd[:, :], cd[:, :], -2.0, 1.0, ALU.mult, ALU.add), t)
    rope = c("rope").rearrange("p (k i) -> p k i", i=16)
    t3 = V(lambda e: e.tensor_tensor(ra[:, :, :], rope, cd[:, 0:16].unsqueeze(1).to_broadcast([128, 8, 16]), ALU.mult), t, g_c[0])
    t4 = V(lambda e: e.tensor_tensor(rb[:, :, :], rope, sd[:, 0:16].unsqueeze(1).to_broadcast([128, 8, 16]), ALU.mult), t1)
    rav = ra[:, :, :].rearrange("p (k f) i -> p k f i", f=2)
    rbv = rb[:, :, :].rearrange("p (k f) i -> p k f i", f=2)
    RTv = RT[:, :, :, :, :].rearrange("p a k f i -> p (a k) f i")
    t5 = V(lambda e: e.tensor_tensor(RTv[:, :, 0, :], rav[:, :, 0, :], rbv[:, :, 1, :], ALU.subtract), t3, t4)
    t_rt = V(lambda e: e.tensor_tensor(RTv[:, :, 1, :], rbv[:, :, 0, :], rav[:, :, 1, :], ALU.add), t3, t4)
    t = V(lambda e: e.tensor_scalar(GT[:, :], c("h1"), cd[:, 16:17], None, ALU.mult), t)
    t = V(lambda e: e.tensor_tensor(GT[:, :], GT[:, :], c("h3"), ALU.add), t)
    t_gt = V(lambda e: e.scalar_tensor_tensor(out=GT[:, :], in0=c("h2"), scalar=sd[:, 16:17], in1=GT[:, :],
                                              op0=ALU.mult, op1=ALU.add), t)

    for f in range(2):
        r = slice(64 * f, 64 * f + 64)
        n, bk, free = pring.take()
        for k in range(4):
            t = PE(lambda e, k=k, r=r, bk=bk: e.matmul(bk[0:64, 32 * k:32 * k + 32], WuqT[r, k, :], WukT[r, k, :],
                                                       start=True, stop=True), *((g_w,) + free if k == 0 else ()))
        t_wabs = V(lambda e, f=f, bk=bk: e.tensor_copy(
            Wq2[:, 0:256].rearrange("p (k f c) -> p f k c", f=2, c=32)[:, f, :, :],
            bk[0:64, 0:128].rearrange("p (k c) -> p k c", c=32)), t)
        pring.give(n, t_wabs)
    for f in range(2):
        r = slice(64 * f, 64 * f + 64)
        n, bk, free = pring.take()
        for k in range(4):
            t = PE(lambda e, r=r, k=k, bk=bk: e.matmul(bk[0:32, 128 * k:128 * k + 128], WuvT[r, k, :], Wout[r, k, :],
                                                       start=True, stop=True), *((g_w,) + free if k == 0 else ()))
        for k in range(4):
            h = 2 * k + f
            x = 32 * (h % 4)
            t_wvo = V(lambda e, k=k, h=h, x=x, bk=bk: e.tensor_copy(Wvo[x:x + 32, h // 4, :], bk[0:32, 128 * k:128 * k + 128]), t)
        pring.give(n, t_wvo)

    QT = sb("QT", [128, 2, NH * 512])
    cqT = sb("cqT", [64, 512])
    kiT = sb("kiT", [128, 512])
    qiT = sb("qiT", [128, 2, 512])
    AB = sb("AB", [128, 4, 288])
    M = sb("M", [128, 4, 288])
    SRC = sb("SRC", [128, 4, 64])
    RS = sb("RS", [128, 4, 64])
    R2 = sb("R2", [128, 4, 64])
    Qtok = sb("Qtok", [128, 4, NH, 128])
    pa = sb("pa", [128, NH, 2, 16])
    pb = sb("pb", [128, NH, 2, 16])
    qa = sb("qa", [128, NH, 2, 16])
    qbuf = sb("qbuf", [128, NH, 2, 16])
    ka = sb("ka", [128, 2, 2, 16])
    kb = sb("kb", [128, 2, 2, 16])
    Kt = sb("Kt", [128, 4, 128])
    Kf = sb("Kf", [128, 2, 128])
    RL = sb("RL", [128, 4, 192])
    I1 = sb("I1", [128, 3, 192])
    V8 = sb("V8", [128, 3, 32])
    IX = sb("IX", [128, 3, 32], U32)
    IXb = sb("IXb", [128, 3, 32], BF16)
    KL = sb("KL", [128, 2, 512])
    KF = sb("KF", [128, 2, 2, 32])
    KG = sb("KG", [128, 2, 4, 3, 128], BF16)
    CK = sb("CK", [128, 2, 4, 32])
    CM = sb("CM", [128, 2, 2, 32])
    BC = sb("BC", [128, 2, 6144], BF16)
    SLOTS = {"OH": 3, "Gs": 4, "Vg": 5, "P": 4, "PT": 3}
    OH = sb("OH", [128, SLOTS["OH"], 512], BF16)
    OH2 = sb("OH2", [64, SLOTS["OH"], 512], BF16)
    Gs = sb("Gs", [128, SLOTS["Gs"], 512])
    Vg = sb("Vg", [128, SLOTS["Vg"], 4, 32])
    P = sb("P", [128, SLOTS["P"], 288])
    mx = sb("mx", [128, SLOTS["P"], 4])
    PT = sb("PT", [128, SLOTS["PT"], 384])
    SM = sb("SUMS", [128, 3, 4])
    OS = sb("OSUM", [128, 2, 4, 32])
    pcT = sb("pcT", [128, 2, 2, 128])
    idxd = nc.dram_tensor("idxd", [B, 192 * 32], BF16, kind="Internal").ap()

    G(lambda e: e.memset(Kt[:, :, :], 0.0))
    t_zero = G(lambda e: e.memset(Kf[:, :, :], 0.0))

    ready, far, ended = {}, {}, {}

    def prepare(p):
        q = p % 2
        before = ended.get(("prepare", p - 1), ()) + ended.get(("attend", 2 * p - 3), ())
        for queue in (PE, S, V, G, SP):
            queue.hold(*before)
        xs = slice(512 * p, 512 * p + 512)

        def project(w, rows, dst, eng, g):
            n, bk, free = pring.take()
            t = PE(lambda e: e.matmul(bk[0:rows, :], w, XT[:, xs], start=True, stop=True), g_x[p], g, *free)
            if eng is S:
                t = S(lambda e: e.activation(dst, bk[0:rows, :], ACT.Copy), t)
            else:
                t = V(lambda e: e.tensor_copy(dst, bk[0:rows, :]), t)
            pring.give(n, t)
            return t

        t_ki = project(Wi[:, 0:128], 128, kiT[:, :], S, g_w1)
        yield
        t_q0 = project(Wi[:, 128:256], 128, qiT[:, 0, :], V, g_w1)
        t_q1 = project(Wi[:, 256:384], 128, qiT[:, 1, :], S, g_w1)
        yield

        used_rl, t_i = [], {}

        def best(k, rows_of, width, mask):
            banks = []
            m = 128 if width == 192 else 64
            for f in range(2):
                n, bk, free = pring.take()
                r = slice(64 * f, 64 * f + 64)
                first = (t_ki, t_q0, t_q1) + free
                for g in range(2):
                    for o, b in rows_of:
                        tq = 256 * b + m
                        t = PE(lambda e, r=r, g=g, o=o, b=b, tq=tq, bk=bk: e.matmul(
                            bk[o:o + m, g * width:g * width + width], qiT[r, g, tq:tq + m],
                            kiT[r, 256 * b:256 * b + width], start=True, stop=True), *first)
                        first = ()
                t = S(lambda e, f=f, bk=bk: e.activation(
                    RL[:, f:4:2, 0:width], bk[:, 0:2 * width].rearrange("p (h s) -> p h s", h=2), ACT.Relu), t, *used_rl)
                pring.give(n, t)
                banks.append(t)
            yield
            I = I1[:, k, 0:width]
            t = V(lambda e: e.scalar_tensor_tensor(out=I, in0=RL[:, 0, 0:width], scalar=wix[:, 0:1], in1=mask,
                                                   op0=ALU.mult, op1=ALU.add), g_c[0], *banks)
            for h in range(1, 4):
                t = V(lambda e, h=h: e.scalar_tensor_tensor(out=I, in0=RL[:, h, 0:width], scalar=wix[:, h:h + 1], in1=I,
                                                            op0=ALU.mult, op1=ALU.add), t)
                if h == 1:
                    yield
            used_rl[:] = [t]
            yield
            for r in range(4):
                v8 = V8[:, k, 8 * r:8 * r + 8]
                t = V(lambda e, v8=v8: e.max(v8, I), t)
                t = V(lambda e, v8=v8, r=r: e.max_index(IX[:, k, 8 * r:8 * r + 8], v8, I), t)
                if r < 3:
                    t = V(lambda e, v8=v8: e.match_replace(I, v8, I, LOW), t)
                    yield
            t_i[k] = V(lambda e: e.tensor_copy(IXb[:, k, :], IX[:, k, :]), t)
            yield

        g_i = [group(f"g_i{2 * p + o}") for o in range(2)]

        def keep(o):
            b = 2 * p + o
            SP.dma(g_i[o], lambda e: e.dma_start(idxd[b, 2048:6144].rearrange("(t k) -> t k", k=32), IXb[:, o, :]), t_i[o])
            SP.dma(g_i[o], lambda e: e.dma_start(idxd[b, 0:2048].rearrange("(t k) -> t k", k=32),
                                                 IXb[64 * o:64 * o + 64, 2, :]), t_i[2])
            far[b] = g_i[o]

        yield from best(2, [(0, 0), (64, 1)], 64, c("im0"))
        yield from best(0, [(0, 0)], 192, c("im1"))
        keep(0)
        t_cq = project(Wp[:, 0:64], 64, cqT[:, :], V, g_w)
        yield

        n, bk, free = pring.take()
        for i in range(4):
            PE(lambda e, i=i, bk=bk: e.matmul(bk[:, 64 * i:64 * i + 64], XT[:, 512 * p + 128 * i:512 * p + 128 * i + 128],
                                              Wp[:, 64:128], start=True, stop=True), *free)
        for o in range(2):
            t = PE(lambda e, o=o, bk=bk: e.matmul(bk[:, 256 + 32 * o:288 + 32 * o],
                                                  XT[:, 512 * p + 256 * o + 64:512 * p + 256 * o + 192], Wp[:, 64:96],
                                                  start=True, stop=True))
        kv = bk[:, 0:256].rearrange("p (i f) -> p i f", i=4)
        S(lambda e, bk=bk: e.activation(CM[:, q, :, :], bk[:, 256:320].rearrange("p (o f) -> p o f", o=2), ACT.Copy), t)
        t = S(lambda e, kv=kv: e.activation(CK[:, q, :, :], kv[:, :, 0:32], ACT.Copy))
        t_z = S(lambda e, kv=kv: e.activation(M[:, :, 0:32], kv[:, :, 32:64], ACT.Copy))
        pring.give(n, t_z)
        ck = CK[:, q, :, :]
        G(lambda e: e.tensor_copy(SRC[:, :, 32:64], ck), t)
        G(lambda e: e.tensor_copy(Kt[:, :, 32:64], ck), t_zero)
        t_ck = G(lambda e: e.tensor_copy(Kf[:, :, 32:64], ck[:, 0:4:2, :]))
        yield
        for i in range(4):
            n, bk, free = pring.take()
            t = PE(lambda e, i=i, bk=bk: e.matmul(bk[:, :], cqT[:, 128 * i:128 * i + 128], Wq2, start=True, stop=True),
                   t_cq, t_wabs, *free)
            t_z = S(lambda e, i=i, bk=bk: e.activation(M[:, i, 32:288], bk[:, 256:512], ACT.Copy), t)
            t_qa = V(lambda e, i=i, bk=bk: e.tensor_copy(Qtok[:, i, :, 32:64],
                                                         bk[:, 0:256].rearrange("p (h f) -> p h f", h=NH)), t_z)
            pring.give(n, t_qa)
            yield
        S(lambda e: e.activation(AB[:, :, :], M[:, :, :], ACT.Abs), t_z)
        yield
        S(lambda e: e.activation(AB[:, :, :], AB[:, :, :], ACT.Exp, scale=-1.0))
        yield
        t = S(lambda e: e.activation(AB[:, :, :], AB[:, :, :], ACT.Ln, bias=1.0))
        t_m = V(lambda e: e.scalar_tensor_tensor(out=M[:, :, :], in0=M[:, :, :], scalar=0.0, in1=AB[:, :, :],
                                                 op0=ALU.max, op1=ALU.add), t)
        yield

        def part3(k):
            return KG[:, q, :, k, 0:64]

        def both(k):
            return KG[:, q, :, k, :].rearrange("p i (r f) -> p i r f", r=2)

        def twice(s):
            return s.unsqueeze(2).to_broadcast([128, 4, 2, 64])

        V(lambda e: e.tensor_copy(SRC[:, :, 0:32], M[:, :, 0:32]))
        V(lambda e: e.tensor_copy(both(0), twice(SRC[:, :, :])), t_ck)
        V(lambda e: e.tensor_tensor(RS[:, :, :], SRC[:, :, :], part3(0), ALU.subtract))
        yield
        V(lambda e: e.tensor_copy(both(1), twice(RS[:, :, :])))
        V(lambda e: e.tensor_tensor(R2[:, :, :], RS[:, :, :], part3(1), ALU.subtract))
        t_kg = V(lambda e: e.tensor_copy(both(2), twice(R2[:, :, :])))
        yield

        for o in range(2):
            mk = M[:, 2 * o:2 * o + 2, 0:32].rearrange("p i (f j) -> p i f j", f=2)
            cs, sn = [RT[:, :, 0, f, :].unsqueeze(2).to_broadcast([128, 2, 2, 16]) for f in range(2)]
            G(lambda e, mk=mk, cs=cs: e.tensor_tensor(ka[:, :, :, :], mk, cs, ALU.mult), t_m, t_rt)
            G(lambda e, mk=mk, sn=sn: e.tensor_tensor(kb[:, :, :, :], mk, sn, ALU.mult))
            G(lambda e, o=o: e.tensor_tensor(Kt[:, 2 * o:2 * o + 2, 96:112], ka[:, :, 0, :], kb[:, :, 1, :], ALU.subtract))
            G(lambda e, o=o: e.tensor_tensor(Kt[:, 2 * o:2 * o + 2, 112:128], kb[:, :, 0, :], ka[:, :, 1, :], ALU.add))
        t_kt = G(lambda e: e.tensor_copy(Kf[:, :, 0:32], Kt[:, 0:4:2, 96:128]))
        n, bk, free = pring.take()
        for i in range(4):
            t = PE(lambda e, i=i, bk=bk: e.transpose(bk[:, 128 * i:128 * i + 128], Kt[:, i, :], ident), t_kt, *free)
        t_kl = S(lambda e, bk=bk: e.activation(KL[:, q, :], bk[:, :], ACT.Copy), t)
        pring.give(n, t_kl)
        n, bk, free = pring.take()
        for o in range(2):
            t = PE(lambda e, o=o, bk=bk: e.transpose(bk[:, 128 * o:128 * o + 128], Kf[:, o, :], ident), *free)
        t_kf = S(lambda e, bk=bk: e.activation(KF[:, q, :, :], bk[:, 0:256].rearrange("p (o s) -> p o s", o=2)[:, :, 64:96], ACT.Copy), t)
        pring.give(n, t_kf)
        yield
        t_qt, rotated = {}, {}

        def rotate(i):
            mq = M[:, i, 32:288].rearrange("p (h f j) -> p h f j", h=NH, f=2)
            rotated[i] = [t_qa]
            for k in range(2):
                E = V if (k == 0 and (i % 2 or p == 0)) else G
                xa, xb = (pa, pb) if E is G else (qa, qbuf)
                at = 96 if k else 0
                cs, sn = [RT[:, i % 2, k, f, :].unsqueeze(1).unsqueeze(1).to_broadcast([128, NH, 2, 16]) for f in range(2)]
                E(lambda e, mq=mq, cs=cs, xa=xa: e.tensor_tensor(xa[:, :, :, :], mq, cs, ALU.mult), t_m, t_rt)
                E(lambda e, mq=mq, sn=sn, xb=xb: e.tensor_tensor(xb[:, :, :, :], mq, sn, ALU.mult))
                if E is V:
                    yield
                E(lambda e, at=at, xa=xa, xb=xb: e.tensor_tensor(Qtok[:, i, :, at:at + 16], xa[:, :, 0, :], xb[:, :, 1, :], ALU.subtract))
                t = E(lambda e, at=at, xa=xa, xb=xb: e.tensor_tensor(Qtok[:, i, :, at + 16:at + 32], xb[:, :, 0, :], xa[:, :, 1, :], ALU.add))
                if k == 0:
                    E(lambda e, xa=xa, xb=xb: e.tensor_tensor(Qtok[:, i, :, 64:80], xb[:, :, 0, :], xa[:, :, 1, :], ALU.add))
                    t = E(lambda e, xa=xa, xb=xb: e.tensor_tensor(Qtok[:, i, :, 80:96], xb[:, :, 1, :], xa[:, :, 0, :], ALU.subtract))
                rotated[i].append(t)
            yield

        def turned(i):
            for f in range(2):
                n, bk, free = pring.take()
                for h in range(4):
                    t = PE(lambda e, h=h, f=f, bk=bk: e.transpose(bk[:, 128 * h:128 * h + 128], Qtok[:, i, 4 * f + h, :], ident),
                           *(free + tuple(rotated[i]) if h == 0 else ()))
                dst = QT[:, q, :].rearrange("p (g h t) -> p h g t", h=NH, t=4)[:, 4 * f:4 * f + 4, 32 * i:32 * i + 32, :]
                src = bk[:, :].rearrange("p (h g t) -> p h g t", h=4, t=4)
                t_qt[i, f] = S(lambda e, dst=dst, src=src: e.activation(dst, src, ACT.Copy), t)
                pring.give(n, t_qt[i, f])
                yield
            ready[p, i] = (t_qt[i, 0], t_qt[i, 1], t_kl, t_kf, t_kg, t_ck)

        for i in range(4):
            yield from rotate(i)
            if i:
                yield from turned(i - 1)
            if i == 1:
                yield from best(1, [(0, 1)], 192, c("im1"))
                keep(1)
        yield from turned(3)
        ended["prepare", p] = (t_qt[3, 1], t_kg, t_kt, g_i[0], g_i[1]) + tuple(rotated[2] + rotated[3])

    g_b = [group(f"g_b{b}") for b in range(B)]
    slot, state = {}, {}

    def spread(b):
        SP.dma(g_b[b], lambda e: e.dma_start(BC[:, b % 2, :], idxd[b, :].partition_broadcast(128)), far[b],
               *ended.get(("onehot", b - 2), ()))

    def old(name, k, *keys):
        k %= SLOTS[name]
        return tuple(slot[name, k, key] for key in keys if (name, k, key) in slot)

    def one_hot(b, r, k):
        t0 = 16 * r
        if t0 < 64:
            return
        cols = slice((t0 - 64) * 32, (t0 - 64) * 32 + 512)
        t = V.free(lambda e: e.tensor_scalar(OH[:, k % SLOTS["OH"], :], BC[:, b % 2, cols], c("iotap")[:, 0:1], None, ALU.is_equal),
              g_b[b], *old("OH", k, "pe"))
        if t0 >= 192:
            t = V.free(lambda e: e.tensor_scalar(OH2[:, k % SLOTS["OH"], :], BC[0:64, b % 2, cols], c("iotap", slice(0, 64))[:, 1:2], None,
                                            ALU.is_equal))
        state["OH", b, r] = t
        if r == 15:
            ended["onehot", b] = (t,)

    def gather(b, r, k):
        t0, o, q = 16 * r, b % 2, (b // 2) % 2
        if t0 < 64:
            return
        n, bk, free = ring.take()
        two = t0 >= 192
        first = (state["OH", b, r],) + ready[b // 2, 2 * o + r // 8] + free
        for f in range(3):
            t = PE(lambda e, f=f: e.matmul(bk[:, :], KG[:, q, 2 * o, f, :], OH[:, k % SLOTS["OH"], :], start=(f == 0),
                                           stop=(f == 2 and not two)), *(first if f == 0 else ()))
        if two:
            for f in range(3):
                t = PE(lambda e, f=f: e.matmul(bk[:, :], KG[0:64, q, 2 * o + 1, f, :], OH2[:, k % SLOTS["OH"], :], start=False,
                                               stop=(f == 2)))
        slot["OH", k % SLOTS["OH"], "pe"] = t
        t = V.free(lambda e: e.tensor_tensor(Gs[:, k % SLOTS["Gs"], :].rearrange("p (t k) -> p t k", k=32),
                                        bk[:, :].rearrange("p (t k) -> p t k", k=32),
                                        GT[:, :].unsqueeze(1).to_broadcast([128, 16, 32]), ALU.mult), t, t_gt,
              *old("Gs", k, "pe"))
        ring.give(n, t)
        state["Gs", b, r] = t

    def widths(r):
        t0 = 16 * r
        far_, future = t0 >= 64, 64 <= t0 < 96
        return (128 if far_ else 96), far_, future

    def score(b, r, k):
        t0, o, q = 16 * r, b % 2, (b // 2) % 2
        tq = 256 * o + t0
        near, far_, future = widths(r)
        s0 = 256 * o + (max(t0 // 64 - 1, 0)) * 64
        width = near + (128 if far_ else 0) + (32 if future else 0)
        n, bk, free = ring.take()
        rows = QT[:, q, 8 * tq:8 * tq + 128]
        t = PE(lambda e: e.matmul(bk[:, 0:near], rows, KL[:, q, s0:s0 + near], start=True, stop=True),
               *(ready[b // 2, 2 * o + r // 8] + free))
        if far_:
            for j in range(4):
                t = PE(lambda e, j=j: e.matmul(bk[32 * j:32 * j + 32, 128:256], QT[:, q, 8 * tq + 32 * j:8 * tq + 32 * j + 32],
                                               Gs[:, k % SLOTS["Gs"], 128 * j:128 * j + 128], start=True, stop=True),
                       *((state["Gs", b, r],) if j == 0 else ()))
            if future:
                t = PE(lambda e: e.matmul(bk[:, 256:288], rows, KF[:, q, o, :], start=True, stop=True))
        waits = (t,) + old("P", k, "pe")
        Pr, m = P[:, k % SLOTS["P"], 0:width], mx[:, k % SLOTS["P"], :]
        if far_:
            mask = c(f"mask{t0 if future else r % 4}")
            t = V.free(lambda e: e.tensor_tensor_reduce(out=Pr, in0=bk[:, 0:width], in1=mask, scale=1.0, scalar=LOW, op0=ALU.add,
                                                   op1=ALU.max, accum_out=m[:, 0:1]), g_c[1], *waits)
            src = Pr
        else:
            t = V.free(lambda e: e.tensor_reduce(m[:, 0:1], bk[:, 0:width], AX, ALU.max), *waits)
            src = bk[:, 0:width]
        t2 = V.free(lambda e: e.tensor_scalar(m[:, 1:2], m[:, 0:1], -SCALE, None, ALU.mult), t)
        t3 = S.free(lambda e: e.activation(Pr, src, ACT.Exp, scale=SCALE, bias=m[:, 1:2],
                                       accum_out=SM[:, (k // 4) % 3, k % 4:k % 4 + 1]), t2)
        ring.give(n, t if far_ else t3)
        state["E", b, r] = t3

    def values_turned(b, r, k):
        if not widths(r)[1]:
            return
        n, bk, free = ring.take()
        for j in range(4):
            t = PE(lambda e, j=j: e.transpose(bk[:, 32 * j:32 * j + 32], Gs[32:64, k % SLOTS["Gs"], 128 * j:128 * j + 128],
                                              ident[32:64, 32:64]), *((state["Gs", b, r],) + free if j == 0 else ()))
        slot["Gs", k % SLOTS["Gs"], "pe"] = t
        t = S.free(lambda e: e.activation(Vg[:, k % SLOTS["Vg"], :, :], bk[:, 0:128].rearrange("p (j f) -> p j f", j=4), ACT.Copy), t,
              *old("Vg", k, "pe"))
        ring.give(n, t)
        state["Vg", b, r] = t

    def turn(b, r, k):
        near, far_, future = widths(r)
        n, bk, free = ring.take()
        t = PE(lambda e: e.transpose(bk[0:near, 0:128], P[:, k % SLOTS["P"], 0:near], ident), state["E", b, r], *free)
        if far_:
            t = PE(lambda e: e.transpose(bk[:, 128:256], P[:, k % SLOTS["P"], 128:256], ident))
        if future:
            t = PE(lambda e: e.transpose(bk[0:32, 256:384], P[:, k % SLOTS["P"], 256:288], ident))
        slot["P", k % SLOTS["P"], "pe"] = t
        waits = (t,) + old("PT", k, "pe")
        if far_:
            t = S.free(lambda e: e.activation(PT[:, k % SLOTS["PT"], 0:256], bk[:, 0:256], ACT.Copy), *waits)
            if future:
                t = S.free(lambda e: e.activation(PT[0:32, k % SLOTS["PT"], 256:384], bk[0:32, 256:384], ACT.Copy))
        else:
            t = S.free(lambda e: e.activation(PT[0:near, k % SLOTS["PT"], 0:128], bk[0:near, 0:128], ACT.Copy), *waits)
        ring.give(n, t)
        state["PT", b, r] = t

    def value(b, r, k):
        o, q = b % 2, (b // 2) % 2
        near, far_, future = widths(r)
        if r % 4 == 0:
            state["pc"] = pcring.take()
        n, bk, free = state["pc"]
        i = r // 4
        v = CK[0:near, q, 2 * o, :] if i < 2 else CM[:, q, o, :] if i == 2 else CK[:, q, 2 * o + 1, :]
        c0 = 32 * (r % 4)
        s = k % SLOTS["PT"]
        state["pc_at", b, r] = state["pc"]
        t = PE(lambda e: e.matmul(bk[:, c0:c0 + 32], PT[0:near, s, 0:128], v, start=True, stop=not far_),
               state["PT", b, r], *(free if r % 4 == 0 else ()))
        if far_:
            for j in range(4):
                t = PE(lambda e, j=j: e.matmul(bk[32 * j:32 * j + 32, c0:c0 + 32], PT[:, s, 128 + 32 * j:160 + 32 * j],
                                               Vg[:, k % SLOTS["Vg"], j, :], start=False, stop=not future),
                       *((state["Vg", b, r],) if j == 0 else ()))
        if future:
            t = PE(lambda e: e.matmul(bk[:, c0:c0 + 32], PT[0:32, s, 256:384], CM[0:32, q, o, :], start=False, stop=True))
        slot["PT", s, "pe"] = slot["Vg", k % SLOTS["Vg"], "pe"] = t
        state["O", b, r] = t

    def divide(b, r, k):
        if r % 4 != 3:
            return
        n, bk, free = state["pc_at", b, r]
        sums = SM[:, (k // 4) % 3, :]
        t = V.free(lambda e: e.reciprocal(sums, sums), state["E", b, r])
        t = V.free(lambda e: e.tensor_tensor(OS[:, (k // 4) % 2, :, :], bk[:, 0:128].rearrange("p (s f) -> p s f", f=32),
                                             sums.unsqueeze(2).to_broadcast([128, 4, 32]), ALU.mult), t, state["O", b, r],
                   *ended.get(("heads", (k // 4) % 2), ()))
        pcring.give(n, t)
        state["OS", b, r] = t

    def heads(b, r, k):
        if r % 4 != 3:
            return
        n, bk, free = ring.take()
        f, g = r // 8, (r // 4) % 2
        first = (state["OS", b, r],) + free
        for s in range(4):
            for x in range(4):
                t = PE(lambda e, s=s, x=x: e.matmul(
                    bk[32 * x:32 * x + 32, 32 * s:32 * s + 32], OS[:, (k // 4) % 2, s, :],
                    ident.rearrange("p (j h x t) -> p x h j t", j=4, h=2, x=4)[:, x, :, :, :], start=True, stop=True), *first)
                first = ()
        ended["heads", (k // 4) % 2] = (t,)
        src = bk[:, 0:128].rearrange("p (s h t) -> p h s t", s=4, h=2)
        t = S.free(lambda e: e.activation(pcT[:, f, :, 64 * g:64 * g + 64].rearrange("p h (s t) -> p h s t", t=16), src, ACT.Copy),
                   t, *ended.get(("out", f), ()))
        ring.give(n, t)
        state["pcT"] = t

    def project_out(b, f):
        i = 2 * b + f
        n, bk, free = pring.take()
        for h in range(2):
            t = PE(lambda e, h=h: e.matmul(bk[:, 0:128], pcT[:, f, h, :], Wvo[:, h, :], start=(h == 0), stop=(h == 1)),
                   *((state["pcT"], t_wvo) + free if h == 0 else ()))
        ended["out", f] = (t,)
        t = V(lambda e: e.tensor_tensor(Y[:, i, :], bk[:, 0:128], X0[:, i, :], ALU.add), t, g_x0)
        pring.give(n, t)
        t = stats(i, t)
        if f == 1:
            ended["attend", b] = (ended["out", 0][0], ended["out", 1][0], t)
        return t

    steps = [(b, r) for b in range(B) for r in range(16)]
    STAGES = ((8, heads), (7, divide), (6, value), (5, turn), (3, score), (3, values_turned), (1, gather), (0, one_hot))
    LAST = 8
    preparing, tails = [prepare(0)], []
    state["spread"] = 0

    def advance(n):
        for _ in range(n):
            if preparing and next(preparing[0], "end") == "end":
                preparing.pop(0)
        b = state["spread"]
        if b in far and (b < 2 or ("onehot", b - 2) in ended):
            spread(b)
            state["spread"] += 1

    for k in range(len(steps) + LAST + 1):
        if k < len(steps):
            b, r = steps[k]
            while (b // 2, 2 * (b % 2) + r // 8) not in ready or state["spread"] <= b:
                advance(1)
        for lag, stage in STAGES:
            if 0 <= k - lag < len(steps):
                stage(*steps[k - lag], k - lag)
        if k > LAST and (k - LAST - 1) % 8 == 7:
            b, r = steps[k - LAST - 1]
            t = project_out(b, r // 8)
            if b % 2 and r == 15:
                tails.append(after_pair(pring, b // 2, t))
        if k % 32 == LAST + 2 and k // 32 < 3:
            preparing.append(prepare(k // 32 + 1))
        if tails and next(tails[0], "end") == "end":
            tails.pop(0)
        advance(2)
    for tail in tails:
        for _ in tail:
            pass
    return ring.join(pring).join(pcring)


def experts(nc, ctx, sem, group, queues, banks, a, c, ident, X0, Y, xs_d, logit, g_z, t_logit, stats, pieces):
    PE, S, V, G, SP = queues
    E, NF, TS = 8, 512, TILES
    AHEAD, EACH = 24, 2

    def sb(name, shape, dt=F32):
        return ctx.enter_context(nc.sbuf_tensor(name, shape, dt))

    ring = Banks(banks)
    W1 = sb("W1", [128, E * NF])
    W2 = sb("W2", [128, E * 4 * 128])
    oneb = sb("oneb", [128, 128], BF16)
    before = sb("before", [128, 128], BF16)
    route = sb("route", [128, NT, E])
    rest = sb("rest", [128, E])
    ones8 = sb("ones8", [128, E])
    top = sb("top", [128, NT])
    pick = sb("pick", [128, NT])
    hot = sb("hot", [128, NT, E])
    hotb = sb("hotb", [128, NT, E], BF16)
    rank = sb("rank", [128, NT, E])
    cnt = sb("cnt", [128, E])
    cmp16 = sb("cmp16", [128, E, 16])
    tiles = sb("tiles", [128, E])
    ends = sb("ends", [128, E])
    starts = sb("starts", [128, E])
    pos = sb("pos", [128, NT])
    posu = sb("posu", [128, NT], U32)
    cmpt = sb("cmpt", [128, TS, E])
    tef = sb("tef", [128, TS])
    tei = sb("tei", [128, TS], I32)
    NB = 4
    Xs = sb("Xs", [128, TS, 128])
    XsT = sb("XsT", [128, NB, 128])
    H = sb("H", [128, NB, NF])
    HT = sb("HT", [128, NB, 4, 128])
    Ys = sb("Ys", [128, NB, 128])
    Yg = Xs
    ys_d = nc.dram_tensor("ys_d", [TS * 128, 128], F32, kind="Internal").ap()

    g_1, g_2, g_s = [group(f"g_f{k}") for k in ("1", "2", "s")]
    for e0 in range(0, E, 4):
        SP.dma(g_1, lambda e, e0=e0: e.dma_start(W1[:, e0 * NF:(e0 + 4) * NF].rearrange("p (e f) -> p e f", e=4),
                                                 a["W1"][e0:e0 + 4].rearrange("e p f -> p e f")))
    for e0 in range(0, E, 4):
        SP.dma(g_2, lambda e, e0=e0: e.dma_start(
            W2[:, e0 * 512:(e0 + 4) * 512].rearrange("p (e c d) -> p (e c) d", e=4, c=4),
            a["W2"][e0:e0 + 4].rearrange("e (c p) d -> p (e c) d", p=128)))
    G(lambda e: e.memset(oneb[:, :], 1.0))
    t_one = G(lambda e: e.affine_select(out=before[:, :], in_=oneb[:, :], compare_op=ALU.is_gt, fill=0.0, base=0,
                                        pattern=[[1, 128]], channel_multiplier=-1))

    def advance(n):
        for _ in range(n):
            next(pieces, None)

    def wide(s):
        return s.unsqueeze(2).to_broadcast([128, NT, E])

    def over(s):
        return s.unsqueeze(1).to_broadcast([128, NT, E])

    t = S(lambda e: e.activation(route[:, :, :], logit[:, :, :], ACT.Sigmoid), t_logit)
    V(lambda e: e.memset(ones8[:, :], 1.0))
    V(lambda e: e.tensor_scalar(rest[:, :], c("iota8"), float(E), None, ALU.subtract))
    t_top = V(lambda e: e.tensor_reduce(top[:, :], route[:, :, :], AX, ALU.max), t)
    V(lambda e: e.tensor_tensor(hot[:, :, :], route[:, :, :], wide(top[:, :]), ALU.is_equal))
    V(lambda e: e.tensor_tensor(hot[:, :, :], hot[:, :, :], over(rest[:, :]), ALU.mult))
    V(lambda e: e.tensor_reduce(pick[:, :], hot[:, :, :], AX, ALU.min))
    V(lambda e: e.tensor_tensor(hot[:, :, :], over(rest[:, :]), wide(pick[:, :]), ALU.is_equal))
    t_hot = V(lambda e: e.tensor_copy(hotb[:, :, :], hot[:, :, :]))
    advance(1)

    n, bk, free = ring.take()
    hots = hotb[:, :, :].rearrange("p i e -> p (i e)")
    PE(lambda e, bk=bk: e.matmul(bk[:, 0:128], before[:, :], hots, start=True, stop=False), t_hot, t_one, *free)
    for k in range(1, NT):
        t = PE(lambda e, k=k, bk=bk: e.matmul(bk[:, E * k:128], oneb[:, :], hots[:, 0:128 - E * k], start=False, stop=(k == NT - 1)))
    t = V(lambda e, bk=bk: e.tensor_copy(rank[:, :, :].rearrange("p i e -> p (i e)"), bk[:, 0:128]), t)
    ring.give(n, t)
    n, bk, free = ring.take()
    for k in range(NT):
        t = PE(lambda e, k=k, bk=bk: e.matmul(bk[:, 0:E], oneb[:, :], hots[:, E * k:E * k + E], start=(k == 0), stop=(k == NT - 1)), *free)
    t = V(lambda e, bk=bk: e.tensor_copy(cnt[:, :], bk[:, 0:E]), t)
    ring.give(n, t)
    V(lambda e: e.tensor_tensor(cmp16[:, :, :], cnt[:, :].unsqueeze(2).to_broadcast([128, E, 16]),
                                c("t128").unsqueeze(1).to_broadcast([128, E, 16]), ALU.is_gt))
    V(lambda e: e.tensor_reduce(tiles[:, :], cmp16[:, :, :], AX, ALU.add))
    V(lambda e: e.tensor_tensor_scan(ends[:, :], ones8[:, :], tiles[:, :], 0.0, ALU.mult, ALU.add))
    V(lambda e: e.tensor_tensor(starts[:, :], ends[:, :], tiles[:, :], ALU.subtract))
    V(lambda e: e.tensor_scalar(starts[:, :], starts[:, :], 128.0, None, ALU.mult))
    V(lambda e: e.tensor_tensor(rank[:, :, :], rank[:, :, :], starts[:, :].unsqueeze(1).to_broadcast([128, NT, E]), ALU.add))
    V(lambda e: e.tensor_tensor(rank[:, :, :], rank[:, :, :], hot[:, :, :], ALU.mult))
    V(lambda e: e.tensor_reduce(pos[:, :], rank[:, :, :], AX, ALU.add))
    t_pos = V(lambda e: e.tensor_copy(posu[:, :], pos[:, :]))
    for i in range(NT):
        G.dma(g_s, lambda e, i=i: e.indirect_dma_start(xs_d, bass.IndirectOffsetOnAxis(posu[:, i:i + 1], 0), X0[:, i, :], None),
              t_pos, g_z)
    advance(1)
    V(lambda e: e.tensor_tensor(cmpt[:, :, :], ends[:, :].unsqueeze(1).to_broadcast([128, TS, E]),
                                c("iotat").unsqueeze(2).to_broadcast([128, TS, E]), ALU.is_le))
    V(lambda e: e.tensor_reduce(tef[:, :], cmpt[:, :, :], AX, ALU.add))
    V(lambda e: e.tensor_scalar(tef[:, :], tef[:, :], float(E - 1), float(NF), ALU.min, ALU.mult))
    t_te = V(lambda e: e.tensor_copy(tei[:, :], tef[:, :]))

    advance(AHEAD)
    at = {}
    GROUPS = [(0, 2), (2, 6), (6, 12), (12, 18), (18, TS)]
    g_ld = [group(f"g_ld{k}") for k in range(len(GROUPS))]
    g_st = [group(f"g_st{k}") for k in range(TS)]
    st, of = {}, {}
    xv = xs_d.rearrange("(k p) d -> p k d", p=128)
    for g, (lo, hi) in enumerate(GROUPS):
        SP.dma(g_ld[g], lambda e, lo=lo, hi=hi: e.dma_start(Xs[:, lo:hi, :], xv[:, lo:hi, :]), g_s)
        of.update({k: g_ld[g] for k in range(lo, hi)})

    def turn(k):
        n, bk, free = ring.take()
        t = PE(lambda e: e.transpose(bk[:, 0:128], Xs[:, k, :], ident), of[k], *free)
        t = V.free(lambda e: e.tensor_copy(XsT[:, k % NB, :], bk[:, 0:128]), t, *([st["h", k - NB]] if k >= NB else []))
        ring.give(n, t)
        st["xt", k] = t

    def first(k):
        n, bk, free = ring.take()

        def mm(e):
            at[k] = e.value_load(tei[0:1, k:k + 1], min_val=0, max_val=(E - 1) * NF)
            return e.matmul(bk[:, :], XsT[:, k % NB, :], W1[:, bass.ds(at[k], NF)], start=True, stop=True)

        t = st["h", k] = PE(mm, st["xt", k], t_te, g_1, *free)
        t = S.free(lambda e: e.activation(H[:, k % NB, :], bk[:, :], ACT.Gelu), t, *([st["ht", k - NB]] if k >= NB else []))
        ring.give(n, t)
        st["g", k] = t

    def second(k):
        n, bk, free = ring.take()
        for f in range(4):
            t = PE(lambda e, f=f: e.transpose(bk[:, 128 * f:128 * f + 128], H[:, k % NB, 128 * f:128 * f + 128], ident),
                   *((st["g", k],) + free if f == 0 else ()))
        st["ht", k] = t
        t = V.free(lambda e: e.tensor_copy(HT[:, k % NB, :, :], bk[:, :].rearrange("p (f t) -> p f t", f=4)), t,
                   *([st["y", k - NB]] if k >= NB else []))
        ring.give(n, t)
        st["hts", k] = t

    def third(k):
        n, bk, free = ring.take()
        for f in range(4):
            t = PE(lambda e, f=f: e.matmul(bk[:, 0:128], HT[:, k % NB, f, :], W2[:, bass.ds(at[k] + 128 * f, 128)],
                                           start=(f == 0), stop=(f == 3)), *((st["hts", k], g_2) + free if f == 0 else ()))
        st["y", k] = t
        t = S.free(lambda e: e.activation(Ys[:, k % NB, :], bk[:, 0:128], ACT.Copy), t, *([g_st[k - NB]] if k >= NB else []))
        ring.give(n, t)
        SP.dma(g_st[k], lambda e: e.dma_start(ys_d[128 * k:128 * k + 128, :], Ys[:, k % NB, :]), t)

    for k in range(TS + 5):
        advance(EACH)
        for lag, stage in ((5, third), (3, second), (1, first), (0, turn)):
            if 0 <= k - lag < TS:
                stage(k - lag)
    g_g = [group(f"g_g{k}") for k in range(4)]
    for i in range(NT):
        G.dma(g_g[i // 4], lambda e, i=i: e.indirect_dma_start(Yg[:, i, :], None, ys_d, bass.IndirectOffsetOnAxis(posu[:, i:i + 1], 0)),
              *g_st)
    advance(1000)
    ts = []
    for i in range(NT):
        t = V.free(lambda e, i=i: e.scalar_tensor_tensor(out=Y[:, i, :], in0=Yg[:, i, :], scalar=top[:, i:i + 1], in1=X0[:, i, :],
                                                    op0=ALU.mult, op1=ALU.add), g_g[i // 4], g_s)
        ts.append(stats(i, t))
    return ts[3::4], ring


def scan_weights(nc, ctx, sem, group, queues, banks, a, c, ident):
    PE, S, V, G, SP = queues
    ring = Banks(banks)

    def sb(name, shape, dt=F32):
        return ctx.enter_context(nc.sbuf_tensor(name, shape, dt))

    SC = sb("SC", [128, 304])
    Af = SC[:, 0:256].rearrange("p (g m) -> p g m", g=16)
    Bc, Cc, Dr = SC[:, 256:272], SC[:, 272:288], SC[:, 288:304]
    PA = [sb(f"PA{k}", [128, 16, 136]) for k in range(4)]
    PB = [sb(f"PB{k}", [128, 16, 136]) for k in range(2)]
    Uc = sb("Uc", [128, 16, 16])
    Vc = sb("Vc", [128, 16, 16])
    Vr = sb("Vr", [128, 16, 16])
    Hk = sb("Hk", [128, 31, 16])
    Tc = sb("Tc", [128, 16, 16])
    BX = sb("BX", [128, 16, 128])
    Win = sb("Win", [128, 16, 128])
    Wou = sb("Wou", [128, 16, 128])
    Wto = sb("Wto", [128, 16, 128])
    made = {"Win": Win, "Wou": Wou, "Wto": Wto, "ES": BX, "EL": PB[0][:, :, 0:128]}
    g_a, g_t = group("g_na"), group("g_nt")
    SP.dma(g_a, lambda e: e.dma_start(SC[:, :], a["packed"]))
    yield made

    def spread(eng, dst, src, *waits):
        return eng(lambda e: e.tensor_tensor(dst[:, :, 0:128].rearrange("p g (i d) -> p g i d", d=8),
                                             src[:, :, :].unsqueeze(3).to_broadcast([128, 16, 16, 8]),
                                             c("d8").unsqueeze(1).unsqueeze(1).to_broadcast([128, 16, 16, 8]), ALU.mult), *waits)

    def out_of(bk, dst, lo, hi, w, k, t):
        got = bk[:, 0:w * (hi - lo)].rearrange("p (g m) -> p g m", m=w)
        if k % 2:
            return S(lambda e: e.activation(dst[:, lo:hi, 0:128], got[:, :, 0:128], ACT.Copy), t)
        return V(lambda e: e.tensor_copy(dst[:, lo:hi, 0:128], got[:, :, 0:128]), t)

    def turn_all(dst, src, *waits):
        toks = []
        for k in range(4):
            n, bk, free = ring.take()
            for g in range(4 * k, 4 * k + 4):
                t = PE(lambda e, g=g, k=k, bk=bk: e.transpose(bk[:, 128 * (g - 4 * k):128 * (g - 4 * k) + 128], src[:, g, 0:128], ident),
                       *(waits + free))
            toks.append(out_of(bk, dst, 4 * k, 4 * k + 4, 128, k, t))
            ring.give(n, toks[-1])
            yield
        return tuple(toks[2:])

    def product(dst, lhs, rhs, *waits, m=0, cols=None):
        per, toks, at = (3 if m else 4), [], []
        for k, lo in enumerate(range(0, 16, per)):
            hi = min(lo + per, 16)
            n, bk, free = ring.take()
            for g in range(lo, hi):
                o = (128 + m) * (g - lo)
                t = PE(lambda e, g=g, o=o, bk=bk: e.matmul(bk[:, o:o + 128 + m], lhs[:, g, 0:128], rhs[:, g, 0:128 + m],
                                                           start=True, stop=True), *(waits + free))
            toks.append(out_of(bk, dst, lo, hi, 128 + m, k, t))
            free = toks[-1:]
            if m:
                got = bk[:, 0:(128 + m) * (hi - lo)].rearrange("p (g m) -> p g m", m=128 + m)[:, :, 128:]
                if k % 2:
                    t = S(lambda e, got=got, lo=lo, hi=hi: e.activation(cols[:, lo:hi, m:2 * m], got, ACT.Copy), t)
                else:
                    t = V(lambda e, got=got, lo=lo, hi=hi: e.tensor_copy(cols[:, lo:hi, m:2 * m], got), t)
                at.append(t)
                free = free + [t]
            ring.give(n, *free)
            yield
        return tuple(toks[-2:] + at[-2:])

    t = spread(V, PA[0], Af, g_a)
    pw = (yield from turn_all(PB[0], PA[0], t))
    pw = pw + (t,)
    n, bk, free = ring.take()
    for g in range(16):
        t = PE(lambda e, g=g: e.matmul(bk[:, g:g + 1], PB[0][:, g, 0:128], Cc[:, g:g + 1], start=True, stop=True), *(pw + free))
    t_u = V(lambda e: e.tensor_copy(Uc[:, :, 0:1], bk[:, 0:16].unsqueeze(2)), t)
    ring.give(n, t_u)
    t_v = G(lambda e: e.tensor_copy(Vc[:, :, 0:1].rearrange("p g o -> p (g o)"), Bc), g_a)
    yield
    cur_a, cur_b = PA[0], PB[0]
    nexta, nextb = [PA[1], PA[0], PA[1], PA[0]], [PB[1], PB[0], PB[1], PB[0]]
    for p in range(4):
        m = 2 ** p
        t_u = G(lambda e, m=m, cur_a=cur_a: e.tensor_copy(cur_a[:, :, 128:128 + m], Uc[:, :, 0:m]), t_u, *pw)
        t_v = G(lambda e, m=m, cur_b=cur_b: e.tensor_copy(cur_b[:, :, 128:128 + m], Vc[:, :, 0:m]), t_v, *pw)
        pa = (yield from product(nexta[p], cur_b, cur_a, t_v, *pw, m=m, cols=Uc))
        pb = (yield from product(nextb[p], cur_a, cur_b, *pw, m=m, cols=Vc))
        t_u, t_v = pa[2], pb[2]
        pw = pa + pb
        cur_a, cur_b = nexta[p], nextb[p]
    for k in range(16):
        t = G(lambda e, k=k: e.tensor_copy(Vr[:, :, 15 - k:16 - k], Vc[:, :, k:k + 1]), *pw)
    t = spread(V, BX, Vr, t)
    t_win = (yield from turn_all(Win, BX, t))
    t_wou = spread(V, Wou, Uc, *pw)
    t = V(lambda e: e.tensor_tensor(Vr[:, :, :], Vc[:, :, :], Cc.unsqueeze(2).to_broadcast([128, 16, 16]), ALU.mult), t)
    n, bk, free = ring.take()
    t = PE(lambda e, bk=bk: e.matmul(bk[:, 0:256], c("rep"), Vr[:, :, :].rearrange("p g k -> p (g k)"), start=True, stop=True), t, *free)
    t = V(lambda e, bk=bk: e.tensor_copy(Hk[:, 15:31, :], bk[:, 0:256].rearrange("p (g k) -> p k g", g=16)), t)
    ring.give(n, t)
    V(lambda e: e.tensor_scalar(Dr, Dr, 1.0, None, ALU.add), g_a)
    t = V(lambda e: e.tensor_tensor(Hk[:, 15, :], Hk[:, 15, :], Dr, ALU.add))
    t2 = G(lambda e: e.memset(Hk[:, 0:15, :], 0.0))
    for j in range(16):
        r = slice(8 * j, 8 * j + 8)
        S.dma(g_t, lambda e, j=j, r=r: e.dma_start(Tc[r, :, :], Hk[r, 15 - j:31 - j, :]), t, t2)
    yield
    power = [cur_a]
    for p in range(3):
        dst = [PA[1], PA[2], PA[3]][p]
        pa = (yield from product(dst, cur_b, cur_a, *pw))
        if p < 2:
            nb = PB[1] if cur_b is PB[0] else PB[0]
            pw = pw + pa + (yield from product(nb, cur_a, cur_b, *pw))
            cur_b = nb
        else:
            pw = pw + pa
        cur_a = dst
        power.append(dst)
    t_wto = spread(V, Wto, Tc[:, :, :].rearrange("p i g -> p g i"), g_t)
    yield
    made.update(ring=ring, power=power, t_win=t_win, t_wou=t_wou, t_wto=t_wto, pw=pw)


def scan(nc, ctx, sem, group, queues, ring, a, c, ident, X0, XT, Y, transposed, stats, normalise, made, x2):
    PE, S, V, G, SP = queues

    def sb(name, shape, dt=F32):
        return ctx.enter_context(nc.sbuf_tensor(name, shape, dt))

    Wg = sb("Wg", [128, 128])
    WgT = sb("WgT", [128, 128])
    bg = sb("bg", [128, 1])
    gam = sb("gam", [128, 128])
    bet = sb("bet", [128, 128])
    bgr = sb("bgr", [1, 512])
    ones = sb("ones0", [1, 128])
    GA = sb("GA", [128, NT, 128])
    U = sb("U", [128, 16, 128])
    XP = sb("XP", [128, NT, 128])
    Win, Wou, Wto, power = [made[k] for k in ("Win", "Wou", "Wto", "power")]
    t_win, t_wou, t_wto, pw = [made[k] for k in ("t_win", "t_wou", "t_wto", "pw")]
    ES, EL = made["ES"], made["EL"]
    g_w = group("g_nw")
    SP.dma(g_w, lambda e: e.dma_start(Wg[:, :], a["Wg"]))
    for k in range(4):
        SP.dma(g_w, lambda e, k=k: e.dma_start(bgr[:, 128 * k:128 * k + 128], a["bg"].rearrange("(o p) -> o p", o=1)))
    SP.dma(g_w, lambda e: e.dma_start(gam[:, :], a["gamma"].partition_broadcast(128)))
    SP.dma(g_w, lambda e: e.dma_start(bet[:, :], a["beta"].partition_broadcast(128)))
    t_one = G(lambda e: e.memset(ones[:, :], 1.0), g_w)
    t_zero = G(lambda e: e.memset(EL, 0.0), *pw)

    n, bk, free = ring.take()
    t = PE(lambda e, bk=bk: e.transpose(bk[:, 0:128], Wg[:, :], ident), g_w, *free)
    t_wg = V(lambda e, bk=bk: e.tensor_copy(WgT[:, :], bk[:, 0:128]), t)
    ring.give(n, t_wg)
    t_xt = tuple(transposed(ring, X0, p, normalise(X0, 4 * p, 4 * p + 4, x2[p])) for p in range(4))

    gated = []
    for p in range(4):
        n, bk, free = ring.take()
        for i in range(4):
            t = PE(lambda e, i=i, p=p, bk=bk: e.transpose(bk[:, 128 * i:128 * i + 128], XT[:, 4 * p + i:2048:16], ident),
                   *(t_xt + free))
        t_xp = V(lambda e, p=p, bk=bk: e.tensor_copy(XP[:, 4 * p:4 * p + 4, :], bk[:, :].rearrange("p (i d) -> p i d", i=4)), t)
        ring.give(n, t_xp)
        n, bk, free = ring.take()
        PE(lambda e, bk=bk: e.matmul(bk[:, :], ones[:, :], bgr[:, :], start=True, stop=False, skip_group_check=True), t_wg, t_one, *free)
        for i in range(4):
            t = PE(lambda e, i=i, p=p, bk=bk: e.matmul(bk[:, 128 * i:128 * i + 128], XT[:, 4 * p + i:2048:16], WgT[:, :], start=False,
                                                       stop=(i == 3), skip_group_check=True))
        t = S(lambda e, p=p, bk=bk: e.activation(GA[:, 4 * p:4 * p + 4, :], bk[:, :].rearrange("p (i d) -> p i d", i=4), ACT.Sigmoid), t)
        ring.give(n, t)
        gated.append(V(lambda e, p=p: e.tensor_tensor(GA[:, 4 * p:4 * p + 4, :], GA[:, 4 * p:4 * p + 4, :], XP[:, 4 * p:4 * p + 4, :],
                                                      ALU.mult), t))
    t_xp = G(lambda e: e.tensor_tensor(XP[:, :, :], XP[:, :, :], bet[:, :].unsqueeze(1).to_broadcast([128, NT, 128]), ALU.add), *gated, g_w)
    gav = GA[:, :, :].rearrange("p j (d g) -> p g (j d)", g=16)
    t_u = []
    for k in range(4):
        n, bk, free = ring.take()
        for g in range(4 * k, 4 * k + 4):
            t = PE(lambda e, g=g, k=k, bk=bk: e.transpose(bk[:, 128 * (g - 4 * k):128 * (g - 4 * k) + 128], gav[:, g, :], ident),
                   *(tuple(gated) + free))
        dst, src = U[:, 4 * k:4 * k + 4, :], bk[:, :].rearrange("p (g q) -> p g q", g=4)
        if k % 2:
            t = S(lambda e, dst=dst, src=src: e.activation(dst, src, ACT.Copy), t)
        else:
            t = V(lambda e, dst=dst, src=src: e.tensor_copy(dst, src), t)
        ring.give(n, t)
        t_u.append(t)

    got = {}
    taken = []
    for k in range(4):
        n, bk, free = ring.take()
        taken.append((n, bk))
        for g in range(4 * k, 4 * k + 4):
            t = PE(lambda e, g=g, k=k, bk=bk: e.matmul(bk[:, 128 * (g - 4 * k):128 * (g - 4 * k) + 128], Win[:, g, :], U[:, g, :],
                                                       start=(g == 4 * k), stop=False, skip_group_check=True),
                   *(t_win + (t_u[k],) + free))
        got[k] = t

    def state_out(k):
        n, bk = taken[k]
        dst, src = ES[:, 4 * k:4 * k + 4, :], bk[:, :].rearrange("p (g q) -> p g q", g=4)
        if k % 2:
            return S(lambda e: e.activation(dst, src, ACT.Copy), got[k], *t_win)
        return V(lambda e: e.tensor_copy(dst, src), got[k], *t_win)

    for p in range(4):
        s = 2 ** p
        outs = [state_out(k) for k in range(4)]
        for k in range(4):
            n, bk = taken[k]
            for g in range(4 * k, 4 * k + 4):
                w = slice(128 * (g - 4 * k), 128 * (g - 4 * k) + 128)
                t = PE(lambda e, g=g, w=w, p=p, s=s, bk=bk: e.matmul(
                    bk[:, w].rearrange("p (b q) -> p b q", b=8)[:, :, s:16], power[p][:, g, 0:128],
                    ES[:, g, :].rearrange("p (b q) -> p b q", b=8)[:, :, 0:16 - s], start=False, stop=(p == 3),
                    skip_group_check=True), outs[k], *pw)
            got[k] = t
    last = []
    for k in range(4):
        n, bk = taken[k]
        dst = EL[:, 4 * k:4 * k + 4, :].rearrange("p g (b q) -> p g b q", b=8)[:, :, :, 1:16]
        src = bk[:, :].rearrange("p (g b q) -> p g b q", g=4, b=8)[:, :, :, 0:15]
        if k % 2:
            t = S(lambda e, dst=dst, src=src: e.activation(dst, src, ACT.Copy), got[k], t_zero)
        else:
            t = V(lambda e, dst=dst, src=src: e.tensor_copy(dst, src), got[k], t_zero)
        ring.give(n, t)
        last.append(t)
    yv = Y[:, :, :].rearrange("p i (d g) -> p g i d", g=16)
    ys = []
    for k in range(4):
        n, bk, free = ring.take()
        for g in range(4 * k, 4 * k + 4):
            w = slice(128 * (g - 4 * k), 128 * (g - 4 * k) + 128)
            PE(lambda e, g=g, w=w, bk=bk: e.matmul(bk[:, w], U[:, g, :], Wto[:, g, :], start=True, stop=False), t_wto, *free)
            t = PE(lambda e, g=g, w=w, bk=bk: e.matmul(bk[:, w], EL[:, g, :], Wou[:, g, :], start=False, stop=True), t_wou, last[k])
        for x in range(4):
            dst, src = yv[:, 4 * k + x, :, :], bk[:, 128 * x:128 * x + 128].rearrange("p (i d) -> p i d", d=8)
            if k % 2:
                t2 = S(lambda e, dst=dst, src=src: e.activation(dst, src, ACT.Copy), t)
            else:
                t2 = V(lambda e, dst=dst, src=src: e.tensor_copy(dst, src), t)
        ring.give(n, t2)
        ys.append(t2)
    return ring, ys, gam, XP, t_xp



def mixture_weights(ctx, nc, group, SP, a):
    def sb(name, shape, dt=F32):
        return ctx.enter_context(nc.sbuf_tensor(name, shape, dt))

    w = {"Wen": sb("Wen", [128, 256]), "ben": sb("ben", [128, 2]), "Wsc": sb("Wsc", [128, 2, 2, 64]), "bsc": sb("bsc", [128, 1]),
         "Wr1": sb("Wr1", [64, 64]), "br1": sb("br1", [64, 1]), "Wr2": sb("Wr2", [64, 8]), "br2": sb("br2", [8, 1]),
         "We1": sb("We1", [128, 4, 128]), "be1": sb("be1", [128, 8]), "We2": sb("We2", [128, 8, 64]), "be2": sb("be2", [128, 64]),
         "Wcs": sb("Wcs", [128, 128]), "bcs": sb("bcs", [128, 2]), "Wde": sb("Wde", [128, 2, 128]), "bde": sb("bde", [128, 128]),
         "gam": sb("lng", [128, 128]), "bet": sb("lnb", [128, 128])}
    g = group("g_m")

    def load(dst, src):
        SP.dma(g, lambda e: e.dma_start(dst, src))

    def col(s):
        return s.rearrange("(p o) -> p o", o=1)

    def load_all():
        load(w["Wen"][:, :], a["enc_W"])
        load(w["ben"][:, :], a["enc_b"])
        for k in range(2):
            load(w["Wsc"][:, :, k, :], a["s2c_W"].rearrange("(k p) m -> p k m", p=128))
            load(w["bsc"][64 * k:64 * k + 64, :], col(a["s2c_b"]))
            load(w["We1"][64 * k:64 * k + 64, :, :], a["We1"].rearrange("(x k) m h -> k m x h", k=2)[k])
            load(w["Wcs"][64 * k:64 * k + 64, :], a["c2s_W"][:, 128 * k:128 * k + 128])
        load(w["Wr1"][:, :], a["rW1"])
        load(w["br1"][:, :], col(a["rb1"]))
        load(w["Wr2"][:, :], a["rW2"])
        load(w["br2"][:, :], col(a["rb2"]))
        load(w["be1"][:, :], a["be1"])
        load(w["We2"][:, :, :], a["We2"].rearrange("e h m -> h e m"))
        load(w["be2"][:, :], a["be2"])
        load(w["bcs"][:, :], a["c2s_b"])
        load(w["Wde"][:, :, :], a["dec_W"].rearrange("(k p) d -> p k d", p=128))
        load(w["bde"][:, :], a["dec_b"].partition_broadcast(128))
        load(w["gam"][:, :], a["ln_g"].partition_broadcast(128))
        load(w["bet"][:, :], a["ln_b"].partition_broadcast(128))

    return w, g, load_all


def mixture(nc, ctx, queues, ring, w, g_w, c, ident, X0, XT, Y, transposed, x3):
    PE, S, V, G, SP = queues
    E = 8

    def sb(name, shape, dt=F32):
        return ctx.enter_context(nc.sbuf_tensor(name, shape, dt))

    Wen, ben, Wsc, bsc, Wr1, br1, Wr2, br2, We1, be1, We2, be2, Wcs, bcs, Wde, bde, gam, bet = [w[k] for k in (
        "Wen", "ben", "Wsc", "bsc", "Wr1", "br1", "Wr2", "br2", "We1", "be1", "We2", "be2", "Wcs", "bcs", "Wde", "bde", "gam", "bet")]
    EN = sb("EN", [128, 2, 2, 512])
    CT = sb("CT", [128, 2048])
    T1 = sb("T1", [64, 2, 512])
    LT = sb("LT", [8, 2, 512])
    LG = sb("LG", [128, NT, E])
    lm = sb("lm", [128, NT])
    ls = sb("ls", [128, NT])
    rest = sb("rest2", [128, E])
    top = sb("top2", [128, NT, 2])
    eq = sb("eq2", [128, NT, E])
    h1 = sb("h1", [128, NT, E])
    h2 = sb("h2", [128, NT, E])
    gtT = sb("gtT", [128, 128])
    BD = sb("BD", [128, NT, 2, 64])
    HE = sb("HE", [128, 2, E, 512])
    PR = sb("PR", [128, 2, 512])
    OF = sb("OF", [128, NT, 2, 64])
    OT = sb("OT", [128, 2, 512])
    SM = sb("SM", [128, 2, 2, 512])
    XB = sb("XB", [128, NT, 128])
    x = {}

    def wide(s, k=E):
        return s.unsqueeze(2).to_broadcast([128, NT, k])

    def over(s):
        return s.unsqueeze(1).to_broadcast([128, NT, E])

    for k in range(2):
        t_bd = G(lambda e, k=k: e.tensor_tensor(BD[:, :, k, :], be2[:, :].unsqueeze(1).to_broadcast([128, NT, 64]),
                                                c("d16").unsqueeze(2).to_broadcast([128, NT, 64]), ALU.mult), g_w)

    def encode(p):
        xs = slice(512 * p, 512 * p + 512)
        t_x = transposed(ring, X0, p, x3(p))
        for k in range(2):
            n, bk, free = ring.take()
            t = PE(lambda e, k=k, bk=bk: e.matmul(bk[:, :], Wen[:, 128 * k:128 * k + 128], XT[:, xs], start=True, stop=True),
                   t_x, g_w, *free)
            t = S(lambda e, k=k, bk=bk: e.activation(EN[:, p % 2, k, :], bk[:, :], ACT.Sigmoid, bias=ben[:, k:k + 1]), t,
                  *x.get(("sc", p - 2), ()))
            ring.give(n, t)
            x["en", p, k] = t

    def compress(p):
        xs = slice(512 * p, 512 * p + 512)
        n, bk, free = ring.take()
        for k in range(2):
            t = PE(lambda e, k=k: e.matmul(bk[:, :], Wsc[:, k, :, :].rearrange("p a m -> p (a m)"), EN[:, p % 2, k, :], start=(k == 0),
                                           stop=(k == 1)), x["en", p, k], *free)
        x["sc", p] = (t,)
        x["ct", p] = t = V(lambda e: e.tensor_scalar(CT[:, xs], bk[:, :], bsc[:, :], None, ALU.add), t)
        ring.give(n, t)

    def router(p):
        xs = slice(512 * p, 512 * p + 512)
        n, bk, free = ring.take()
        t = PE(lambda e: e.matmul(bk[0:64, :], Wr1[:, :], CT[0:64, xs], start=True, stop=True), x["ct", p], *free)
        t = S(lambda e: e.activation(T1[:, p % 2, :], bk[0:64, :], ACT.Tanh, bias=br1[:, :]), t, *x.get(("t1", p - 2), ()))
        ring.give(n, t)
        x["t", p] = t

    def logits(p):
        n, bk, free = ring.take()
        t = PE(lambda e: e.matmul(bk[0:8, :], Wr2[:, :], T1[:, p % 2, :], start=True, stop=True), x["t", p], *free)
        x["t1", p] = (t,)
        t = V(lambda e: e.tensor_scalar(LT[:, p % 2, :], bk[0:8, :], br2[:, :], None, ALU.add), t, *x.get(("lt", p - 2), ()))
        ring.give(n, t)
        x["l", p] = t

    def logits_turned(p):
        n, bk, free = ring.take()
        for i in range(4):
            t = PE(lambda e, i=i: e.transpose(bk[:, 8 * i:8 * i + 8], LT[:, p % 2, 128 * i:128 * i + 128], ident[0:8, 0:8]),
                   x["l", p], *free)
        x["lt", p] = (t,)
        x["lg"] = V(lambda e: e.tensor_copy(LG[:, 4 * p:4 * p + 4, :], bk[:, 0:32].rearrange("p (i e) -> p i e", e=E)), t)
        ring.give(n, x["lg"])

    def gates():
        V(lambda e: e.tensor_reduce(lm[:, :], LG[:, :, :], AX, ALU.max))
        t = V(lambda e: e.tensor_tensor(LG[:, :, :], LG[:, :, :], wide(lm[:, :]), ALU.subtract))
        t = S(lambda e: e.activation(LG[:, :, :], LG[:, :, :], ACT.Exp), t)
        V(lambda e: e.tensor_scalar(rest[:, :], c("iota8"), float(E), None, ALU.subtract))
        V(lambda e: e.tensor_reduce(ls[:, :], LG[:, :, :], AX, ALU.add), t)
        V(lambda e: e.reciprocal(ls[:, :], ls[:, :]))
        V(lambda e: e.tensor_tensor(LG[:, :, :], LG[:, :, :], wide(ls[:, :]), ALU.mult))
        for k, hot in enumerate((h1, h2)):
            V(lambda e, k=k: e.tensor_reduce(top[:, :, k], LG[:, :, :], AX, ALU.max))
            V(lambda e, k=k: e.tensor_tensor(eq[:, :, :], LG[:, :, :], wide(top[:, :, k]), ALU.is_equal))
            V(lambda e: e.tensor_tensor(eq[:, :, :], eq[:, :, :], over(rest[:, :]), ALU.mult))
            V(lambda e: e.tensor_reduce(lm[:, :], eq[:, :, :], AX, ALU.min))
            V(lambda e, hot=hot: e.tensor_tensor(hot[:, :, :], over(rest[:, :]), wide(lm[:, :]), ALU.is_equal))
            if k == 0:
                V(lambda e: e.scalar_tensor_tensor(out=LG[:, :, :], in0=h1[:, :, :], scalar=-4.0, in1=LG[:, :, :], op0=ALU.mult,
                                                   op1=ALU.add))
        V(lambda e: e.tensor_tensor(ls[:, :], top[:, :, 0], top[:, :, 1], ALU.add))
        V(lambda e: e.reciprocal(ls[:, :], ls[:, :]))
        V(lambda e: e.tensor_tensor(top[:, :, :], top[:, :, :], wide(ls[:, :], 2), ALU.mult))
        for k, hot in enumerate((h1, h2)):
            V(lambda e, k=k, hot=hot: e.tensor_tensor(hot[:, :, :], hot[:, :, :], wide(top[:, :, k]), ALU.mult))
        x["gt"] = V(lambda e: e.tensor_tensor(h1[:, :, :], h1[:, :, :], h2[:, :, :], ALU.add))

    def gates_turned():
        n, bk, free = ring.take()
        t = PE(lambda e: e.transpose(bk[:, 0:128], h1[:, :, :].rearrange("p i e -> p (i e)"), ident), x["gt"], *free)
        x["gtT"] = S(lambda e: e.activation(gtT[:, :], bk[:, 0:128], ACT.Copy), t)
        ring.give(n, x["gtT"])

    def hidden(p):
        xs = slice(512 * p, 512 * p + 512)
        for k in range(0, E, 2):
            two = [ring.take(), ring.take()]
            for f, (n, bk, free) in enumerate(two):
                r = slice(64 * f, 64 * f + 64)
                t = PE(lambda e, k=k, r=r, bk=bk: e.matmul(bk[:, :], We1[r, k // 2, :], CT[r, xs], start=True, stop=True),
                       x["ct", p], *free)
                o = k + f
                if f or p == 0:
                    t = S(lambda e, o=o, bk=bk: e.activation(HE[:, p % 2, o, :], bk[:, :], ACT.Relu, bias=be1[:, o:o + 1]), t,
                          *x.get(("we2", p - 2), ()))
                else:
                    t = V.free(lambda e, o=o, bk=bk: e.tensor_scalar(HE[:, p % 2, o, :], bk[:, :], be1[:, o:o + 1], 0.0, ALU.add, ALU.max),
                               t, *x.get(("we2", p - 2), ()))
                ring.give(n, t)
                x["he", p, o] = t

    def expert(p):
        for i in range(4 * p, 4 * p + 4):
            n, bk, free = ring.take()
            o = 128 * (i - 4 * p)
            for k in range(E):
                t = PE(lambda e, k=k, o=o, bk=bk: e.matmul(bk[:, 64 * k:64 * k + 64], HE[:, p % 2, k, o:o + 128], We2[:, k, :], start=True,
                                                           stop=True), x["he", p, k], *free)
            t = V.free(lambda e, i=i, bk=bk: e.tensor_tensor(PR[:, i % 2, :].rearrange("p (e m) -> p e m", e=E),
                                                             bk[:, :].rearrange("p (e m) -> p e m", e=E),
                                                             h1[:, i, :].unsqueeze(2).to_broadcast([128, E, 64]), ALU.mult), t, x["gt"],
                       *x.get(("of", i - 2), ()))
            ring.give(n, t)
            t2 = V.free(lambda e, i=i: e.tensor_reduce(OF[:, i, 0, :], PR[:, i % 2, :].rearrange("p (e m) -> p m e", e=E), AX, ALU.add), t)
            x["of", i] = (t2,)
            x["of2", p] = G(lambda e, i=i: e.tensor_copy(OF[:, i, 1, :], OF[:, i, 0, :]), t2)
        x["we2", p] = (t,)

    def mixed(p):
        n, bk, free = ring.take()
        for i in range(4 * p, 4 * p + 4):
            o = 128 * (i - 4 * p)
            PE(lambda e, i=i, o=o: e.matmul(bk[:, o:o + 128], OF[:, i, :, :].rearrange("p a m -> p (a m)"), ident, start=True, stop=False),
               x["of2", p], *free)
            t = PE(lambda e, i=i, o=o: e.matmul(bk[:, o:o + 128], BD[:, i, :, :].rearrange("p a m -> p (a m)"), gtT[:, :], start=False,
                                                stop=True), x["gtT"], t_bd)
        x["ot", p] = S(lambda e: e.activation(OT[:, p % 2, :], bk[:, :], ACT.Copy), t, *x.get(("cs", p - 2), ()))
        ring.give(n, x["ot", p])

    def spikes(p):
        two = [ring.take(), ring.take()]
        for k, (n, bk, free) in enumerate(two):
            r = slice(64 * k, 64 * k + 64)
            t = PE(lambda e, r=r, bk=bk: e.matmul(bk[:, :], Wcs[r, :], OT[r, p % 2, :], start=True, stop=True), x["ot", p], *free)
            x["cs", p] = (t,)
            t = S(lambda e, k=k, bk=bk: e.activation(SM[:, p % 2, k, :], bk[:, :], ACT.Sigmoid, bias=bcs[:, k:k + 1]), t,
                  *x.get(("de", p - 2), ()))
            ring.give(n, t)
            x["sm", p, k] = t

    def decode(p):
        n, bk, free = ring.take()
        for i in range(4):
            o = slice(128 * i, 128 * i + 128)
            for k in range(2):
                t = PE(lambda e, k=k, o=o: e.matmul(bk[:, o], SM[:, p % 2, k, o], Wde[:, k, :], start=(k == 0), stop=(k == 1)),
                       x["sm", p, 0], x["sm", p, 1], *free)
        x["de", p] = (t,)
        yp = Y[:, 4 * p:4 * p + 4, :]
        t = V.free(lambda e: e.tensor_tensor(yp, bk[:, :].rearrange("p (i d) -> p i d", i=4),
                                             bde[:, :].unsqueeze(1).to_broadcast([128, 4, 128]), ALU.add), t)
        ring.give(n, t)
        x["y", p] = S(lambda e: e.activation(yp, yp, ACT.Sigmoid), t)

    for s in range(4 + 4):
        for lag, stage in ((0, encode), (1, compress), (2, router), (3, logits), (4, logits_turned)):
            if 0 <= s - lag < 4:
                stage(s - lag)
    t_xb = G(lambda e: e.tensor_tensor(XB[:, :, :], X0[:, :, :], bet[:, :].unsqueeze(1).to_broadcast([128, NT, 128]), ALU.add),
             x["lg"])
    gates()
    for s in range(4 + 4):
        for lag, stage in ((0, hidden), (1, expert), (2, mixed), (3, spikes), (4, decode)):
            if 0 <= s - lag < 4:
                if stage is mixed and s == 2:
                    gates_turned()
                stage(s - lag)
    return [x["y", p] for p in range(4)], gam, XB, t_xb


def program(nc, x, a, f0, a1, f1, const, out):
    with ExitStack() as ctx:
        def sb(name, shape, dt=F32):
            return ctx.enter_context(nc.sbuf_tensor(name, shape, dt))

        def sem(name):
            return ctx.enter_context(nc.semaphore(name))

        def group(name):
            return Group(sem(name))

        PE, S, V, G, SP = [Queue(sem(n), n in ("s_act", "s_dve", "s_pool"))
                           for n in ("s_pe", "s_act", "s_dve", "s_pool", "s_sp")]
        bank = [ctx.enter_context(nc.psum_tensor(f"bank{i}", [128, 512], F32)) for i in range(8)]

        C = sb("C", [128, CONST.shape[1]])

        def c(name, rows=slice(0, 128)):
            return C[rows, CAT[name][0]:CAT[name][1]]

        ident = c("ident")
        X0 = sb("X0", [128, NT, D])
        Y = sb("Y", [128, NT, D])
        XT = sb("XT", [128, NT * 128])
        st6 = sb("st6", [128, 2 * NT, 6])
        mv = sb("mv", [128, 2 * NT, 2])
        rstd = sb("rstd", [128, 2 * NT])
        shift = sb("shift", [128, NT])

        g_c = [group(f"g_c{i}") for i in range(2)]
        g_x0, g_x = group("g_xtok"), [group(f"g_x{i}") for i in range(4)]
        def transposed(ring, src, p, *waits):
            n, bk, free = ring.take()
            for i in range(4):
                t = PE(lambda e, i=i: e.transpose(bk[:, i * 128:i * 128 + 128], src[:, 4 * p + i, :], ident),
                       *((free + waits) if i == 0 else ()))
            t = S(lambda e: e.activation(XT[:, p * 512:p * 512 + 512], bk[:, :], ACT.Copy), t)
            ring.give(n, t)
            return t

        def stats(i, *waits, k=0):
            x = NT * k + i
            t = V.free(lambda e: e.bn_stats(st6[:, x, :], Y[:, i, :]), *waits)
            return V.free(lambda e: e.bn_aggr(mv[:, x, :], st6[:, x, :]), t)

        def spread_of(lo, hi, k, *waits):
            lo, hi = lo + NT * k, hi + NT * k
            t = S(lambda e: e.activation(rstd[:, lo:hi], mv[:, lo:hi, 1], ACT.Sqrt, bias=c("eps")), *waits)
            return V.free(lambda e: e.reciprocal(rstd[:, lo:hi], rstd[:, lo:hi]), t)

        def normalise(dst, lo, hi, *waits, k=0):
            r = spread_of(lo, hi, k, *waits)
            for i in range(lo, hi):
                x = NT * k + i
                t = V.free(lambda e, i=i, x=x: e.tensor_scalar(dst[:, i, :], Y[:, i, :], mv[:, x, 0:1], rstd[:, x:x + 1],
                                                               ALU.subtract, ALU.mult), r)
            return t

        def twice_normalised(waits, gam, XP, t_xp, after):
            t = {}

            def first(p):
                for i in range(4 * p, 4 * p + 4):
                    t["s"] = stats(i, *waits[p])
                r = spread_of(4 * p, 4 * p + 4, 0, t["s"])
                t["r", p] = V.free(lambda e: e.scalar_tensor_tensor(out=shift[:, 4 * p:4 * p + 4], in0=mv[:, 4 * p:4 * p + 4, 0], scalar=-1.0,
                                                                    in1=rstd[:, 4 * p:4 * p + 4], op0=ALU.mult, op1=ALU.mult), r)

            def second(p):
                for i in range(4 * p, 4 * p + 4):
                    x = S.free(lambda e, i=i: e.activation(Y[:, i, :], Y[:, i, :], ACT.Identity, scale=rstd[:, i:i + 1], bias=shift[:, i:i + 1]),
                               t["r", p])
                yp = Y[:, 4 * p:4 * p + 4, :]
                t["g", p] = G(lambda e: e.tensor_tensor(yp, yp, gam[:, :].unsqueeze(1).to_broadcast([128, 4, 128]), ALU.mult), x)

            def third(p):
                yp = Y[:, 4 * p:4 * p + 4, :]
                x = V.free(lambda e: e.tensor_tensor(yp, yp, XP[:, 4 * p:4 * p + 4, :], ALU.add), t["g", p], t_xp)
                for i in range(4 * p, 4 * p + 4):
                    t["z", p] = stats(i, x, k=1)

            def fourth(p):
                after(p, normalise(X0, 4 * p, 4 * p + 4, t["z", p], k=1))

            for s in range(4 + 3):
                for lag, stage in ((0, first), (1, second), (2, third), (3, fourth)):
                    if 0 <= s - lag < 4:
                        stage(s - lag)

        def fence():
            ends = [q.items[-1][2] for q in (PE, S, V, G)]
            for q in (PE, S, V, G, SP):
                q.hold(*ends)

        masks = CAT["mask0"][0]

        def load_x(part):
            for p in [0] if part == 0 else [1, 2, 3]:
                SP.dma(g_x[p], lambda e, p=p: e.dma_start(XT[:, 512 * p:512 * p + 512], a["xT"][:, 512 * p:512 * p + 512]))
                if p == 0:
                    SP.dma(g_c[0], lambda e: e.dma_start(C[:, 0:masks], const[:, 0:masks]))
                if p == 1:
                    SP.dma(g_c[1], lambda e: e.dma_start(C[:, masks:], const[:, masks:]))
            if part:
                load_router()
                SP.dma(g_x0, lambda e: e.dma_start(X0[:, :, :], x.rearrange("b (h p) d -> p (b h) d", p=128)))

        Wr, br, turned, zero = sb("Wr", [128, 8]), sb("br", [8, 1]), sb("turned", [8, 512]), sb("zero", [128, 512])
        logit = sb("logit", [128, NT, 8])
        g_r, g_z = group("g_fr"), group("g_fz")
        xs_d = nc.dram_tensor("xs_d", [TILES * 128, 128], F32, kind="Internal").ap()
        t_z = G(lambda e: e.memset(zero[:, :], 0.0))

        def load_router():
            SP.dma(g_r, lambda e: e.dma_start(Wr[:, :], f0["Wr"]))
            SP.dma(g_r, lambda e: e.dma_start(br[:, :], f0["br"].rearrange("(n o) -> n o", o=1)))
            zv = xs_d.rearrange("(p r) d -> p (r d)", p=128)
            for k in range(0, TILES * 128, 512):
                w = min(512, TILES * 128 - k)
                SP.dma(g_z, lambda e, k=k, w=w: e.dma_start(zv[:, k:k + w], zero[:, 0:w]), t_z)

        done = {}

        def after_attention(ring, p, t):
            t = normalise(X0, 4 * p, 4 * p + 4, t)
            yield
            yield
            t_x = transposed(ring, X0, p, t)
            yield
            n, bk, free = ring.take()
            t = PE(lambda e: e.matmul(bk[0:8, :], Wr[:, :], XT[:, 512 * p:512 * p + 512], start=True, stop=True), t_x, g_r, *free)
            t = V.free(lambda e: e.tensor_scalar(turned[:, :], bk[0:8, :], br[:, :], None, ALU.add), t, *done.get("turned", ()))
            ring.give(n, t)
            yield
            n, bk2, free = ring.take()
            for i in range(4):
                t = PE(lambda e, i=i: e.transpose(bk2[:, 8 * i:8 * i + 8], turned[:, 128 * i:128 * i + 128], ident[0:8, 0:8]), t, *free)
            done["turned"] = (t,)
            done["logit"] = V(lambda e: e.tensor_copy(logit[:, 4 * p:4 * p + 4, :], bk2[:, 0:32].rearrange("p (i e) -> p i e", e=8)), t)
            ring.give(n, done["logit"])

        with ExitStack() as part:
            ring = attention(nc, part, sem, group, (PE, S, V, G, SP), bank, a, c, ident, X0, XT, Y, g_c, g_x0, g_x, stats, load_x,
                             after_attention)
        fence()
        everything = (PE, S, V, G, SP)
        w1, g_w1, load_mixture = mixture_weights(ctx, nc, group, SP, f1)
        with ExitStack() as both:
            pieces = scan_weights(nc, both, sem, group, everything, bank[5:8], a1, c, ident)
            made = next(pieces)
            with ExitStack() as part:
                x2, ring = experts(nc, part, sem, group, everything, bank[0:5], f0, c, ident, X0, Y, xs_d, logit, g_z,
                                   done["logit"], stats, pieces)
            ring = ring.join(made["ring"])
            load_mixture()
            with ExitStack() as part:
                ring, ys, gam, XP, t_xp = scan(nc, part, sem, group, everything, ring, a1, c, ident, X0, XT, Y, transposed, stats,
                                               normalise, made, x2)
            x3 = {}
            twice_normalised([ys] * 4, gam, XP, t_xp, x3.__setitem__)
            fence()
        with ExitStack() as part:
            ys, gam, XB, t_xb = mixture(nc, part, everything, ring, w1, g_w1, c, ident, X0, XT, Y, transposed, x3.get)
            g_out = group("g_out")
            ov = out.rearrange("b (q i) d -> (b q) i d", i=16)

            def store(p, t):
                SP.dma(g_out, lambda e: e.dma_start(ov[:, 4 * p:4 * p + 4, :], X0[:, 4 * p:4 * p + 4, :]), t)

            twice_normalised([[y] for y in ys], gam, XB, t_xb, store)
        SP.hold(g_out)

        queues = (PE, S, V, G, SP)
        for q in queues:
            q.count()
        block = ctx.enter_context(nc.Block())

        @block.tensor
        def _(eng):
            PE.write(eng)

        @block.scalar
        def _(eng):
            S.write(eng)

        @block.vector
        def _(eng):
            V.write(eng)

        @block.gpsimd
        def _(eng):
            G.write(eng)

        @block.sync
        def _(eng):
            SP.write(eng)


NAMES = ['L0_attn_x', 'L0_attn_W_dkv', 'L0_attn_W_uk', 'L0_attn_W_uv', 'L0_attn_W_dq', 'L0_attn_W_uq', 'L0_attn_W_qr', 'L0_attn_W_kr', 'L0_attn_W_out', 'L0_attn_idx_wq', 'L0_attn_idx_wk', 'L0_attn_idx_w', 'L0_attn_raw_delta', 'L0_ffn_Wr', 'L0_ffn_br', 'L0_ffn_W1', 'L0_ffn_W2', 'L1_attn_A', 'L1_attn_Bp', 'L1_attn_Cp', 'L1_attn_Dp', 'L1_attn_Wg', 'L1_attn_bg', 'L1_attn_gamma', 'L1_attn_beta', 'L1_ffn_enc_W', 'L1_ffn_enc_b', 'L1_ffn_s2c_W', 'L1_ffn_s2c_b', 'L1_ffn_rW1', 'L1_ffn_rb1', 'L1_ffn_rW2', 'L1_ffn_rb2', 'L1_ffn_We1', 'L1_ffn_be1', 'L1_ffn_We2', 'L1_ffn_be2', 'L1_ffn_c2s_W', 'L1_ffn_c2s_b', 'L1_ffn_dec_W', 'L1_ffn_dec_b', 'L1_ffn_ln_g', 'L1_ffn_ln_b']


def kernel(**inputs):
    import concourse.bacc as bacc
    from concourse.bass_utils import run_bass_kernel_spmd

    nc = bacc.Bacc("TRN2", target_bir_lowering=False, num_devices=1)
    arrays, aps = {}, {}
    for name in NAMES:
        v = np.ascontiguousarray(inputs[name])
        arrays[name] = v
        aps[name] = nc.dram_tensor(name, v.shape, mybir.dt.from_np(v.dtype), kind="ExternalInput").ap()
    arrays["shape_constants"] = CONST
    const = nc.dram_tensor("shape_constants", CONST.shape, F32, kind="ExternalInput").ap()
    out = nc.dram_tensor("result", (B, L, D), F32, kind="ExternalOutput").ap()

    def part(prefix):
        return {n[len(prefix):]: aps[n] for n in NAMES if n.startswith(prefix)}

    def lay(name, v):
        arrays[name] = v = np.ascontiguousarray(v)
        return nc.dram_tensor(name, v.shape, F32, kind="ExternalInput").ap()

    def by_state(v):
        v = v.reshape((8, 16) + v.shape[1:])
        return v.transpose((2, 0, 1) + tuple(range(3, v.ndim))).reshape(128, -1)

    def block(v, k):
        return v.reshape(k, 128, -1).transpose(1, 0, 2).reshape(128, -1)

    a0 = {n[8:]: np.asarray(inputs[n]) for n in NAMES if n.startswith("L0_attn_")}
    heads = {"Wp": np.concatenate([a0["W_dq"], a0["W_dkv"], a0["W_kr"]], 1),
             "Wi": np.concatenate([a0["idx_wk"], a0["idx_wk"], a0["idx_wq"]], 1),
             "WuqT": block(a0["W_uq"].T, 4), "WukT": block(a0["W_uk"].T, 4), "WuvT": block(a0["W_uv"].T, 4),
             "Wout": block(a0["W_out"], 4),
             "Wq2": np.pad(a0["W_qr"], ((0, 64), (256, 0))),
             "wix": np.broadcast_to(a0["idx_w"], (128, 4)),
             "rd": np.concatenate([np.broadcast_to(a0["raw_delta"], (128, 16)), np.tile(a0["raw_delta"], 8)[:, None]], 1)}
    at0 = {"packed": lay("attention_packed", np.concatenate([heads[n] for n, _ in PACK], 1)),
           "xT": lay("x_features", a0["x"].reshape(B * L, D).T)}
    a1, f1 = part("L1_attn_"), part("L1_ffn_")
    skip = np.broadcast_to(np.asarray(inputs["L1_attn_Dp"])[:, None], (128, 16))
    a1["packed"] = lay("scan_packed", np.concatenate(
        [by_state(np.asarray(inputs[f"L1_attn_{k}"])) for k in ("A", "Bp", "Cp")] + [by_state(skip)], 1))
    for k in ("enc_b", "c2s_b"):
        f1[k] = lay(f"{k}_columns", np.asarray(inputs[f"L1_ffn_{k}"]).reshape(2, 128).T)
    f1["be2"] = lay("be2_rows", np.tile(np.asarray(inputs["L1_ffn_be2"]), (16, 1)))
    f1["be1"] = lay("be1_columns", np.asarray(inputs["L1_ffn_be1"]).T)
    program(nc, aps["L0_attn_x"], at0, part("L0_ffn_"), a1, f1, const, out)
    r = run_bass_kernel_spmd(nc, [arrays], core_ids=[0])
    return r.results[0]["result"]
```

```python
from contextlib import ExitStack

import numpy as np
import concourse.bass as bass
from concourse import mybir

F32 = mybir.dt.float32
BF16 = mybir.dt.bfloat16
U32 = mybir.dt.uint32
I32 = mybir.dt.int32
ALU = mybir.AluOpType
ACT = mybir.ActivationFunctionType
AX = mybir.AxisListType.X

B, L, D = 8, 256, 128
NT = B * L // 128
NH = 8
TILES = NT + 7
SCALE = 96.0 ** -0.5
BIG = 1.0e30
LOW = -3.0e38


class Tok:

    def __init__(self, queue):
        self.queue, self.used, self.value = queue, False, 0

    def target(self):
        return self.queue.sem, self.value


class Group:

    def __init__(self, sem):
        self.sem, self.count, self.used = sem, 0, False

    def target(self):
        return self.sem, 16 * self.count


class Queue:

    def __init__(self, sem, chained):
        self.sem, self.items, self.chained, self.last = sem, [], chained, None

    def __call__(self, fn, *waits):
        tok = Tok(self)
        if self.chained:
            waits += (self.last,) if self.last else ()
            self.last = tok
        for w in waits:
            w.used = True
        self.items.append((waits, fn, tok))
        return tok

    def free(self, fn, *waits):
        tok = Tok(self)
        if self.chained:
            self.last = tok
        for w in waits:
            w.used = True
        self.items.append((waits, fn, tok))
        return tok

    def dma(self, group, fn, *waits):
        for w in waits:
            w.used = True
        group.count += 1
        self.items.append((waits, fn, group))
        return group

    def hold(self, *waits):
        for w in waits:
            w.used = True
        self.items.append((waits, None, None))

    def count(self):
        n = 0
        for _, _, tok in self.items:
            if isinstance(tok, Tok) and tok.used:
                n += 1
                tok.value = n

    def write(self, eng):
        reached = {}
        for waits, fn, tok in self.items:
            for w in waits:
                sem, value = w.target()
                if reached.get(id(sem), 0) < value:
                    eng.wait_ge(sem, value)
                    reached[id(sem)] = value
            if fn is None:
                continue
            ins = fn(eng)
            if isinstance(tok, Group):
                ins.then_inc(tok.sem, 16)
            elif tok.used:
                ins.then_inc(self.sem, 1)


class Banks:

    def __init__(self, banks):
        self.banks, self.free, self.at = banks, [() for _ in banks], 0

    def take(self):
        n = self.at % len(self.banks)
        self.at += 1
        free = self.free[n]
        assert free is not None
        self.free[n] = None
        return n, self.banks[n], free

    def give(self, n, *toks):
        self.free[n] = toks


    def join(self, other):
        both = Banks(self.banks + other.banks)
        both.free = self.free + other.free
        return both


def constants():
    cols, at = [], {}

    def put(name, a):
        a = np.asarray(a, np.float32).reshape(128, -1)
        start = sum(c.shape[1] for c in cols)
        cols.append(a)
        at[name] = (start, start + a.shape[1])

    p = np.arange(128)
    put("ident", np.eye(128))
    put("d8", p[:, None] % 8 == np.arange(8)[None])
    put("rep", p[:, None] % 8 == p[None] % 8)
    put("iotap", np.stack([p, p % 64, 128 + p % 64], 1))
    put("iota8", np.broadcast_to(np.arange(8), (128, 8)))
    half = 16
    theta = (1.0 / np.float32(10000.0) ** (np.float32(2.0) * np.arange(half, dtype=np.float32) / np.float32(32))).astype(np.float32)
    t = np.arange(L)
    ang = [(t.astype(np.float32)[:, None] * theta[None]).astype(np.float32),
           ((t + np.maximum(t - 63, 0)).astype(np.float32)[:, None] * theta[None]).astype(np.float32)]
    tab = np.stack([np.stack([np.cos(a.astype(np.float64)), np.sin(a.astype(np.float64))], 1) for a in ang], 1)
    put("rope", tab.reshape(2, 128, 4, 16).transpose(1, 0, 2, 3))
    ak = ((64 + np.arange(32)).astype(np.float32)[None] * theta[:, None]).astype(np.float32).astype(np.float64)
    c, s = np.cos(ak), np.sin(ak)
    z = np.zeros((32, 32))
    put("h1", np.concatenate([c, c, z, s, s, z]))
    put("h2", np.concatenate([-s, -s, z, c, c, z]))
    put("h3", np.concatenate([z, z + 1, z, z]))
    s192 = np.arange(192)
    put("im1", np.where(s192[None] <= p[:, None] + 64, 0.0, -BIG))
    put("im0", np.where(np.arange(64)[None] <= p[:, None] % 64, 0.0, -BIG))
    put("t128", np.broadcast_to(128 * np.arange(16), (128, 16)))
    put("iotat", np.broadcast_to(np.arange(NT + 7), (128, NT + 7)))
    put("eps", np.full((128, 1), 1e-5))
    put("mpi", np.full((128, 1), -np.pi))
    j, h, tt = p // 32, (p // 4) % 8, p % 4
    for r in range(4):
        for t0 in ([192 + 16 * r] + ([64 + 16 * r] if r < 2 else [])):
            tok = t0 + 4 * j + tt
            s0 = (t0 // 64 - 1) * 64
            sl = s0 + np.arange(128)
            ok = (sl[None] >= tok[:, None] - 63) & (sl[None] <= tok[:, None])
            col = np.arange(128)
            near = (col[None] // 32 == tt[:, None]) & (col[None] % 32 < tok[:, None] - 63)
            m = np.concatenate([ok, near], 1)
            if t0 < 96:
                sf = 64 + np.arange(32)
                m = np.concatenate([m, sf[None] > tok[:, None]], 1)
            put(f"mask{t0 if t0 < 96 else r}", np.where(m, 0.0, -BIG))
    return np.ascontiguousarray(np.concatenate(cols, 1)), at


CONST, CAT = constants()


PACK = (("Wp", 128), ("rd", 17), ("WuqT", 256), ("WukT", 128), ("Wq2", 512), ("Wi", 384), ("wix", 4), ("WuvT", 128), ("Wout", 512))
PACK_AT, PACK_COLS = {}, 0
for _name, _width in PACK:
    PACK_AT[_name] = (PACK_COLS, PACK_COLS + _width)
    PACK_COLS += _width


def attention(nc, ctx, sem, group, queues, bank, a, c, ident, X0, XT, Y, g_c, g_x0, g_x, stats, load_x, after_pair):
    PE, S, V, G, SP = queues

    def sb(name, shape, dt=F32):
        return ctx.enter_context(nc.sbuf_tensor(name, shape, dt))

    ring = Banks(bank[0:4])
    pring = Banks(bank[4:6])
    pcring = Banks(bank[6:8])

    WP = sb("WP", [128, PACK_COLS])

    def w(name, rows=slice(0, 128)):
        return WP[rows, PACK_AT[name][0]:PACK_AT[name][1]]

    Wp, Wi, Wq2 = w("Wp"), w("Wi"), w("Wq2", slice(0, 64))
    WuqT, WukT, WuvT, Wout = [w(n).rearrange("p (k r) -> p k r", k=4) for n in ("WuqT", "WukT", "WuvT", "Wout")]
    wix, RD = w("wix"), w("rd")
    Wvo = sb("Wvo", [128, 2, 128])
    g_w, g_wi, g_wo = [group(f"g_w{k}") for k in ("q", "i", "o")]
    load_x(0)
    for g, lo, hi in ((g_w, "Wp", "Wq2"), (g_wi, "Wi", "wix"), (g_wo, "WuvT", "Wout")):
        cols = slice(PACK_AT[lo][0], PACK_AT[hi][1])
        SP.dma(g, lambda e, cols=cols: e.dma_start(WP[:, cols], a["packed"][:, cols]))
    load_x(1)

    sd = sb("sd", [128, 17])
    cd = sb("cd", [128, 17])
    ra = sb("ra", [128, 8, 16])
    rb = sb("rb", [128, 8, 16])
    RT = sb("RT", [128, 2, 2, 2, 16])
    GT = sb("GT", [128, 32])
    t = S(lambda e: e.activation(RD, RD, ACT.Exp, scale=-1.0), g_w)
    t = V(lambda e: e.tensor_scalar(RD, RD, 1.0, None, ALU.add), t)
    t = V(lambda e: e.reciprocal(RD, RD), t)
    t1 = S(lambda e: e.activation(sd[:, :], RD, ACT.Sin, scale=float(np.float32(2 * np.pi)), bias=c("mpi")), t, g_c[0])
    t2 = S(lambda e: e.activation(cd[:, :], RD, ACT.Sin, scale=float(np.float32(np.pi))), t)
    t = V(lambda e: e.tensor_tensor(cd[:, :], cd[:, :], cd[:, :], ALU.mult), t2)
    t = V(lambda e: e.tensor_scalar(cd[:, :], cd[:, :], -2.0, 1.0, ALU.mult, ALU.add), t)
    rope = c("rope").rearrange("p (k i) -> p k i", i=16)
    t3 = V(lambda e: e.tensor_tensor(ra[:, :, :], rope, cd[:, 0:16].unsqueeze(1).to_broadcast([128, 8, 16]), ALU.mult), t, g_c[0])
    t4 = V(lambda e: e.tensor_tensor(rb[:, :, :], rope, sd[:, 0:16].unsqueeze(1).to_broadcast([128, 8, 16]), ALU.mult), t1)
    rav = ra[:, :, :].rearrange("p (k f) i -> p k f i", f=2)
    rbv = rb[:, :, :].rearrange("p (k f) i -> p k f i", f=2)
    RTv = RT[:, :, :, :, :].rearrange("p a k f i -> p (a k) f i")
    t5 = V(lambda e: e.tensor_tensor(RTv[:, :, 0, :], rav[:, :, 0, :], rbv[:, :, 1, :], ALU.subtract), t3, t4)
    t_rt = V(lambda e: e.tensor_tensor(RTv[:, :, 1, :], rbv[:, :, 0, :], rav[:, :, 1, :], ALU.add), t3, t4)
    t = V(lambda e: e.tensor_scalar(GT[:, :], c("h1"), cd[:, 16:17], None, ALU.mult), t)
    t = V(lambda e: e.tensor_tensor(GT[:, :], GT[:, :], c("h3"), ALU.add), t)
    t_gt = V(lambda e: e.scalar_tensor_tensor(out=GT[:, :], in0=c("h2"), scalar=sd[:, 16:17], in1=GT[:, :],
                                              op0=ALU.mult, op1=ALU.add), t)

    for f in range(2):
        r = slice(64 * f, 64 * f + 64)
        n, bk, free = pring.take()
        for k in range(4):
            t = PE(lambda e, k=k, r=r, bk=bk: e.matmul(bk[0:64, 32 * k:32 * k + 32], WuqT[r, k, :], WukT[r, k, :],
                                                       start=True, stop=True), *((g_w,) + free if k == 0 else ()))
        t_wabs = V(lambda e, f=f, bk=bk: e.tensor_copy(
            Wq2[:, 0:256].rearrange("p (k f c) -> p f k c", f=2, c=32)[:, f, :, :],
            bk[0:64, 0:128].rearrange("p (k c) -> p k c", c=32)), t)
        pring.give(n, t_wabs)
    made = {}

    def value_weights():
        for f in range(2):
            r = slice(64 * f, 64 * f + 64)
            n, bk, free = pring.take()
            for k in range(4):
                t = PE(lambda e, r=r, k=k, bk=bk: e.matmul(bk[0:32, 128 * k:128 * k + 128], WuvT[r, k, :], Wout[r, k, :],
                                                           start=True, stop=True), *((g_wo,) + free if k == 0 else ()))
            for k in range(4):
                h = 2 * k + f
                x = 32 * (h % 4)
                made["wvo"] = V(lambda e, k=k, h=h, x=x, bk=bk: e.tensor_copy(Wvo[x:x + 32, h // 4, :], bk[0:32, 128 * k:128 * k + 128]), t)
            pring.give(n, made["wvo"])
            yield

    QT = sb("QT", [128, 2, NH * 512])
    cqT = sb("cqT", [64, 512])
    kiT = sb("kiT", [128, 512])
    qiT = sb("qiT", [128, 2, 512])
    AB = sb("AB", [128, 4, 288])
    M = sb("M", [128, 4, 288])
    SRC = sb("SRC", [128, 4, 64])
    RS = sb("RS", [128, 4, 64])
    R2 = sb("R2", [128, 4, 64])
    Qtok = sb("Qtok", [128, 4, NH, 128])
    pa = sb("pa", [128, NH, 2, 16])
    pb = sb("pb", [128, NH, 2, 16])
    qa = sb("qa", [128, NH, 2, 16])
    qbuf = sb("qbuf", [128, NH, 2, 16])
    ka = sb("ka", [128, 2, 2, 16])
    kb = sb("kb", [128, 2, 2, 16])
    Kt = sb("Kt", [128, 4, 128])
    Kf = sb("Kf", [128, 2, 128])
    RL = sb("RL", [128, 4, 192])
    I1 = sb("I1", [128, 3, 192])
    V8 = sb("V8", [128, 3, 32])
    IX = sb("IX", [128, 3, 32], U32)
    IXb = sb("IXb", [128, 3, 32], BF16)
    KL = sb("KL", [128, 2, 512])
    KF = sb("KF", [128, 2, 2, 32])
    KG = sb("KG", [128, 2, 4, 3, 128], BF16)
    KS = sb("KS", [128, 2, 4, 128], BF16)
    CK = sb("CK", [128, 2, 4, 32])
    CM = sb("CM", [128, 2, 2, 32])
    BC = sb("BC", [128, 2, 6144], BF16)
    SLOTS = {"OH": 3, "Gs": 4, "Vg": 5, "P": 4, "PT": 3}
    OH = sb("OH", [128, SLOTS["OH"], 512], BF16)
    OH2 = sb("OH2", [128, SLOTS["OH"], 512], BF16)
    Gs = sb("Gs", [128, SLOTS["Gs"], 512])
    Vg = sb("Vg", [128, SLOTS["Vg"], 4, 32])
    P = sb("P", [128, SLOTS["P"], 288])
    mx = sb("mx", [128, SLOTS["P"], 4])
    PT = sb("PT", [128, SLOTS["PT"], 384])
    SM = sb("SUMS", [128, 3, 4])
    OS = sb("OSUM", [128, 2, 4, 32])
    pcT = sb("pcT", [128, 2, 2, 128])
    idxd = nc.dram_tensor("idxd", [B, 192 * 32], BF16, kind="Internal").ap()

    G(lambda e: e.memset(Kt[:, :, :], 0.0))
    t_zero = G(lambda e: e.memset(Kf[:, :, :], 0.0))

    ready, far, ended, table = {}, {}, {}, {}

    def prepare(p):
        q = p % 2
        before = ended.get(("prepare", p - 1), ()) + ended.get(("attend", 2 * p - 3), ())
        for queue in (PE, S, V, G, SP):
            queue.hold(*before)
        xs = slice(512 * p, 512 * p + 512)

        def project(w, rows, dst, eng, g):
            n, bk, free = pring.take()
            t = PE(lambda e: e.matmul(bk[0:rows, :], w, XT[:, xs], start=True, stop=True), g_x[p], g, *free)
            if eng is S:
                t = S(lambda e: e.activation(dst, bk[0:rows, :], ACT.Copy), t)
            else:
                t = V.free(lambda e: e.tensor_copy(dst, bk[0:rows, :]), t)
            pring.give(n, t)
            return t

        t_in = []

        def index_inputs():
            t_in.append(project(Wi[:, 0:128], 128, kiT[:, :], S, g_wi))
            yield
            t_in.append(project(Wi[:, 128:256], 128, qiT[:, 0, :], V, g_wi))
            t_in.append(project(Wi[:, 256:384], 128, qiT[:, 1, :], S, g_wi))
            yield

        used_rl, t_i = [], {}

        def best(k, rows_of, width, mask):
            banks = []
            m = 128 if width == 192 else 64
            for f in range(2):
                n, bk, free = pring.take()
                r = slice(64 * f, 64 * f + 64)
                first = tuple(t_in) + free
                for g in range(2):
                    for o, b in rows_of:
                        tq = 256 * b + m
                        t = PE(lambda e, r=r, g=g, o=o, b=b, tq=tq, bk=bk: e.matmul(
                            bk[o:o + m, g * width:g * width + width], qiT[r, g, tq:tq + m],
                            kiT[r, 256 * b:256 * b + width], start=True, stop=True), *first)
                        first = ()
                t = S(lambda e, f=f, bk=bk: e.activation(
                    RL[:, f:4:2, 0:width], bk[:, 0:2 * width].rearrange("p (h s) -> p h s", h=2), ACT.Relu), t, *used_rl)
                pring.give(n, t)
                banks.append(t)
            yield
            I = I1[:, k, 0:width]
            t = V(lambda e: e.scalar_tensor_tensor(out=I, in0=RL[:, 0, 0:width], scalar=wix[:, 0:1], in1=mask,
                                                   op0=ALU.mult, op1=ALU.add), g_c[0], *banks)
            for h in range(1, 4):
                t = V(lambda e, h=h: e.scalar_tensor_tensor(out=I, in0=RL[:, h, 0:width], scalar=wix[:, h:h + 1], in1=I,
                                                            op0=ALU.mult, op1=ALU.add), t)
                if h == 1:
                    yield
            used_rl[:] = [t]
            yield
            for r in range(4):
                v8 = V8[:, k, 8 * r:8 * r + 8]
                t = V(lambda e, v8=v8: e.max(v8, I), t)
                V(lambda e, v8=v8, r=r: e.max_index(IX[:, k, 8 * r:8 * r + 8], v8, I), t)
                if r < 3:
                    t = V.free(lambda e, v8=v8: e.match_replace(I, v8, I, LOW), t)
                    yield
            t_i[k] = V(lambda e: e.tensor_copy(IXb[:, k, :], IX[:, k, :]), t)
            yield

        g_i = [group(f"g_i{2 * p + o}") for o in range(2)]

        def keep(o):
            b = 2 * p + o
            SP.dma(g_i[o], lambda e: e.dma_start(idxd[b, 2048:6144].rearrange("(t k) -> t k", k=32), IXb[:, o, :]), t_i[o])
            SP.dma(g_i[o], lambda e: e.dma_start(idxd[b, 0:2048].rearrange("(t k) -> t k", k=32),
                                                 IXb[64 * o:64 * o + 64, 2, :]), t_i[2])
            far[b] = g_i[o]

        def far_first():
            yield from index_inputs()
            yield from best(2, [(0, 0), (64, 1)], 64, c("im0"))
            yield from best(0, [(0, 0)], 192, c("im1"))
            keep(0)

        if p:
            yield from far_first()
        else:
            state["side"] = far_first()
        t_cq = project(Wp[:, 0:64], 64, cqT[:, :], V, g_w)
        yield

        n, bk, free = pring.take()
        for i in range(4):
            PE(lambda e, i=i, bk=bk: e.matmul(bk[:, 64 * i:64 * i + 64], XT[:, 512 * p + 128 * i:512 * p + 128 * i + 128],
                                              Wp[:, 64:128], start=True, stop=True), *free)
        for o in range(2):
            t = PE(lambda e, o=o, bk=bk: e.matmul(bk[:, 256 + 32 * o:288 + 32 * o],
                                                  XT[:, 512 * p + 256 * o + 64:512 * p + 256 * o + 192], Wp[:, 64:96],
                                                  start=True, stop=True))
        kv = bk[:, 0:256].rearrange("p (i f) -> p i f", i=4)
        S(lambda e, bk=bk: e.activation(CM[:, q, :, :], bk[:, 256:320].rearrange("p (o f) -> p o f", o=2), ACT.Copy), t)
        t = S(lambda e, kv=kv: e.activation(CK[:, q, :, :], kv[:, :, 0:32], ACT.Copy))
        t_z = S(lambda e, kv=kv: e.activation(M[:, :, 0:32], kv[:, :, 32:64], ACT.Copy))
        pring.give(n, t_z)
        ck = CK[:, q, :, :]
        G(lambda e: e.tensor_copy(SRC[:, :, 32:64], ck), t)
        G(lambda e: e.tensor_copy(Kt[:, :, 32:64], ck), t_zero)
        t_ck = G(lambda e: e.tensor_copy(Kf[:, :, 32:64], ck[:, 0:4:2, :]))
        yield
        for i in range(4):
            n, bk, free = pring.take()
            t = PE(lambda e, i=i, bk=bk: e.matmul(bk[:, :], cqT[:, 128 * i:128 * i + 128], Wq2, start=True, stop=True),
                   t_cq, t_wabs, *free)
            t_z = S(lambda e, i=i, bk=bk: e.activation(M[:, i, 32:288], bk[:, 256:512], ACT.Copy), t)
            t_qa = V.free(lambda e, i=i, bk=bk: e.tensor_copy(Qtok[:, i, :, 32:64],
                                                         bk[:, 0:256].rearrange("p (h f) -> p h f", h=NH)), t_z)
            pring.give(n, t_qa)
            yield
        S(lambda e: e.activation(AB[:, :, :], M[:, :, :], ACT.Abs), t_z)
        yield
        S(lambda e: e.activation(AB[:, :, :], AB[:, :, :], ACT.Exp, scale=-1.0))
        yield
        t = S(lambda e: e.activation(AB[:, :, :], AB[:, :, :], ACT.Ln, bias=1.0))
        t_m = V(lambda e: e.scalar_tensor_tensor(out=M[:, :, :], in0=M[:, :, :], scalar=0.0, in1=AB[:, :, :],
                                                 op0=ALU.max, op1=ALU.add), t)
        yield

        def part3(k):
            return KG[:, q, :, k, 0:64]

        def both(k):
            return KG[:, q, :, k, :].rearrange("p i (r f) -> p i r f", r=2)

        def twice(s):
            return s.unsqueeze(2).to_broadcast([128, 4, 2, 64])

        def parts():
            V(lambda e: e.tensor_copy(SRC[:, :, 0:32], M[:, :, 0:32]))
            V(lambda e: e.tensor_copy(both(0), twice(SRC[:, :, :])), t_ck)
            V(lambda e: e.tensor_tensor(RS[:, :, :], SRC[:, :, :], part3(0), ALU.subtract))
            yield
            V(lambda e: e.tensor_copy(both(1), twice(RS[:, :, :])))
            V(lambda e: e.tensor_tensor(R2[:, :, :], RS[:, :, :], part3(1), ALU.subtract))
            t = V(lambda e: e.tensor_copy(both(2), twice(R2[:, :, :])))
            for f in range(2):
                t = V(lambda e, f=f: e.tensor_copy(KS[64 * f:64 * f + 64, q, :, :], KG[0:64, q, :, f, :]), t)
            table[p] = t
            yield

        if p:
            yield from parts()

        for o in range(2):
            mk = M[:, 2 * o:2 * o + 2, 0:32].rearrange("p i (f j) -> p i f j", f=2)
            cs, sn = [RT[:, :, 0, f, :].unsqueeze(2).to_broadcast([128, 2, 2, 16]) for f in range(2)]
            G(lambda e, mk=mk, cs=cs: e.tensor_tensor(ka[:, :, :, :], mk, cs, ALU.mult), t_m, t_rt)
            G(lambda e, mk=mk, sn=sn: e.tensor_tensor(kb[:, :, :, :], mk, sn, ALU.mult))
            G(lambda e, o=o: e.tensor_tensor(Kt[:, 2 * o:2 * o + 2, 96:112], ka[:, :, 0, :], kb[:, :, 1, :], ALU.subtract))
            G(lambda e, o=o: e.tensor_tensor(Kt[:, 2 * o:2 * o + 2, 112:128], kb[:, :, 0, :], ka[:, :, 1, :], ALU.add))
        t_kt = G(lambda e: e.tensor_copy(Kf[:, :, 0:32], Kt[:, 0:4:2, 96:128]))
        for _ in range(4 if p else 0):
            yield
        n, bk, free = pring.take()
        for i in range(4):
            t = PE(lambda e, i=i, bk=bk: e.transpose(bk[:, 128 * i:128 * i + 128], Kt[:, i, :], ident), t_kt, *free)
        t_kl = S(lambda e, bk=bk: e.activation(KL[:, q, :], bk[:, :], ACT.Copy), t)
        pring.give(n, t_kl)
        n, bk, free = pring.take()
        for o in range(2):
            t = PE(lambda e, o=o, bk=bk: e.transpose(bk[:, 128 * o:128 * o + 128], Kf[:, o, :], ident), *free)
        t_kf = S(lambda e, bk=bk: e.activation(KF[:, q, :, :], bk[:, 0:256].rearrange("p (o s) -> p o s", o=2)[:, :, 64:96], ACT.Copy), t)
        pring.give(n, t_kf)
        yield
        t_qt, rotated = {}, {}

        def rotate(i):
            mq = M[:, i, 32:288].rearrange("p (h f j) -> p h f j", h=NH, f=2)
            rotated[i] = [t_qa]
            for k in range(2):
                E = V if (k == 0 and (i % 2 or p == 0)) else G
                xa, xb = (pa, pb) if E is G else (qa, qbuf)
                at = 96 if k else 0
                cs, sn = [RT[:, i % 2, k, f, :].unsqueeze(1).unsqueeze(1).to_broadcast([128, NH, 2, 16]) for f in range(2)]
                E(lambda e, mq=mq, cs=cs, xa=xa: e.tensor_tensor(xa[:, :, :, :], mq, cs, ALU.mult), t_m, t_rt)
                E(lambda e, mq=mq, sn=sn, xb=xb: e.tensor_tensor(xb[:, :, :, :], mq, sn, ALU.mult))
                if E is V:
                    yield
                E(lambda e, at=at, xa=xa, xb=xb: e.tensor_tensor(Qtok[:, i, :, at:at + 16], xa[:, :, 0, :], xb[:, :, 1, :], ALU.subtract))
                t = E(lambda e, at=at, xa=xa, xb=xb: e.tensor_tensor(Qtok[:, i, :, at + 16:at + 32], xb[:, :, 0, :], xa[:, :, 1, :], ALU.add))
                if k == 0:
                    E(lambda e, xa=xa, xb=xb: e.tensor_tensor(Qtok[:, i, :, 64:80], xb[:, :, 0, :], xa[:, :, 1, :], ALU.add))
                    t = E(lambda e, xa=xa, xb=xb: e.tensor_tensor(Qtok[:, i, :, 80:96], xb[:, :, 1, :], xa[:, :, 0, :], ALU.subtract))
                rotated[i].append(t)
            yield

        def turned(i):
            for f in range(2):
                n, bk, free = pring.take()
                for h in range(4):
                    t = PE(lambda e, h=h, f=f, bk=bk: e.transpose(bk[:, 128 * h:128 * h + 128], Qtok[:, i, 4 * f + h, :], ident),
                           *(free + tuple(rotated[i]) if h == 0 else ()))
                dst = QT[:, q, :].rearrange("p (g h t) -> p h g t", h=NH, t=4)[:, 4 * f:4 * f + 4, 32 * i:32 * i + 32, :]
                src = bk[:, :].rearrange("p (h g t) -> p h g t", h=4, t=4)
                t_qt[i, f] = S(lambda e, dst=dst, src=src: e.activation(dst, src, ACT.Copy), t)
                pring.give(n, t_qt[i, f])
                yield
            ready[p, i] = (t_qt[i, 0], t_qt[i, 1], t_kl, t_kf, t_ck)

        if p == 0:
            yield from rotate(0)
            yield from turned(0)
            yield from state.pop("side")
            yield from parts()
            yield from value_weights()
        for i in range(0 if p else 1, 4):
            yield from rotate(i)
            if i > 1 or p:
                yield from turned(i - 1) if i else ()
            if i == 1:
                yield from best(1, [(0, 1)], 192, c("im1"))
                keep(1)
        yield from turned(3)
        ended["prepare", p] = (t_qt[3, 1], table[p], t_kt, g_i[0], g_i[1]) + tuple(rotated[2] + rotated[3])

    g_b = [group(f"g_b{b}") for b in range(B)]
    slot, state = {}, {}

    def spread(b):
        SP.dma(g_b[b], lambda e: e.dma_start(BC[:, b % 2, :], idxd[b, :].partition_broadcast(128)), far[b],
               *ended.get(("onehot", b - 2), ()))

    def old(name, k, *keys):
        k %= SLOTS[name]
        return tuple(slot[name, k, key] for key in keys if (name, k, key) in slot)

    def one_hot(b, r, k):
        t0 = 16 * r
        if t0 < 64:
            return
        cols = slice((t0 - 64) * 32, (t0 - 64) * 32 + 512)
        few = c("iotap")[:, 1:2] if t0 < 128 else c("iotap")[:, 0:1]
        t = V.free(lambda e: e.tensor_scalar(OH[:, k % SLOTS["OH"], :], BC[:, b % 2, cols], few, None, ALU.is_equal),
                   g_b[b], *old("OH", k, "pe"))
        if t0 >= 192:
            t = V.free(lambda e: e.tensor_scalar(OH2[:, k % SLOTS["OH"], :], BC[:, b % 2, cols], c("iotap")[:, 2:3], None, ALU.is_equal))
        state["OH", b, r] = t
        if r == 15:
            ended["onehot", b] = (t,)

    def gather(b, r, k):
        t0, o, q = 16 * r, b % 2, (b // 2) % 2
        if t0 < 64:
            return
        n, bk, free = ring.take()
        hot, hot2 = OH[:, k % SLOTS["OH"], :], OH2[:, k % SLOTS["OH"], :]
        terms = [(KG[:, q, 2 * o, f, :], hot) for f in range(3)]
        if t0 < 128:
            terms = [(KS[:, q, 2 * o, :], hot), (KG[0:64, q, 2 * o, 2, :], hot[0:64])]
        if t0 >= 192:
            terms += [(KS[:, q, 2 * o + 1, :], hot2), (KG[0:64, q, 2 * o + 1, 2, :], hot2[0:64])]
        first = (state["OH", b, r], table[b // 2]) + ready[b // 2, 2 * o + r // 8] + free
        for f, (part, one) in enumerate(terms):
            t = PE(lambda e, f=f, part=part, one=one: e.matmul(bk[:, :], part, one, start=(f == 0), stop=(f == len(terms) - 1)),
                   *(first if f == 0 else ()))
        slot["OH", k % SLOTS["OH"], "pe"] = t
        t = V.free(lambda e: e.tensor_tensor(Gs[:, k % SLOTS["Gs"], :].rearrange("p (t k) -> p t k", k=32),
                                        bk[:, :].rearrange("p (t k) -> p t k", k=32),
                                        GT[:, :].unsqueeze(1).to_broadcast([128, 16, 32]), ALU.mult), t, t_gt,
              *old("Gs", k, "pe"))
        ring.give(n, t)
        state["Gs", b, r] = t

    def widths(r):
        t0 = 16 * r
        far_, future = t0 >= 64, 64 <= t0 < 96
        return (128 if far_ else 96), far_, future

    def score(b, r, k):
        t0, o, q = 16 * r, b % 2, (b // 2) % 2
        tq = 256 * o + t0
        near, far_, future = widths(r)
        s0 = 256 * o + (max(t0 // 64 - 1, 0)) * 64
        width = near + (128 if far_ else 0) + (32 if future else 0)
        n, bk, free = ring.take()
        rows = QT[:, q, 8 * tq:8 * tq + 128]
        t = PE(lambda e: e.matmul(bk[:, 0:near], rows, KL[:, q, s0:s0 + near], start=True, stop=True),
               *(ready[b // 2, 2 * o + r // 8] + free))
        if far_:
            for j in range(4):
                t = PE(lambda e, j=j: e.matmul(bk[32 * j:32 * j + 32, 128:256], QT[:, q, 8 * tq + 32 * j:8 * tq + 32 * j + 32],
                                               Gs[:, k % SLOTS["Gs"], 128 * j:128 * j + 128], start=True, stop=True),
                       *((state["Gs", b, r],) if j == 0 else ()))
            if future:
                t = PE(lambda e: e.matmul(bk[:, 256:288], rows, KF[:, q, o, :], start=True, stop=True))
        waits = (t,) + old("P", k, "pe")
        Pr, m = P[:, k % SLOTS["P"], 0:width], mx[:, k % SLOTS["P"], :]
        if far_:
            mask = c(f"mask{t0 if future else r % 4}")
            t = V.free(lambda e: e.tensor_tensor_reduce(out=Pr, in0=bk[:, 0:width], in1=mask, scale=1.0, scalar=LOW, op0=ALU.add,
                                                   op1=ALU.max, accum_out=m[:, 0:1]), g_c[1], *waits)
            src = Pr
        else:
            t = V.free(lambda e: e.tensor_reduce(m[:, 0:1], bk[:, 0:width], AX, ALU.max), *waits)
            src = bk[:, 0:width]
        t2 = V.free(lambda e: e.tensor_scalar(m[:, 1:2], m[:, 0:1], -SCALE, None, ALU.mult), t)
        t3 = S.free(lambda e: e.activation(Pr, src, ACT.Exp, scale=SCALE, bias=m[:, 1:2],
                                       accum_out=SM[:, (k // 4) % 3, k % 4:k % 4 + 1]), t2)
        ring.give(n, t if far_ else t3)
        state["E", b, r] = t3

    def turn(k):
        later = steps[k - 3] if 0 <= k - 3 < len(steps) and widths(steps[k - 3][1])[1] else None
        now = steps[k - 5] if 0 <= k - 5 < len(steps) else None
        if not (later or now):
            return
        n, bk, free = ring.take()
        toks = []
        if later:
            x = k - 3
            for j in range(4):
                t = PE(lambda e, j=j: e.transpose(bk[:, 384 + 32 * j:416 + 32 * j], Gs[32:64, x % SLOTS["Gs"], 128 * j:128 * j + 128],
                                                  ident[32:64, 32:64]), *((state["Gs", later[0], later[1]],) + free if j == 0 else ()))
            slot["Gs", x % SLOTS["Gs"], "pe"] = t
        if now:
            b, r = now
            y = k - 5
            near, far_, future = widths(r)
            t = PE(lambda e: e.transpose(bk[0:near, 0:128], P[:, y % SLOTS["P"], 0:near], ident), state["E", b, r], *free)
            if far_:
                t = PE(lambda e: e.transpose(bk[:, 128:256], P[:, y % SLOTS["P"], 128:256], ident))
            if future:
                t = PE(lambda e: e.transpose(bk[0:32, 256:384], P[:, y % SLOTS["P"], 256:288], ident))
            slot["P", y % SLOTS["P"], "pe"] = t
            waits = (t,) + old("PT", y, "pe")
            rows, cols = (128, 256) if far_ else (near, 128)
            toks.append(S.free(lambda e: e.activation(PT[0:rows, y % SLOTS["PT"], 0:cols], bk[0:rows, 0:cols], ACT.Copy), *waits))
            if future:
                toks.append(S.free(lambda e: e.activation(PT[0:32, y % SLOTS["PT"], 256:384], bk[0:32, 256:384], ACT.Copy)))
            state["PT", b, r] = toks[-1]
        if later:
            toks.append(S.free(lambda e: e.activation(Vg[:, x % SLOTS["Vg"], :, :], bk[:, 384:512].rearrange("p (j f) -> p j f", j=4), ACT.Copy),
                               t, *old("Vg", x, "pe")))
            state["Vg", later[0], later[1]] = toks[-1]
        ring.give(n, toks[-1])

    def value(b, r, k):
        o, q = b % 2, (b // 2) % 2
        near, far_, future = widths(r)
        if r % 4 == 0:
            state["pc"] = pcring.take()
        n, bk, free = state["pc"]
        i = r // 4
        v = CK[0:near, q, 2 * o, :] if i < 2 else CM[:, q, o, :] if i == 2 else CK[:, q, 2 * o + 1, :]
        c0 = 32 * (r % 4)
        s = k % SLOTS["PT"]
        state["pc_at", b, r] = state["pc"]
        t = PE(lambda e: e.matmul(bk[:, c0:c0 + 32], PT[0:near, s, 0:128], v, start=True, stop=not far_),
               state["PT", b, r], *(free if r % 4 == 0 else ()))
        if far_:
            for j in range(4):
                t = PE(lambda e, j=j: e.matmul(bk[32 * j:32 * j + 32, c0:c0 + 32], PT[:, s, 128 + 32 * j:160 + 32 * j],
                                               Vg[:, k % SLOTS["Vg"], j, :], start=False, stop=not future),
                       *((state["Vg", b, r],) if j == 0 else ()))
        if future:
            t = PE(lambda e: e.matmul(bk[:, c0:c0 + 32], PT[0:32, s, 256:384], CM[0:32, q, o, :], start=False, stop=True))
        slot["PT", s, "pe"] = slot["Vg", k % SLOTS["Vg"], "pe"] = t
        state["O", b, r] = t

    def divide(b, r, k):
        if r % 4 != 3:
            return
        n, bk, free = state["pc_at", b, r]
        sums = SM[:, (k // 4) % 3, :]
        t = V.free(lambda e: e.reciprocal(sums, sums), state["E", b, r])
        t = V.free(lambda e: e.tensor_tensor(OS[:, (k // 4) % 2, :, :], bk[:, 0:128].rearrange("p (s f) -> p s f", f=32),
                                             sums.unsqueeze(2).to_broadcast([128, 4, 32]), ALU.mult), t, state["O", b, r],
                   *ended.get(("heads", (k // 4) % 2), ()))
        pcring.give(n, t)
        state["OS", b, r] = t

    def heads(b, r, k):
        if r % 4 != 3:
            return
        n, bk, free = ring.take()
        f, g = r // 8, (r // 4) % 2
        first = (state["OS", b, r],) + free
        for s in range(4):
            for x in range(4):
                t = PE(lambda e, s=s, x=x: e.matmul(
                    bk[32 * x:32 * x + 32, 32 * s:32 * s + 32], OS[:, (k // 4) % 2, s, :],
                    ident.rearrange("p (j h x t) -> p x h j t", j=4, h=2, x=4)[:, x, :, :, :], start=True, stop=True), *first)
                first = ()
        ended["heads", (k // 4) % 2] = (t,)
        src = bk[:, 0:128].rearrange("p (s h t) -> p h s t", s=4, h=2)
        t = S.free(lambda e: e.activation(pcT[:, f, :, 64 * g:64 * g + 64].rearrange("p h (s t) -> p h s t", t=16), src, ACT.Copy),
                   t, *ended.get(("out", f), ()))
        ring.give(n, t)
        state["pcT"] = t

    def project_out(b, f):
        i = 2 * b + f
        n, bk, free = pring.take()
        for h in range(2):
            t = PE(lambda e, h=h: e.matmul(bk[:, 0:128], pcT[:, f, h, :], Wvo[:, h, :], start=(h == 0), stop=(h == 1)),
                   *((state["pcT"], made["wvo"]) + free if h == 0 else ()))
        ended["out", f] = (t,)
        t = V.free(lambda e: e.tensor_tensor(Y[:, i, :], bk[:, 0:128], X0[:, i, :], ALU.add), t, g_x0)
        pring.give(n, t)
        t = stats([i], t)
        if f == 1:
            ended["attend", b] = (ended["out", 0][0], ended["out", 1][0], t)
        return t

    steps = [(b, r) for b in range(B) for r in range(16)]
    STAGES = ((0, one_hot), (8, heads), (7, divide), (6, value), (None, turn), (3, score), (1, gather))
    LAST = 8
    preparing, tails = [prepare(0)], []
    state["spread"] = 0

    def advance(n):
        for _ in range(n):
            next(state.get("side", iter(())), None)
            if preparing and next(preparing[0], "end") == "end":
                preparing.pop(0)
        b = state["spread"]
        if b in far and (b < 2 or ("onehot", b - 2) in ended):
            spread(b)
            state["spread"] += 1

    for k in range(len(steps) + LAST + 1):
        if k < len(steps):
            b, r = steps[k]
            while (b // 2, 2 * (b % 2) + r // 8) not in ready or (r >= 4 and (state["spread"] <= b or b // 2 not in table)):
                advance(1)
        for lag, stage in STAGES:
            if stage is turn:
                turn(k)
            elif 0 <= k - lag < len(steps):
                stage(*steps[k - lag], k - lag)
        if k > LAST and (k - LAST - 1) % 8 == 7:
            b, r = steps[k - LAST - 1]
            t = project_out(b, r // 8)
            if b % 2 and r == 15:
                tails.append(after_pair(pring, b // 2, t))
        if k % 32 == LAST + 2 and k // 32 < 3:
            preparing.append(prepare(k // 32 + 1))
        if tails and next(tails[0], "end") == "end":
            tails.pop(0)
        advance(2)
    for tail in tails:
        for _ in tail:
            pass
    return ring.join(pring).join(pcring)


def experts(nc, ctx, sem, group, queues, banks, a, c, ident, X0, Y, xs_d, logit, g_z, t_logit, stats, root, divided, pieces):
    PE, S, V, G, SP = queues
    E, NF, TS = 8, 512, TILES
    AHEAD, EACH = 36, 1

    def sb(name, shape, dt=F32):
        return ctx.enter_context(nc.sbuf_tensor(name, shape, dt))

    ring = Banks(banks)
    W1 = sb("W1", [128, E * NF])
    W2 = sb("W2", [128, E * 4 * 128])
    oneb = sb("oneb", [128, 128], BF16)
    before = sb("before", [128, 128], BF16)
    route = sb("route", [128, NT, E])
    rest = sb("rest", [128, E])
    ones8 = sb("ones8", [128, E])
    top = sb("top", [128, NT])
    pick = sb("pick", [128, NT])
    hot = sb("hot", [128, NT, E])
    hotb = sb("hotb", [128, NT, E], BF16)
    rank = sb("rank", [128, NT, E])
    cnt = sb("cnt", [128, E])
    cmp16 = sb("cmp16", [128, E, 16])
    tiles = sb("tiles", [128, E])
    ends = sb("ends", [128, E])
    starts = sb("starts", [128, E])
    pos = sb("pos", [128, NT])
    posu = sb("posu", [128, NT], U32)
    cmpt = sb("cmpt", [128, TS, E])
    tef = sb("tef", [128, TS])
    tei = sb("tei", [128, TS], I32)
    NB = 4
    Xs = sb("Xs", [128, TS, 128])
    XsT = sb("XsT", [128, NB, 128])
    H = sb("H", [128, NB, NF])
    HT = sb("HT", [128, NB, 4, 128])
    Ys = sb("Ys", [128, NB, 128])
    Yg = Xs
    ys_d = nc.dram_tensor("ys_d", [TS * 128, 128], F32, kind="Internal").ap()

    g_1, g_2, g_s = [group(f"g_f{k}") for k in ("1", "2", "s")]
    for e0 in range(0, E, 4):
        SP.dma(g_1, lambda e, e0=e0: e.dma_start(W1[:, e0 * NF:(e0 + 4) * NF].rearrange("p (e f) -> p e f", e=4),
                                                 a["W1"][e0:e0 + 4].rearrange("e p f -> p e f")))
    for e0 in range(0, E, 4):
        SP.dma(g_2, lambda e, e0=e0: e.dma_start(
            W2[:, e0 * 512:(e0 + 4) * 512].rearrange("p (e c d) -> p (e c) d", e=4, c=4),
            a["W2"][e0:e0 + 4].rearrange("e (c p) d -> p (e c) d", p=128)))
    G(lambda e: e.memset(oneb[:, :], 1.0))
    t_one = G(lambda e: e.affine_select(out=before[:, :], in_=oneb[:, :], compare_op=ALU.is_gt, fill=0.0, base=0,
                                        pattern=[[1, 128]], channel_multiplier=-1))

    def advance(n):
        for _ in range(n):
            next(pieces, None)

    def wide(s):
        return s.unsqueeze(2).to_broadcast([128, NT, E])

    def over(s):
        return s.unsqueeze(1).to_broadcast([128, NT, E])

    t = S(lambda e: e.activation(route[:, :, :], logit[:, :, :], ACT.Sigmoid), t_logit)
    V(lambda e: e.memset(ones8[:, :], 1.0))
    V(lambda e: e.tensor_scalar(rest[:, :], c("iota8"), float(E), None, ALU.subtract))
    t_top = V(lambda e: e.tensor_reduce(top[:, :], route[:, :, :], AX, ALU.max), t)
    V(lambda e: e.tensor_tensor(hot[:, :, :], route[:, :, :], wide(top[:, :]), ALU.is_equal))
    V(lambda e: e.tensor_tensor(hot[:, :, :], hot[:, :, :], over(rest[:, :]), ALU.mult))
    V(lambda e: e.tensor_reduce(pick[:, :], hot[:, :, :], AX, ALU.min))
    V(lambda e: e.tensor_tensor(hot[:, :, :], over(rest[:, :]), wide(pick[:, :]), ALU.is_equal))
    t_hot = V(lambda e: e.tensor_copy(hotb[:, :, :], hot[:, :, :]))

    n, bk, free = ring.take()
    hots = hotb[:, :, :].rearrange("p i e -> p (i e)")
    PE(lambda e, bk=bk: e.matmul(bk[:, 0:128], before[:, :], hots, start=True, stop=False), t_hot, t_one, *free)
    for k in range(1, NT):
        t = PE(lambda e, k=k, bk=bk: e.matmul(bk[:, E * k:128], oneb[:, :], hots[:, 0:128 - E * k], start=False, stop=(k == NT - 1)))
    t = V(lambda e, bk=bk: e.tensor_copy(rank[:, :, :].rearrange("p i e -> p (i e)"), bk[:, 0:128]), t)
    ring.give(n, t)
    n, bk, free = ring.take()
    for k in range(NT):
        t = PE(lambda e, k=k, bk=bk: e.matmul(bk[:, 0:E], oneb[:, :], hots[:, E * k:E * k + E], start=(k == 0), stop=(k == NT - 1)), *free)
    t = V(lambda e, bk=bk: e.tensor_copy(cnt[:, :], bk[:, 0:E]), t)
    ring.give(n, t)
    V(lambda e: e.tensor_tensor(cmp16[:, :, :], cnt[:, :].unsqueeze(2).to_broadcast([128, E, 16]),
                                c("t128").unsqueeze(1).to_broadcast([128, E, 16]), ALU.is_gt))
    V(lambda e: e.tensor_reduce(tiles[:, :], cmp16[:, :, :], AX, ALU.add))
    V(lambda e: e.tensor_tensor_scan(ends[:, :], ones8[:, :], tiles[:, :], 0.0, ALU.mult, ALU.add))
    V(lambda e: e.tensor_tensor(starts[:, :], ends[:, :], tiles[:, :], ALU.subtract))
    V(lambda e: e.tensor_scalar(starts[:, :], starts[:, :], 128.0, None, ALU.mult))
    V(lambda e: e.tensor_tensor(rank[:, :, :], rank[:, :, :], starts[:, :].unsqueeze(1).to_broadcast([128, NT, E]), ALU.add))
    V(lambda e: e.tensor_tensor(rank[:, :, :], rank[:, :, :], hot[:, :, :], ALU.mult))
    V(lambda e: e.tensor_reduce(pos[:, :], rank[:, :, :], AX, ALU.add))
    t_pos = V(lambda e: e.tensor_copy(posu[:, :], pos[:, :]))
    for i in range(NT):
        G.dma(g_s, lambda e, i=i: e.indirect_dma_start(xs_d, bass.IndirectOffsetOnAxis(posu[:, i:i + 1], 0), X0[:, i, :], None),
              t_pos, g_z)
    V(lambda e: e.tensor_tensor(cmpt[:, :, :], ends[:, :].unsqueeze(1).to_broadcast([128, TS, E]),
                                c("iotat").unsqueeze(2).to_broadcast([128, TS, E]), ALU.is_le))
    V(lambda e: e.tensor_reduce(tef[:, :], cmpt[:, :, :], AX, ALU.add))
    V(lambda e: e.tensor_scalar(tef[:, :], tef[:, :], float(E - 1), float(NF), ALU.min, ALU.mult))
    t_te = V(lambda e: e.tensor_copy(tei[:, :], tef[:, :]))

    advance(AHEAD)
    at = {}
    GROUPS = [(0, 2), (2, 6), (6, 12), (12, 18), (18, TS)]
    g_ld = [group(f"g_ld{k}") for k in range(len(GROUPS))]
    g_st = [group(f"g_st{k}") for k in range(TS)]
    st, of = {}, {}
    xv = xs_d.rearrange("(k p) d -> p k d", p=128)
    for g, (lo, hi) in enumerate(GROUPS):
        SP.dma(g_ld[g], lambda e, lo=lo, hi=hi: e.dma_start(Xs[:, lo:hi, :], xv[:, lo:hi, :]), g_s)
        of.update({k: g_ld[g] for k in range(lo, hi)})

    def turn(k):
        n, bk, free = ring.take()
        t = PE(lambda e: e.transpose(bk[:, 0:128], Xs[:, k, :], ident), of[k], *free)
        t = V.free(lambda e: e.tensor_copy(XsT[:, k % NB, :], bk[:, 0:128]), t, *([st["h", k - NB]] if k >= NB else []))
        ring.give(n, t)
        st["xt", k] = t

    def first(k):
        n, bk, free = ring.take()

        def mm(e):
            at[k] = e.value_load(tei[0:1, k:k + 1], min_val=0, max_val=(E - 1) * NF)
            return e.matmul(bk[:, :], XsT[:, k % NB, :], W1[:, bass.ds(at[k], NF)], start=True, stop=True)

        t = st["h", k] = PE(mm, st["xt", k], t_te, g_1, *free)
        t = S.free(lambda e: e.activation(H[:, k % NB, :], bk[:, :], ACT.Gelu), t, *([st["ht", k - NB]] if k >= NB else []))
        ring.give(n, t)
        st["g", k] = t

    def second(k):
        n, bk, free = ring.take()
        for f in range(4):
            t = PE(lambda e, f=f: e.transpose(bk[:, 128 * f:128 * f + 128], H[:, k % NB, 128 * f:128 * f + 128], ident),
                   *((st["g", k],) + free if f == 0 else ()))
        st["ht", k] = t
        t = V.free(lambda e: e.tensor_copy(HT[:, k % NB, :, :], bk[:, :].rearrange("p (f t) -> p f t", f=4)), t,
                   *([st["y", k - NB]] if k >= NB else []))
        ring.give(n, t)
        st["hts", k] = t

    def third(k):
        n, bk, free = ring.take()
        for f in range(4):
            t = PE(lambda e, f=f: e.matmul(bk[:, 0:128], HT[:, k % NB, f, :], W2[:, bass.ds(at[k] + 128 * f, 128)],
                                           start=(f == 0), stop=(f == 3)), *((st["hts", k], g_2) + free if f == 0 else ()))
        st["y", k] = t
        t = S.free(lambda e: e.activation(Ys[:, k % NB, :], bk[:, 0:128], ACT.Copy), t, *([g_st[k - NB]] if k >= NB else []))
        ring.give(n, t)
        SP.dma(g_st[k], lambda e: e.dma_start(ys_d[128 * k:128 * k + 128, :], Ys[:, k % NB, :]), t)

    for k in range(TS + 5):
        advance(int(EACH * (k + 1)) - int(EACH * k))
        for lag, stage in ((5, third), (3, second), (1, first), (0, turn)):
            if 0 <= k - lag < TS:
                stage(k - lag)
    g_g = [group(f"g_g{k}") for k in range(4)]
    for i in range(NT):
        G.dma(g_g[i // 4], lambda e, i=i: e.indirect_dma_start(Yg[:, i, :], None, ys_d, bass.IndirectOffsetOnAxis(posu[:, i:i + 1], 0)),
              *g_st)
    advance(1000)
    ts, roots = [], []
    for p in range(4):
        for i in range(4 * p, 4 * p + 4):
            t = V.free(lambda e, i=i: e.scalar_tensor_tensor(out=Y[:, i, :], in0=Yg[:, i, :], scalar=top[:, i:i + 1], in1=X0[:, i, :],
                                                             op0=ALU.mult, op1=ALU.add), g_g[p], g_s)
        roots.append(root(p, stats(range(4 * p, 4 * p + 4), t)))
        if p:
            ts.append(divided(X0, p - 1, roots[p - 1]))
    ts.append(divided(X0, 3, roots[3]))
    return ts, ring


def scan_weights(nc, ctx, sem, group, queues, banks, a, c, ident):
    PE, S, V, G, SP = queues
    ring = Banks(banks)

    def sb(name, shape, dt=F32):
        return ctx.enter_context(nc.sbuf_tensor(name, shape, dt))

    SC = sb("SC", [128, 304])
    Af = SC[:, 0:256].rearrange("p (g m) -> p g m", g=16)
    Bc, Cc, Dr = SC[:, 256:272], SC[:, 272:288], SC[:, 288:304]
    PA = [sb(f"PA{k}", [128, 16, 136]) for k in range(4)]
    PB = [sb(f"PB{k}", [128, 16, 136]) for k in range(2)]
    Uc = sb("Uc", [128, 16, 16])
    Vc = sb("Vc", [128, 16, 16])
    Vr = sb("Vr", [128, 16, 16])
    Hk = sb("Hk", [128, 31, 16])
    Tc = sb("Tc", [128, 16, 16])
    BX = sb("BX", [128, 16, 128])
    Win = sb("Win", [128, 16, 128])
    Wou = sb("Wou", [128, 16, 128])
    Wto = sb("Wto", [128, 16, 128])
    made = {"Win": Win, "Wou": Wou, "Wto": Wto, "ES": BX, "EL": PB[0][:, :, 0:128]}
    g_a, g_t = group("g_na"), group("g_nt")
    SP.dma(g_a, lambda e: e.dma_start(SC[:, :], a["packed"]))
    yield made

    def spread(eng, dst, src, *waits):
        return eng(lambda e: e.tensor_tensor(dst[:, :, 0:128].rearrange("p g (i d) -> p g i d", d=8),
                                             src[:, :, :].unsqueeze(3).to_broadcast([128, 16, 16, 8]),
                                             c("d8").unsqueeze(1).unsqueeze(1).to_broadcast([128, 16, 16, 8]), ALU.mult), *waits)

    def out_of(bk, dst, lo, hi, w, k, t):
        got = bk[:, 0:w * (hi - lo)].rearrange("p (g m) -> p g m", m=w)
        if k % 2:
            return S(lambda e: e.activation(dst[:, lo:hi, 0:128], got[:, :, 0:128], ACT.Copy), t)
        return V(lambda e: e.tensor_copy(dst[:, lo:hi, 0:128], got[:, :, 0:128]), t)

    def turn_all(dst, src, *waits):
        toks = []
        for k in range(4):
            n, bk, free = ring.take()
            for g in range(4 * k, 4 * k + 4):
                t = PE(lambda e, g=g, k=k, bk=bk: e.transpose(bk[:, 128 * (g - 4 * k):128 * (g - 4 * k) + 128], src[:, g, 0:128], ident),
                       *(waits + free))
            toks.append(out_of(bk, dst, 4 * k, 4 * k + 4, 128, k, t))
            ring.give(n, toks[-1])
            yield
        return tuple(toks[2:])

    def product(dst, lhs, rhs, *waits, m=0, cols=None):
        per, toks, at = (3 if m else 4), [], []
        for k, lo in enumerate(range(0, 16, per)):
            hi = min(lo + per, 16)
            n, bk, free = ring.take()
            for g in range(lo, hi):
                o = (128 + m) * (g - lo)
                t = PE(lambda e, g=g, o=o, bk=bk: e.matmul(bk[:, o:o + 128 + m], lhs[:, g, 0:128], rhs[:, g, 0:128 + m],
                                                           start=True, stop=True), *(waits + free))
            toks.append(out_of(bk, dst, lo, hi, 128 + m, k, t))
            free = toks[-1:]
            if m:
                got = bk[:, 0:(128 + m) * (hi - lo)].rearrange("p (g m) -> p g m", m=128 + m)[:, :, 128:]
                if k % 2:
                    t = S(lambda e, got=got, lo=lo, hi=hi: e.activation(cols[:, lo:hi, m:2 * m], got, ACT.Copy), t)
                else:
                    t = V(lambda e, got=got, lo=lo, hi=hi: e.tensor_copy(cols[:, lo:hi, m:2 * m], got), t)
                at.append(t)
                free = free + [t]
            ring.give(n, *free)
            yield
        return tuple(toks[-2:] + at[-2:])

    t = spread(V, PA[0], Af, g_a)
    pw = (yield from turn_all(PB[0], PA[0], t))
    pw = pw + (t,)
    n, bk, free = ring.take()
    for g in range(16):
        t = PE(lambda e, g=g: e.matmul(bk[:, g:g + 1], PB[0][:, g, 0:128], Cc[:, g:g + 1], start=True, stop=True), *(pw + free))
    t_u = V(lambda e: e.tensor_copy(Uc[:, :, 0:1], bk[:, 0:16].unsqueeze(2)), t)
    ring.give(n, t_u)
    t_v = G(lambda e: e.tensor_copy(Vc[:, :, 0:1].rearrange("p g o -> p (g o)"), Bc), g_a)
    yield
    cur_a, cur_b = PA[0], PB[0]
    nexta, nextb = [PA[1], PA[0], PA[1], PA[0]], [PB[1], PB[0], PB[1], PB[0]]
    for p in range(4):
        m = 2 ** p
        t_u = G(lambda e, m=m, cur_a=cur_a: e.tensor_copy(cur_a[:, :, 128:128 + m], Uc[:, :, 0:m]), t_u, *pw)
        t_v = G(lambda e, m=m, cur_b=cur_b: e.tensor_copy(cur_b[:, :, 128:128 + m], Vc[:, :, 0:m]), t_v, *pw)
        pa = (yield from product(nexta[p], cur_b, cur_a, t_v, *pw, m=m, cols=Uc))
        pb = (yield from product(nextb[p], cur_a, cur_b, *pw, m=m, cols=Vc))
        t_u, t_v = pa[2], pb[2]
        pw = pa + pb
        cur_a, cur_b = nexta[p], nextb[p]
    for k in range(16):
        t = G(lambda e, k=k: e.tensor_copy(Vr[:, :, 15 - k:16 - k], Vc[:, :, k:k + 1]), *pw)
    t = spread(V, BX, Vr, t)
    t_win = (yield from turn_all(Win, BX, t))
    t_wou = spread(V, Wou, Uc, *pw)
    t = V(lambda e: e.tensor_tensor(Vr[:, :, :], Vc[:, :, :], Cc.unsqueeze(2).to_broadcast([128, 16, 16]), ALU.mult), t)
    n, bk, free = ring.take()
    t = PE(lambda e, bk=bk: e.matmul(bk[:, 0:256], c("rep"), Vr[:, :, :].rearrange("p g k -> p (g k)"), start=True, stop=True), t, *free)
    t = V(lambda e, bk=bk: e.tensor_copy(Hk[:, 15:31, :], bk[:, 0:256].rearrange("p (g k) -> p k g", g=16)), t)
    ring.give(n, t)
    V(lambda e: e.tensor_scalar(Dr, Dr, 1.0, None, ALU.add), g_a)
    t = V(lambda e: e.tensor_tensor(Hk[:, 15, :], Hk[:, 15, :], Dr, ALU.add))
    t2 = G(lambda e: e.memset(Hk[:, 0:15, :], 0.0))
    for j in range(16):
        r = slice(8 * j, 8 * j + 8)
        G.dma(g_t, lambda e, j=j, r=r: e.dma_start(Tc[r, :, :], Hk[r, 15 - j:31 - j, :]), t, t2)
    yield
    power = [cur_a]
    for p in range(3):
        dst = [PA[1], PA[2], PA[3]][p]
        pa = (yield from product(dst, cur_b, cur_a, *pw))
        if p < 2:
            nb = PB[1] if cur_b is PB[0] else PB[0]
            pw = pw + pa + (yield from product(nb, cur_a, cur_b, *pw))
            cur_b = nb
        else:
            pw = pw + pa
        cur_a = dst
        power.append(dst)
    t_wto = spread(V, Wto, Tc[:, :, :].rearrange("p i g -> p g i"), g_t)
    yield
    made.update(ring=ring, power=power, t_win=t_win, t_wou=t_wou, t_wto=t_wto, pw=pw)


def scan(nc, ctx, sem, group, queues, ring, a, c, ident, X0, XT, Y, transposed, made, x2):
    PE, S, V, G, SP = queues

    def sb(name, shape, dt=F32):
        return ctx.enter_context(nc.sbuf_tensor(name, shape, dt))

    Wg = sb("Wg", [128, 128])
    WgT = sb("WgT", [128, 128])
    bg = sb("bg", [128, 1])
    gam = sb("gam", [128, 128])
    bet = sb("bet", [128, 128])
    bgr = sb("bgr", [1, 512])
    ones = sb("ones0", [1, 128])
    GA = sb("GA", [128, NT, 128])
    U = sb("U", [128, 16, 128])
    XP = sb("XP", [128, NT, 128])
    Win, Wou, Wto, power = [made[k] for k in ("Win", "Wou", "Wto", "power")]
    t_win, t_wou, t_wto, pw = [made[k] for k in ("t_win", "t_wou", "t_wto", "pw")]
    ES, EL = made["ES"], made["EL"]
    g_w = group("g_nw")
    SP.dma(g_w, lambda e: e.dma_start(Wg[:, :], a["Wg"]))
    for k in range(4):
        SP.dma(g_w, lambda e, k=k: e.dma_start(bgr[:, 128 * k:128 * k + 128], a["bg"].rearrange("(o p) -> o p", o=1)))
    SP.dma(g_w, lambda e: e.dma_start(gam[:, :], a["gamma"].partition_broadcast(128)))
    SP.dma(g_w, lambda e: e.dma_start(bet[:, :], a["beta"].partition_broadcast(128)))
    t_one = G(lambda e: e.memset(ones[:, :], 1.0), g_w)
    t_zero = G(lambda e: e.memset(EL, 0.0), *pw)

    n, bk, free = ring.take()
    t = PE(lambda e, bk=bk: e.transpose(bk[:, 0:128], Wg[:, :], ident), g_w, *free)
    t_wg = V(lambda e, bk=bk: e.tensor_copy(WgT[:, :], bk[:, 0:128]), t)
    ring.give(n, t_wg)
    t_xt = tuple(transposed(ring, X0, p, *x2[p]) for p in range(4))

    gated = []
    for p in range(4):
        n, bk, free = ring.take()
        for i in range(4):
            t = PE(lambda e, i=i, p=p, bk=bk: e.transpose(bk[:, 128 * i:128 * i + 128], XT[:, 4 * p + i:2048:16], ident),
                   *(t_xt + free))
        t_xp = V(lambda e, p=p, bk=bk: e.tensor_copy(XP[:, 4 * p:4 * p + 4, :], bk[:, :].rearrange("p (i d) -> p i d", i=4)), t)
        ring.give(n, t_xp)
        n, bk, free = ring.take()
        PE(lambda e, bk=bk: e.matmul(bk[:, :], ones[:, :], bgr[:, :], start=True, stop=False, skip_group_check=True), t_wg, t_one, *free)
        for i in range(4):
            t = PE(lambda e, i=i, p=p, bk=bk: e.matmul(bk[:, 128 * i:128 * i + 128], XT[:, 4 * p + i:2048:16], WgT[:, :], start=False,
                                                       stop=(i == 3), skip_group_check=True))
        t = S(lambda e, p=p, bk=bk: e.activation(GA[:, 4 * p:4 * p + 4, :], bk[:, :].rearrange("p (i d) -> p i d", i=4), ACT.Sigmoid), t)
        ring.give(n, t)
        gated.append(V(lambda e, p=p: e.tensor_tensor(GA[:, 4 * p:4 * p + 4, :], GA[:, 4 * p:4 * p + 4, :], XP[:, 4 * p:4 * p + 4, :],
                                                      ALU.mult), t))
    t_xp = G(lambda e: e.tensor_tensor(XP[:, :, :], XP[:, :, :], bet[:, :].unsqueeze(1).to_broadcast([128, NT, 128]), ALU.add), *gated, g_w)
    gav = GA[:, :, :].rearrange("p j (d g) -> p g (j d)", g=16)
    t_u = []
    for k in range(4):
        n, bk, free = ring.take()
        for g in range(4 * k, 4 * k + 4):
            t = PE(lambda e, g=g, k=k, bk=bk: e.transpose(bk[:, 128 * (g - 4 * k):128 * (g - 4 * k) + 128], gav[:, g, :], ident),
                   *(tuple(gated) + free))
        dst, src = U[:, 4 * k:4 * k + 4, :], bk[:, :].rearrange("p (g q) -> p g q", g=4)
        if k % 2:
            t = S(lambda e, dst=dst, src=src: e.activation(dst, src, ACT.Copy), t)
        else:
            t = V(lambda e, dst=dst, src=src: e.tensor_copy(dst, src), t)
        ring.give(n, t)
        t_u.append(t)

    got = {}
    taken = []
    for k in range(4):
        n, bk, free = ring.take()
        taken.append((n, bk))
        for g in range(4 * k, 4 * k + 4):
            t = PE(lambda e, g=g, k=k, bk=bk: e.matmul(bk[:, 128 * (g - 4 * k):128 * (g - 4 * k) + 128], Win[:, g, :], U[:, g, :],
                                                       start=(g == 4 * k), stop=False, skip_group_check=True),
                   *(t_win + (t_u[k],) + free))
        got[k] = t

    def state_out(k):
        n, bk = taken[k]
        dst, src = ES[:, 4 * k:4 * k + 4, :], bk[:, :].rearrange("p (g q) -> p g q", g=4)
        if k % 2:
            return S(lambda e: e.activation(dst, src, ACT.Copy), got[k], *t_win)
        return V(lambda e: e.tensor_copy(dst, src), got[k], *t_win)

    for p in range(4):
        s = 2 ** p
        outs = [state_out(k) for k in range(4)]
        for k in range(4):
            n, bk = taken[k]
            for g in range(4 * k, 4 * k + 4):
                w = slice(128 * (g - 4 * k), 128 * (g - 4 * k) + 128)
                t = PE(lambda e, g=g, w=w, p=p, s=s, bk=bk: e.matmul(
                    bk[:, w].rearrange("p (b q) -> p b q", b=8)[:, :, s:16], power[p][:, g, 0:128],
                    ES[:, g, :].rearrange("p (b q) -> p b q", b=8)[:, :, 0:16 - s], start=False, stop=(p == 3),
                    skip_group_check=True), outs[k], *pw)
            got[k] = t
    last = []
    for k in range(4):
        n, bk = taken[k]
        dst = EL[:, 4 * k:4 * k + 4, :].rearrange("p g (b q) -> p g b q", b=8)[:, :, :, 1:16]
        src = bk[:, :].rearrange("p (g b q) -> p g b q", g=4, b=8)[:, :, :, 0:15]
        if k % 2:
            t = S(lambda e, dst=dst, src=src: e.activation(dst, src, ACT.Copy), got[k], t_zero)
        else:
            t = V(lambda e, dst=dst, src=src: e.tensor_copy(dst, src), got[k], t_zero)
        ring.give(n, t)
        last.append(t)
    yv = Y[:, :, :].rearrange("p i (d g) -> p g i d", g=16)
    ys = []
    for k in range(4):
        n, bk, free = ring.take()
        for g in range(4 * k, 4 * k + 4):
            w = slice(128 * (g - 4 * k), 128 * (g - 4 * k) + 128)
            PE(lambda e, g=g, w=w, bk=bk: e.matmul(bk[:, w], U[:, g, :], Wto[:, g, :], start=True, stop=False), t_wto, *free)
            t = PE(lambda e, g=g, w=w, bk=bk: e.matmul(bk[:, w], EL[:, g, :], Wou[:, g, :], start=False, stop=True), t_wou, last[k])
        for x in range(4):
            dst, src = yv[:, 4 * k + x, :, :], bk[:, 128 * x:128 * x + 128].rearrange("p (i d) -> p i d", d=8)
            if k % 2:
                t2 = S(lambda e, dst=dst, src=src: e.activation(dst, src, ACT.Copy), t)
            else:
                t2 = V(lambda e, dst=dst, src=src: e.tensor_copy(dst, src), t)
        ring.give(n, t2)
        ys.append(t2)
    return ring, ys, gam, XP, t_xp



def mixture_weights(ctx, nc, group, SP, a):
    def sb(name, shape, dt=F32):
        return ctx.enter_context(nc.sbuf_tensor(name, shape, dt))

    w = {"Wen": sb("Wen", [128, 256]), "ben": sb("ben", [128, 2]), "Wsc": sb("Wsc", [128, 2, 2, 64]), "bsc": sb("bsc", [128, 1]),
         "Wr1": sb("Wr1", [64, 64]), "br1": sb("br1", [64, 1]), "Wr2": sb("Wr2", [64, 8]), "br2": sb("br2", [8, 1]),
         "We1": sb("We1", [128, 8, 128]), "be1": sb("be1", [128, 8]), "We2": sb("We2", [128, 8, 64]), "be2": sb("be2", [128, 4]),
         "Wcs": sb("Wcs", [128, 256]), "bcs": sb("bcs", [128, 2]), "Wde": sb("Wde", [128, 2, 128]), "bde": sb("bde", [128, 128]),
         "gam": sb("lng", [128, 128]), "bet": sb("lnb", [128, 128])}
    g = group("g_m")

    def load(dst, src):
        SP.dma(g, lambda e: e.dma_start(dst, src))

    def col(s):
        return s.rearrange("(p o) -> p o", o=1)

    def load_all():
        load(w["Wen"][:, :], a["enc_W"])
        load(w["ben"][:, :], a["enc_b"])
        for k in range(2):
            load(w["Wsc"][:, :, k, :], a["s2c_W"].rearrange("(k p) m -> p k m", p=128))
            load(w["bsc"][64 * k:64 * k + 64, :], col(a["s2c_b"]))
            load(w["Wcs"][64 * k:64 * k + 64, :], a["c2s_W"])
        load(w["We1"][0:64, :, :], a["We1"].rearrange("e m h -> m e h"))
        load(w["Wr1"][:, :], a["rW1"])
        load(w["br1"][:, :], col(a["rb1"]))
        load(w["Wr2"][:, :], a["rW2"])
        load(w["br2"][:, :], col(a["rb2"]))
        load(w["be1"][:, :], a["be1"])
        load(w["We2"][:, :, :], a["We2"].rearrange("e h m -> h e m"))
        load(w["be2"][:, :], a["be2"])
        load(w["bcs"][:, :], a["c2s_b"])
        load(w["Wde"][:, :, :], a["dec_W"].rearrange("(k p) d -> p k d", p=128))
        load(w["bde"][:, :], a["dec_b"].partition_broadcast(128))
        load(w["gam"][:, :], a["ln_g"].partition_broadcast(128))
        load(w["bet"][:, :], a["ln_b"].partition_broadcast(128))

    return w, g, load_all


def mixture(nc, ctx, group, queues, ring, w, g_w, c, ident, X0, XT, Y, transposed, x3):
    PE, S, V, G, SP = queues
    E = 8

    def sb(name, shape, dt=F32):
        return ctx.enter_context(nc.sbuf_tensor(name, shape, dt))

    Wen, ben, Wsc, bsc, Wr1, br1, Wr2, br2, We1, be1, We2, be2, Wcs, bcs, Wde, bde, gam, bet = [w[k] for k in (
        "Wen", "ben", "Wsc", "bsc", "Wr1", "br1", "Wr2", "br2", "We1", "be1", "We2", "be2", "Wcs", "bcs", "Wde", "bde", "gam", "bet")]
    EN = sb("EN", [128, 2, 2, 512])
    CT = sb("CT", [128, 2048])
    T1 = sb("T1", [64, 2, 512])
    LT = sb("LT", [8, 2, 512])
    LG = sb("LG", [128, NT, E])
    lm = sb("lm", [128, NT])
    ls = sb("ls", [128, NT])
    rest = sb("rest2", [128, E])
    top = sb("top2", [128, NT, 2])
    eq = sb("eq2", [128, NT, E])
    h1 = sb("h1", [128, NT, E])
    h2 = sb("h2", [128, NT, E])
    hg = sb("hg", [128, 2, 4, NT])
    gtT = sb("gtT", [128, 128])
    GB = sb("GB", [128, 4, 4, 512])
    HE = sb("HE", [128, 2, E, 512])
    PR = sb("PR", [128, 2, 512])
    OT = sb("OT", [128, 2, 512])
    gt_d = nc.dram_tensor("gt_d", [128, 128], F32, kind="Internal").ap()
    SM = sb("SM", [128, 2, 2, 512])
    XB = sb("XB", [128, NT, 128])
    x = {}

    def wide(s, k=E):
        return s.unsqueeze(2).to_broadcast([128, NT, k])

    def over(s):
        return s.unsqueeze(1).to_broadcast([128, NT, E])

    t_zero = G(lambda e: e.memset(We1[64:128, :, :], 0.0))

    def encode(p):
        xs = slice(512 * p, 512 * p + 512)
        t_x = transposed(ring, X0, p, *x3(p))
        for k in range(2):
            n, bk, free = ring.take()
            t = PE(lambda e, k=k, bk=bk: e.matmul(bk[:, :], Wen[:, 128 * k:128 * k + 128], XT[:, xs], start=True, stop=True),
                   t_x, g_w, *free)
            t = S(lambda e, k=k, bk=bk: e.activation(EN[:, p % 2, k, :], bk[:, :], ACT.Sigmoid, bias=ben[:, k:k + 1]), t,
                  *x.get(("sc", p - 2), ()))
            ring.give(n, t)
            x["en", p, k] = t

    def compress(p):
        xs = slice(512 * p, 512 * p + 512)
        n, bk, free = ring.take()
        for k in range(2):
            t = PE(lambda e, k=k: e.matmul(bk[:, :], Wsc[:, k, :, :].rearrange("p a m -> p (a m)"), EN[:, p % 2, k, :], start=(k == 0),
                                           stop=(k == 1)), x["en", p, k], *free)
        x["sc", p] = (t,)
        x["ct", p] = t = V(lambda e: e.tensor_scalar(CT[:, xs], bk[:, :], bsc[:, :], None, ALU.add), t)
        ring.give(n, t)

    def router(p):
        xs = slice(512 * p, 512 * p + 512)
        n, bk, free = ring.take()
        t = PE(lambda e: e.matmul(bk[0:64, :], Wr1[:, :], CT[0:64, xs], start=True, stop=True), x["ct", p], *free)
        t = S(lambda e: e.activation(T1[:, p % 2, :], bk[0:64, :], ACT.Tanh, bias=br1[:, :]), t, *x.get(("t1", p - 2), ()))
        ring.give(n, t)
        x["t", p] = t

    def logits(p):
        n, bk, free = ring.take()
        t = PE(lambda e: e.matmul(bk[0:8, :], Wr2[:, :], T1[:, p % 2, :], start=True, stop=True), x["t", p], *free)
        x["t1", p] = (t,)
        t = V(lambda e: e.tensor_scalar(LT[:, p % 2, :], bk[0:8, :], br2[:, :], None, ALU.add), t, *x.get(("lt", p - 2), ()))
        ring.give(n, t)
        x["l", p] = t

    def logits_turned(p):
        n, bk, free = ring.take()
        for i in range(4):
            t = PE(lambda e, i=i: e.transpose(bk[:, 8 * i:8 * i + 8], LT[:, p % 2, 128 * i:128 * i + 128], ident[0:8, 0:8]),
                   x["l", p], *free)
        x["lt", p] = (t,)
        x["lg"] = V(lambda e: e.tensor_copy(LG[:, 4 * p:4 * p + 4, :], bk[:, 0:32].rearrange("p (i e) -> p i e", e=E)), t)
        ring.give(n, x["lg"])

    def gates():
        V(lambda e: e.tensor_reduce(lm[:, :], LG[:, :, :], AX, ALU.max))
        t = V(lambda e: e.tensor_tensor(LG[:, :, :], LG[:, :, :], wide(lm[:, :]), ALU.subtract))
        t = S(lambda e: e.activation(LG[:, :, :], LG[:, :, :], ACT.Exp), t)
        V(lambda e: e.tensor_scalar(rest[:, :], c("iota8"), float(E), None, ALU.subtract))
        V(lambda e: e.tensor_reduce(ls[:, :], LG[:, :, :], AX, ALU.add), t)
        V(lambda e: e.reciprocal(ls[:, :], ls[:, :]))
        V(lambda e: e.tensor_tensor(LG[:, :, :], LG[:, :, :], wide(ls[:, :]), ALU.mult))
        for k, hot in enumerate((h1, h2)):
            V(lambda e, k=k: e.tensor_reduce(top[:, :, k], LG[:, :, :], AX, ALU.max))
            V(lambda e, k=k: e.tensor_tensor(eq[:, :, :], LG[:, :, :], wide(top[:, :, k]), ALU.is_equal))
            V(lambda e: e.tensor_tensor(eq[:, :, :], eq[:, :, :], over(rest[:, :]), ALU.mult))
            V(lambda e: e.tensor_reduce(lm[:, :], eq[:, :, :], AX, ALU.min))
            V(lambda e, hot=hot: e.tensor_tensor(hot[:, :, :], over(rest[:, :]), wide(lm[:, :]), ALU.is_equal))
            if k == 0:
                V(lambda e: e.scalar_tensor_tensor(out=LG[:, :, :], in0=h1[:, :, :], scalar=-4.0, in1=LG[:, :, :], op0=ALU.mult,
                                                   op1=ALU.add))
        V(lambda e: e.tensor_tensor(ls[:, :], top[:, :, 0], top[:, :, 1], ALU.add))
        V(lambda e: e.reciprocal(ls[:, :], ls[:, :]))
        V(lambda e: e.tensor_tensor(top[:, :, :], top[:, :, :], wide(ls[:, :], 2), ALU.mult))
        for k, hot in enumerate((h1, h2)):
            V(lambda e, k=k, hot=hot: e.tensor_tensor(hot[:, :, :], hot[:, :, :], wide(top[:, :, k]), ALU.mult))
        x["gt"] = V(lambda e: e.tensor_tensor(hg[:, :, :, :], h1[:, :, :].rearrange("p i (k f) -> p f k i", f=2),
                                              h2[:, :, :].rearrange("p i (k f) -> p f k i", f=2), ALU.add))

    g_g, g_b = group("g_mg"), [group(f"g_mb{p}") for p in range(4)]

    def gates_spread():
        n, bk, free = ring.take()
        t = PE(lambda e: e.transpose(bk[:, 0:128], hg[:, :, :, :].rearrange("p f k i -> p (f k i)"), ident), x["gt"], *free)
        t = S(lambda e: e.activation(gtT[:, :], bk[:, 0:128], ACT.Copy), t)
        ring.give(n, t)
        SP.dma(g_g, lambda e: e.dma_start(gt_d, gtT[:, :]), t)
        gv = gt_d.rearrange("(f k i) t -> f k (i t)", f=2, k=4)
        for p in range(4):
            for q in range(2):
                SP.dma(g_b[p], lambda e, p=p, q=q: e.dma_start(GB[64 * q:64 * q + 64, p, :, :],
                                                               gv[q][:, 512 * p:512 * p + 512].partition_broadcast(64)), g_g)

    def hidden(p):
        xs = slice(512 * p, 512 * p + 512)
        for k in range(E):
            n, bk, free = ring.take()
            t = PE(lambda e, k=k, bk=bk: e.matmul(bk[:, :], We1[:, k, :], CT[:, xs], start=True, stop=True), x["ct", p], t_zero, *free)
            if k % 2 or p == 0:
                t = S.free(lambda e, k=k, bk=bk: e.activation(HE[:, p % 2, k, :], bk[:, :], ACT.Relu, bias=be1[:, k:k + 1]), t,
                           *x.get(("we2", p - 2), ()))
            else:
                t = V.free(lambda e, k=k, bk=bk: e.tensor_scalar(HE[:, p % 2, k, :], bk[:, :], be1[:, k:k + 1], 0.0, ALU.add, ALU.max),
                           t, *x.get(("we2", p - 2), ()))
            ring.give(n, t)
            x["he", p, k] = t

    def expert(p):
        for k in range(4):
            n, bk, free = ring.take()
            for f in range(2):
                t = PE(lambda e, k=k, f=f, bk=bk: e.matmul(bk[64 * f:64 * f + 64, :], We2[:, 2 * k + f, :], HE[:, p % 2, 2 * k + f, :],
                                                           start=True, stop=True), x["he", p, 2 * k + f], *free)
            dst = PR[:, k % 2, :] if k else OT[:, p % 2, :]
            t2 = V.free(lambda e, k=k, bk=bk, dst=dst: e.scalar_tensor_tensor(out=dst, in0=bk[:, :], scalar=be2[:, k:k + 1],
                                                                              in1=GB[:, p, k, :], op0=ALU.add, op1=ALU.mult),
                        t, g_b[p], *x.get(("pr", k % 2) if k else ("cs", p - 2), ()))
            ring.give(n, t2)
            if k:
                t2 = V.free(lambda e, k=k: e.tensor_tensor(OT[:, p % 2, :], OT[:, p % 2, :], PR[:, k % 2, :], ALU.add), t2, x["ot", p])
                x["pr", k % 2] = (t2,)
            x["ot", p] = t2
        x["we2", p] = (t,)

    def spikes(p):
        for k in range(2):
            n, bk, free = ring.take()
            t = PE(lambda e, k=k, bk=bk: e.matmul(bk[:, :], Wcs[:, 128 * k:128 * k + 128], OT[:, p % 2, :], start=True, stop=True),
                   x["ot", p], *free)
            x["cs", p] = (t,)
            t = S.free(lambda e, k=k, bk=bk: e.activation(SM[:, p % 2, k, :], bk[:, :], ACT.Sigmoid, bias=bcs[:, k:k + 1]), t,
                       *x.get(("de", p - 2), ()))
            ring.give(n, t)
            x["sm", p, k] = t

    def decode(p):
        n, bk, free = ring.take()
        for i in range(4):
            o = slice(128 * i, 128 * i + 128)
            for k in range(2):
                t = PE(lambda e, k=k, o=o: e.matmul(bk[:, o], SM[:, p % 2, k, o], Wde[:, k, :], start=(k == 0), stop=(k == 1)),
                       x["sm", p, 0], x["sm", p, 1], *free)
        x["de", p] = (t,)
        yp = Y[:, 4 * p:4 * p + 4, :]
        t = V.free(lambda e: e.tensor_tensor(yp, bk[:, :].rearrange("p (i d) -> p i d", i=4),
                                             bde[:, :].unsqueeze(1).to_broadcast([128, 4, 128]), ALU.add), t)
        ring.give(n, t)
        x["y", p] = S.free(lambda e: e.activation(yp, yp, ACT.Sigmoid), t)

    for s in range(4 + 4):
        for lag, stage in ((0, encode), (1, compress), (2, router), (3, logits), (4, logits_turned)):
            if 0 <= s - lag < 4:
                stage(s - lag)
    t_xb = G(lambda e: e.tensor_tensor(XB[:, :, :], X0[:, :, :], bet[:, :].unsqueeze(1).to_broadcast([128, NT, 128]), ALU.add),
             x["lg"])
    gates()
    for s in range(4 + 3):
        for lag, stage in ((0, hidden), (1, expert), (2, spikes), (3, decode)):
            if 0 <= s - lag < 4:
                stage(s - lag)
        if s == 0:
            gates_spread()
    return [x["y", p] for p in range(4)], gam, XB, t_xb


LAGS = (0, 1, 3, 4)


def program(nc, x, a, f0, a1, f1, const, out):
    with ExitStack() as ctx:
        def sb(name, shape, dt=F32):
            return ctx.enter_context(nc.sbuf_tensor(name, shape, dt))

        def sem(name):
            return ctx.enter_context(nc.semaphore(name))

        def group(name):
            return Group(sem(name))

        PE, S, V, G, SP = [Queue(sem(n), n in ("s_act", "s_dve", "s_pool"))
                           for n in ("s_pe", "s_act", "s_dve", "s_pool", "s_sp")]
        bank = [ctx.enter_context(nc.psum_tensor(f"bank{i}", [128, 512], F32)) for i in range(8)]

        C = sb("C", [128, CONST.shape[1]])

        def c(name, rows=slice(0, 128)):
            return C[rows, CAT[name][0]:CAT[name][1]]

        ident = c("ident")
        X0 = sb("X0", [128, NT, D])
        Y = sb("Y", [128, NT, D])
        XT = sb("XT", [128, NT * 128])
        st6 = sb("st6", [128, 2 * NT, 6])
        mv = sb("mv", [128, 2 * NT, 2])
        rstd = sb("rstd", [128, 2 * NT])
        shift = sb("shift", [128, 2 * NT])

        g_c = [group(f"g_c{i}") for i in range(2)]
        g_x0, g_x = group("g_xtok"), [group(f"g_x{i}") for i in range(4)]
        def transposed(ring, src, p, *waits):
            n, bk, free = ring.take()
            for i in range(4):
                t = PE(lambda e, i=i: e.transpose(bk[:, i * 128:i * 128 + 128], src[:, 4 * p + i, :], ident),
                       *((free + waits) if i == 0 else ()))
            t = S(lambda e: e.activation(XT[:, p * 512:p * 512 + 512], bk[:, :], ACT.Copy), t)
            ring.give(n, t)
            return t

        def stats(tiles, *waits, k=0):
            toks = [V.free(lambda e, i=i: e.bn_stats(st6[:, NT * k + i, :], Y[:, i, :]), *waits) for i in tiles]
            for i, t in zip(tiles, toks):
                t = V.free(lambda e, i=i: e.bn_aggr(mv[:, NT * k + i, :], st6[:, NT * k + i, :]), t)
            return t

        def root(p, *waits, k=0):
            lo, hi = 4 * p + NT * k, 4 * p + 4 + NT * k
            return S(lambda e: e.activation(rstd[:, lo:hi], mv[:, lo:hi, 1], ACT.Sqrt, bias=c("eps")), *waits)

        def divided(dst, p, t, k=0):
            lo, hi = 4 * p + NT * k, 4 * p + 4 + NT * k
            t = V.free(lambda e: e.reciprocal(rstd[:, lo:hi], rstd[:, lo:hi]), t)
            r = V.free(lambda e: e.scalar_tensor_tensor(out=shift[:, lo:hi], in0=mv[:, lo:hi, 0], scalar=-1.0, in1=rstd[:, lo:hi],
                                                        op0=ALU.mult, op1=ALU.mult), t)
            for i in range(4 * p, 4 * p + 4):
                x = NT * k + i
                if i % 4:
                    t_s = S.free(lambda e, i=i, x=x: e.activation(dst[:, i, :], Y[:, i, :], ACT.Identity, scale=rstd[:, x:x + 1],
                                                                  bias=shift[:, x:x + 1]), r)
                else:
                    t_v = V.free(lambda e, i=i, x=x: e.tensor_scalar(dst[:, i, :], Y[:, i, :], mv[:, x, 0:1], rstd[:, x:x + 1],
                                                                     ALU.subtract, ALU.mult), t)
            return t_s, t_v

        def twice_normalised(waits, gam, XP, t_xp, after):
            t = {}

            def first(p):
                t["r", p] = root(p, stats(range(4 * p, 4 * p + 4), *waits[p]))

            def second(p):
                yp = Y[:, 4 * p:4 * p + 4, :]
                E = V if p == 3 else G
                x = E(lambda e: e.tensor_tensor(yp, yp, gam[:, :].unsqueeze(1).to_broadcast([128, 4, 128]), ALU.mult),
                      *divided(Y, p, t["r", p]))
                t["g", p] = E(lambda e: e.tensor_tensor(yp, yp, XP[:, 4 * p:4 * p + 4, :], ALU.add), x, t_xp)

            def third(p):
                t["z", p] = root(p, stats(range(4 * p, 4 * p + 4), t["g", p], k=1), k=1)

            def fourth(p):
                after(p, divided(X0, p, t["z", p], k=1))

            for s in range(4 + LAGS[3]):
                for lag, stage in zip(LAGS, (first, second, third, fourth)):
                    if 0 <= s - lag < 4:
                        stage(s - lag)

        def fence():
            ends = [q.items[-1][2] for q in (PE, S, V, G)]
            for q in (PE, S, V, G, SP):
                q.hold(*ends)

        masks = CAT["mask0"][0]

        def load_x(part):
            for p in [0] if part == 0 else [1, 2, 3]:
                SP.dma(g_x[p], lambda e, p=p: e.dma_start(XT[:, 512 * p:512 * p + 512], a["xT"][:, 512 * p:512 * p + 512]))
                if p == 0:
                    SP.dma(g_c[0], lambda e: e.dma_start(C[:, 0:masks], const[:, 0:masks]))
                if p == 1:
                    SP.dma(g_c[1], lambda e: e.dma_start(C[:, masks:], const[:, masks:]))
            if part:
                load_router()
                SP.dma(g_x0, lambda e: e.dma_start(X0[:, :, :], x.rearrange("b (h p) d -> p (b h) d", p=128)))

        Wr, br, zero = sb("Wr", [128, 8]), sb("br", [8, 1]), sb("zero", [128, 512])
        logit = sb("logit", [128, NT, 8])
        g_r, g_z = group("g_fr"), group("g_fz")
        xs_d = nc.dram_tensor("xs_d", [TILES * 128, 128], F32, kind="Internal").ap()
        t_z = G(lambda e: e.memset(zero[:, :], 0.0))

        def load_router():
            SP.dma(g_r, lambda e: e.dma_start(Wr[:, :], f0["Wr"]))
            SP.dma(g_r, lambda e: e.dma_start(br[:, :], f0["br"].rearrange("(n o) -> n o", o=1)))
            zv = xs_d.rearrange("(p r) d -> p (r d)", p=128)
            for k in range(0, TILES * 128, 512):
                w = min(512, TILES * 128 - k)
                SP.dma(g_z, lambda e, k=k, w=w: e.dma_start(zv[:, k:k + w], zero[:, 0:w]), t_z)

        done = {}

        def after_attention(ring, p, t):
            t = divided(X0, p, root(p, t))
            yield
            yield
            t_x = transposed(ring, X0, p, *t)
            yield
            n, bk, free = ring.take()
            t = PE(lambda e: e.matmul(bk[0:8, :], Wr[:, :], XT[:, 512 * p:512 * p + 512], start=True, stop=True), t_x, g_r, *free)
            t = V.free(lambda e: e.tensor_scalar(turned[:, :], bk[0:8, :], br[:, :], None, ALU.add), t, *done.get("turned", ()))
            ring.give(n, t)
            yield
            n, bk2, free = ring.take()
            for i in range(4):
                t = PE(lambda e, i=i: e.transpose(bk2[:, 8 * i:8 * i + 8], turned[:, 128 * i:128 * i + 128], ident[0:8, 0:8]), t, *free)
            done["turned"] = (t,)
            done["logit"] = V(lambda e: e.tensor_copy(logit[:, 4 * p:4 * p + 4, :], bk2[:, 0:32].rearrange("p (i e) -> p i e", e=8)), t)
            ring.give(n, done["logit"])

        with ExitStack() as part:
            turned = part.enter_context(nc.sbuf_tensor("turned", [8, 512], F32))
            ring = attention(nc, part, sem, group, (PE, S, V, G, SP), bank, a, c, ident, X0, XT, Y, g_c, g_x0, g_x, stats, load_x,
                             after_attention)
        fence()
        everything = (PE, S, V, G, SP)
        w1, g_w1, load_mixture = mixture_weights(ctx, nc, group, SP, f1)
        with ExitStack() as both:
            pieces = scan_weights(nc, both, sem, group, everything, bank[5:8], a1, c, ident)
            made = next(pieces)
            with ExitStack() as part:
                x2, ring = experts(nc, part, sem, group, everything, bank[0:5], f0, c, ident, X0, Y, xs_d, logit, g_z,
                                   done["logit"], stats, root, divided, pieces)
            ring = ring.join(made["ring"])
            load_mixture()
            with ExitStack() as part:
                ring, ys, gam, XP, t_xp = scan(nc, part, sem, group, everything, ring, a1, c, ident, X0, XT, Y, transposed, made, x2)
            x3 = {}
            twice_normalised([ys] * 4, gam, XP, t_xp, x3.__setitem__)
            fence()
        with ExitStack() as part:
            ys, gam, XB, t_xb = mixture(nc, part, group, everything, ring, w1, g_w1, c, ident, X0, XT, Y, transposed, x3.get)
            g_out = group("g_out")
            ov = out.rearrange("b (q i) d -> (b q) i d", i=16)

            def store(p, t):
                SP.dma(g_out, lambda e: e.dma_start(ov[:, 4 * p:4 * p + 4, :], X0[:, 4 * p:4 * p + 4, :]), *t)

            twice_normalised([[y] for y in ys], gam, XB, t_xb, store)
        SP.hold(g_out)

        queues = (PE, S, V, G, SP)
        for q in queues:
            q.count()
        block = ctx.enter_context(nc.Block())

        @block.tensor
        def _(eng):
            PE.write(eng)

        @block.scalar
        def _(eng):
            S.write(eng)

        @block.vector
        def _(eng):
            V.write(eng)

        @block.gpsimd
        def _(eng):
            G.write(eng)

        @block.sync
        def _(eng):
            SP.write(eng)


NAMES = ['L0_attn_x', 'L0_attn_W_dkv', 'L0_attn_W_uk', 'L0_attn_W_uv', 'L0_attn_W_dq', 'L0_attn_W_uq', 'L0_attn_W_qr', 'L0_attn_W_kr', 'L0_attn_W_out', 'L0_attn_idx_wq', 'L0_attn_idx_wk', 'L0_attn_idx_w', 'L0_attn_raw_delta', 'L0_ffn_Wr', 'L0_ffn_br', 'L0_ffn_W1', 'L0_ffn_W2', 'L1_attn_A', 'L1_attn_Bp', 'L1_attn_Cp', 'L1_attn_Dp', 'L1_attn_Wg', 'L1_attn_bg', 'L1_attn_gamma', 'L1_attn_beta', 'L1_ffn_enc_W', 'L1_ffn_enc_b', 'L1_ffn_s2c_W', 'L1_ffn_s2c_b', 'L1_ffn_rW1', 'L1_ffn_rb1', 'L1_ffn_rW2', 'L1_ffn_rb2', 'L1_ffn_We1', 'L1_ffn_be1', 'L1_ffn_We2', 'L1_ffn_be2', 'L1_ffn_c2s_W', 'L1_ffn_c2s_b', 'L1_ffn_dec_W', 'L1_ffn_dec_b', 'L1_ffn_ln_g', 'L1_ffn_ln_b']


def kernel(**inputs):
    import concourse.bacc as bacc
    from concourse.bass_utils import run_bass_kernel_spmd

    nc = bacc.Bacc("TRN2", target_bir_lowering=False, num_devices=1)
    arrays, aps = {}, {}
    for name in NAMES:
        v = np.ascontiguousarray(inputs[name])
        arrays[name] = v
        aps[name] = nc.dram_tensor(name, v.shape, mybir.dt.from_np(v.dtype), kind="ExternalInput").ap()
    arrays["shape_constants"] = CONST
    const = nc.dram_tensor("shape_constants", CONST.shape, F32, kind="ExternalInput").ap()
    out = nc.dram_tensor("result", (B, L, D), F32, kind="ExternalOutput").ap()

    def part(prefix):
        return {n[len(prefix):]: aps[n] for n in NAMES if n.startswith(prefix)}

    def lay(name, v):
        arrays[name] = v = np.ascontiguousarray(v)
        return nc.dram_tensor(name, v.shape, F32, kind="ExternalInput").ap()

    def by_state(v):
        v = v.reshape((8, 16) + v.shape[1:])
        return v.transpose((2, 0, 1) + tuple(range(3, v.ndim))).reshape(128, -1)

    def block(v, k):
        return v.reshape(k, 128, -1).transpose(1, 0, 2).reshape(128, -1)

    a0 = {n[8:]: np.asarray(inputs[n]) for n in NAMES if n.startswith("L0_attn_")}
    heads = {"Wp": np.concatenate([a0["W_dq"], a0["W_dkv"], a0["W_kr"]], 1),
             "Wi": np.concatenate([a0["idx_wk"], a0["idx_wk"], a0["idx_wq"]], 1),
             "WuqT": block(a0["W_uq"].T, 4), "WukT": block(a0["W_uk"].T, 4), "WuvT": block(a0["W_uv"].T, 4),
             "Wout": block(a0["W_out"], 4),
             "Wq2": np.pad(a0["W_qr"], ((0, 64), (256, 0))),
             "wix": np.broadcast_to(a0["idx_w"], (128, 4)),
             "rd": np.concatenate([np.broadcast_to(a0["raw_delta"], (128, 16)), np.tile(a0["raw_delta"], 8)[:, None]], 1)}
    at0 = {"packed": lay("attention_packed", np.concatenate([heads[n] for n, _ in PACK], 1)),
           "xT": lay("x_features", a0["x"].reshape(B * L, D).T)}
    a1, f1 = part("L1_attn_"), part("L1_ffn_")
    skip = np.broadcast_to(np.asarray(inputs["L1_attn_Dp"])[:, None], (128, 16))
    a1["packed"] = lay("scan_packed", np.concatenate(
        [by_state(np.asarray(inputs[f"L1_attn_{k}"])) for k in ("A", "Bp", "Cp")] + [by_state(skip)], 1))
    for k in ("enc_b", "c2s_b"):
        f1[k] = lay(f"{k}_columns", np.asarray(inputs[f"L1_ffn_{k}"]).reshape(2, 128).T)
    f1["be2"] = lay("be2_columns", np.asarray(inputs["L1_ffn_be2"]).reshape(4, 128).T)
    f1["be1"] = lay("be1_columns", np.asarray(inputs["L1_ffn_be1"]).T)
    program(nc, aps["L0_attn_x"], at0, part("L0_ffn_"), a1, f1, const, out)
    r = run_bass_kernel_spmd(nc, [arrays], core_ids=[0])
    return r.results[0]["result"]
```
